# Optimizing a Trainium2 kernel written in Bass

```python
import numpy as np
import jax
import jax.numpy as jnp

def _softmax(x, axis=-1):
    return jax.nn.softmax(x, axis=axis)

def _gelu(x):
    return jax.nn.gelu(x, approximate=True)

def _silu(x):
    return jax.nn.silu(x)

def _sigmoid(x):
    return jax.nn.sigmoid(x)

def _layernorm(x, axis=-1, eps=1e-05):
    m = jnp.mean(x, axis=axis, keepdims=True)
    v = jnp.var(x, axis=axis, keepdims=True)
    return (x - m) / jnp.sqrt(v + eps)

def _scatter_add(tgt, idx, src, axis=0):
    return tgt.at[idx].add(src)

def _segment_sum(src, seg, n):
    return jax.ops.segment_sum(src, seg, n)
kernel_name = 'mk_audio_tower_d1_tok_aud1d768_r4_ddd79c'

def setup_inputs(seed: int=0):
    np.random.seed(seed)
    _w = jnp.asarray

    def _rec_inputs():
        import jax
        import jax.numpy as jnp
        _rk = jax.random.key(seed)
        x = -0.000869125 + 1.00042 * jax.random.normal(jax.random.fold_in(_rk, 1), (8, 120000), jnp.float32)
        return x
    x = _rec_inputs()

    def _L0_tok_setup():
        import jax, jax.numpy as jnp
        import numpy as np
        CONVS = [(128, 10, 5)] + [(128, 3, 2)] * 4 + [(128, 2, 2)] * 2

        def _fp32_layernorm(x, g, b, eps=1e-05):
            xf = x.astype(jnp.float32)
            mu = xf.mean(-1, keepdims=True)
            var = xf.var(-1, keepdims=True)
            y = (xf - mu) * jax.lax.rsqrt(var + eps) * g.astype(jnp.float32) + b.astype(jnp.float32)
            return y.astype(x.dtype)

        def _conv1d(x, w, stride):
            return jax.lax.conv_general_dilated(x, w, (stride,), 'VALID', dimension_numbers=('NCH', 'OIH', 'NCH'))
        key = jax.random.key(seed)
        keys = jax.random.split(key, 16)
        inp = {'x': jax.random.normal(keys[0], (8, 40000), jnp.float32)}
        in_d = 1
        for i, (dim, k, s) in enumerate(CONVS):
            fan_in = in_d * k
            inp[f'conv_w{i}'] = jax.random.normal(keys[1 + i], (dim, in_d, k), jnp.float32) * np.float32(np.sqrt(2.0 / fan_in))
            inp[f'ln_g{i}'] = jnp.ones((dim,), jnp.float32)
            inp[f'ln_b{i}'] = jnp.zeros((dim,), jnp.float32)
            in_d = dim
        inp['fln_g'] = jnp.ones((128,), jnp.float32)
        inp['fln_b'] = jnp.zeros((128,), jnp.float32)
        inp['proj_w'] = jax.random.normal(keys[9], (128, 192), jnp.float32) * np.float32(0.02)
        inp['proj_b'] = jnp.zeros((192,), jnp.float32)
        return inp
    _L0_tok_all = _L0_tok_setup()
    _L0_tok_in = {k: v for k, v in _L0_tok_all.items() if k in ('conv_w0', 'ln_g0', 'ln_b0', 'conv_w1', 'ln_g1', 'ln_b1', 'conv_w2', 'ln_g2', 'ln_b2', 'conv_w3', 'ln_g3', 'ln_b3', 'conv_w4', 'ln_g4', 'ln_b4', 'conv_w5', 'ln_g5', 'ln_b5', 'conv_w6', 'ln_g6', 'ln_b6', 'fln_g', 'fln_b', 'proj_w', 'proj_b')}
    del _L0_tok_all

    def _L0_attn_setup():
        import jax, jax.numpy as jnp
        import numpy as np
        NUM_HEADS = 12
        EPS = 1e-06
        key = jax.random.key(seed)
        k1, k2, k3, k4 = jax.random.split(key, 4)
        N, B, D = (1025, 8, 192)
        x = jax.random.normal(k1, (N, B, D), dtype=jnp.float32)
        w_qkv = jax.random.normal(k2, (3 * D, D), dtype=jnp.float32) * D ** (-0.5)
        w_proj = jax.random.normal(k3, (D, D), dtype=jnp.float32) * D ** (-0.5)
        b_proj = jax.random.normal(k4, (D,), dtype=jnp.float32) * 0.01
        return {'x': x, 'w_qkv': w_qkv, 'w_proj': w_proj, 'b_proj': b_proj}
    _L0_attn_all = _L0_attn_setup()
    _L0_attn_in = {k: v for k, v in _L0_attn_all.items() if k in ('w_qkv', 'w_proj', 'b_proj')}
    del _L0_attn_all

    def _L0_ffn_setup():
        import jax, jax.numpy as jnp
        import numpy as np
        from jax import lax
        DIM = 192
        INTER = 128
        E = 8
        G = 4
        TOPK_G = 2
        TOPK = 2
        ROUTE_SCALE = 1.0

        def _gate(x2, gate_weight, gate_bias):
            T = x2.shape[0]
            scores = jax.nn.sigmoid(x2 @ gate_weight.T)
            s = scores + gate_bias
            sv = s.reshape(T, G, E // G)
            top2, _ = lax.top_k(sv, 2)
            group_scores = top2.sum(-1)
            _, gidx = lax.top_k(group_scores, TOPK_G)
            gmask = jnp.zeros((T, G), bool).at[jnp.arange(T)[:, None], gidx].set(True)
            masked = jnp.where(gmask[:, :, None], sv, -jnp.inf).reshape(T, E)
            _, idx = lax.top_k(masked, TOPK)
            w = jnp.take_along_axis(scores, idx, axis=1)
            w = w / (w.sum(-1, keepdims=True) + 1e-06) * ROUTE_SCALE
            return (w, idx)
        key = jax.random.key(seed)
        ks = jax.random.split(key, 9)
        s = 1.0 / np.sqrt(DIM)
        si = 1.0 / np.sqrt(INTER)
        return {'x': jax.random.normal(ks[0], (4, 1024, DIM), jnp.float32), 'gate_weight': jax.random.uniform(ks[1], (E, DIM), jnp.float32, -s, s), 'gate_bias': jnp.zeros((E,), jnp.float32), 'w1': jax.random.uniform(ks[2], (E, INTER, DIM), jnp.float32, -s, s), 'w2': jax.random.uniform(ks[3], (E, DIM, INTER), jnp.float32, -si, si), 'w3': jax.random.uniform(ks[4], (E, INTER, DIM), jnp.float32, -s, s), 'sw1': jax.random.uniform(ks[5], (INTER, DIM), jnp.float32, -s, s), 'sw2': jax.random.uniform(ks[6], (DIM, INTER), jnp.float32, -si, si), 'sw3': jax.random.uniform(ks[7], (INTER, DIM), jnp.float32, -s, s)}
    _L0_ffn_all = _L0_ffn_setup()
    _L0_ffn_in = {k: v for k, v in _L0_ffn_all.items() if k in ('gate_weight', 'gate_bias', 'w1', 'w2', 'w3', 'sw1', 'sw2', 'sw3')}
    del _L0_ffn_all
    return {'x': x, 'L0_tok_conv_w0': _L0_tok_in['conv_w0'], 'L0_tok_ln_g0': _L0_tok_in['ln_g0'], 'L0_tok_ln_b0': _L0_tok_in['ln_b0'], 'L0_tok_conv_w1': _L0_tok_in['conv_w1'], 'L0_tok_ln_g1': _L0_tok_in['ln_g1'], 'L0_tok_ln_b1': _L0_tok_in['ln_b1'], 'L0_tok_conv_w2': _L0_tok_in['conv_w2'], 'L0_tok_ln_g2': _L0_tok_in['ln_g2'], 'L0_tok_ln_b2': _L0_tok_in['ln_b2'], 'L0_tok_conv_w3': _L0_tok_in['conv_w3'], 'L0_tok_ln_g3': _L0_tok_in['ln_g3'], 'L0_tok_ln_b3': _L0_tok_in['ln_b3'], 'L0_tok_conv_w4': _L0_tok_in['conv_w4'], 'L0_tok_ln_g4': _L0_tok_in['ln_g4'], 'L0_tok_ln_b4': _L0_tok_in['ln_b4'], 'L0_tok_conv_w5': _L0_tok_in['conv_w5'], 'L0_tok_ln_g5': _L0_tok_in['ln_g5'], 'L0_tok_ln_b5': _L0_tok_in['ln_b5'], 'L0_tok_conv_w6': _L0_tok_in['conv_w6'], 'L0_tok_ln_g6': _L0_tok_in['ln_g6'], 'L0_tok_ln_b6': _L0_tok_in['ln_b6'], 'L0_tok_fln_g': _L0_tok_in['fln_g'], 'L0_tok_fln_b': _L0_tok_in['fln_b'], 'L0_tok_proj_w': _L0_tok_in['proj_w'], 'L0_tok_proj_b': _L0_tok_in['proj_b'], 'L0_attn_w_qkv': _L0_attn_in['w_qkv'], 'L0_attn_w_proj': _L0_attn_in['w_proj'], 'L0_attn_b_proj': _L0_attn_in['b_proj'], 'L0_ffn_gate_weight': _L0_ffn_in['gate_weight'], 'L0_ffn_gate_bias': _L0_ffn_in['gate_bias'], 'L0_ffn_w1': _L0_ffn_in['w1'], 'L0_ffn_w2': _L0_ffn_in['w2'], 'L0_ffn_w3': _L0_ffn_in['w3'], 'L0_ffn_sw1': _L0_ffn_in['sw1'], 'L0_ffn_sw2': _L0_ffn_in['sw2'], 'L0_ffn_sw3': _L0_ffn_in['sw3']}

def reference(x, L0_tok_conv_w0, L0_tok_ln_g0, L0_tok_ln_b0, L0_tok_conv_w1, L0_tok_ln_g1, L0_tok_ln_b1, L0_tok_conv_w2, L0_tok_ln_g2, L0_tok_ln_b2, L0_tok_conv_w3, L0_tok_ln_g3, L0_tok_ln_b3, L0_tok_conv_w4, L0_tok_ln_g4, L0_tok_ln_b4, L0_tok_conv_w5, L0_tok_ln_g5, L0_tok_ln_b5, L0_tok_conv_w6, L0_tok_ln_g6, L0_tok_ln_b6, L0_tok_fln_g, L0_tok_fln_b, L0_tok_proj_w, L0_tok_proj_b, L0_attn_w_qkv, L0_attn_w_proj, L0_attn_b_proj, L0_ffn_gate_weight, L0_ffn_gate_bias, L0_ffn_w1, L0_ffn_w2, L0_ffn_w3, L0_ffn_sw1, L0_ffn_sw2, L0_ffn_sw3):
    import jax
    import jax.numpy as jnp

    def _L0_tok_ref(x, conv_w0, ln_g0, ln_b0, conv_w1, ln_g1, ln_b1, conv_w2, ln_g2, ln_b2, conv_w3, ln_g3, ln_b3, conv_w4, ln_g4, ln_b4, conv_w5, ln_g5, ln_b5, conv_w6, ln_g6, ln_b6, fln_g, fln_b, proj_w, proj_b):
        import jax, jax.numpy as jnp
        import numpy as np
        CONVS = [(128, 10, 5)] + [(128, 3, 2)] * 4 + [(128, 2, 2)] * 2

        def _fp32_layernorm(x, g, b, eps=1e-05):
            xf = x.astype(jnp.float32)
            mu = xf.mean(-1, keepdims=True)
            var = xf.var(-1, keepdims=True)
            y = (xf - mu) * jax.lax.rsqrt(var + eps) * g.astype(jnp.float32) + b.astype(jnp.float32)
            return y.astype(x.dtype)

        def _conv1d(x, w, stride):
            return jax.lax.conv_general_dilated(x, w, (stride,), 'VALID', dimension_numbers=('NCH', 'OIH', 'NCH'))
        conv_ws = [conv_w0, conv_w1, conv_w2, conv_w3, conv_w4, conv_w5, conv_w6]
        ln_gs = [ln_g0, ln_g1, ln_g2, ln_g3, ln_g4, ln_g5, ln_g6]
        ln_bs = [ln_b0, ln_b1, ln_b2, ln_b3, ln_b4, ln_b5, ln_b6]
        strides = [s for _, _, s in CONVS]
        h = x[:, None, :]
        for w, g, b, s in zip(conv_ws, ln_gs, ln_bs, strides):
            h = _conv1d(h, w, s)
            h = jnp.swapaxes(h, -2, -1)
            h = _fp32_layernorm(h, g, b)
            h = jnp.swapaxes(h, -2, -1)
            h = jax.nn.gelu(h, approximate=False)
        h = jnp.swapaxes(h, 1, 2)
        norm_h = _fp32_layernorm(h, fln_g, fln_b)
        out = norm_h @ proj_w + proj_b
        return out

    def _L0_attn_ref(x, w_qkv, w_proj, b_proj):
        import jax, jax.numpy as jnp
        import numpy as np
        NUM_HEADS = 12
        EPS = 1e-06
        N, B, D = x.shape
        H = NUM_HEADS
        hd = D // H
        scale = hd ** (-0.5)
        scale_vv = scale * 1.0
        xb = jnp.transpose(x, (1, 0, 2))
        qkv = xb @ w_qkv.T
        qkv = qkv.reshape(B, N, 3, H, hd).transpose(2, 0, 3, 1, 4)
        q, k, v = (qkv[0], qkv[1], qkv[2])
        scores0 = jnp.einsum('bhqd,bhkd->bhqk', q[:, :, :1], k) * scale
        attn0 = jax.nn.softmax(scores0, axis=-1)
        out0 = jnp.einsum('bhqk,bhkd->bhqd', attn0, v)
        vn = v / jnp.maximum(jnp.linalg.norm(v, axis=-1, keepdims=True), EPS)
        scores_vv = jnp.einsum('bhqd,bhkd->bhqk', vn[:, :, 1:], vn) * scale_vv
        attn_vv = jax.nn.softmax(scores_vv, axis=-1)
        out_vv = jnp.einsum('bhqk,bhkd->bhqd', attn_vv, v)
        out = jnp.concatenate([out0, out_vv], axis=2)
        out = out.transpose(0, 2, 1, 3).reshape(B, N, D)
        out = out @ w_proj.T + b_proj
        return jnp.transpose(out, (1, 0, 2))

    def _L0_ffn_ref(x, gate_weight, gate_bias, w1, w2, w3, sw1, sw2, sw3):
        import jax, jax.numpy as jnp
        import numpy as np
        from jax import lax
        DIM = 192
        INTER = 128
        E = 8
        G = 4
        TOPK_G = 2
        TOPK = 2
        ROUTE_SCALE = 1.0

        def _gate(x2, gate_weight, gate_bias):
            T = x2.shape[0]
            scores = jax.nn.sigmoid(x2 @ gate_weight.T)
            s = scores + gate_bias
            sv = s.reshape(T, G, E // G)
            top2, _ = lax.top_k(sv, 2)
            group_scores = top2.sum(-1)
            _, gidx = lax.top_k(group_scores, TOPK_G)
            gmask = jnp.zeros((T, G), bool).at[jnp.arange(T)[:, None], gidx].set(True)
            masked = jnp.where(gmask[:, :, None], sv, -jnp.inf).reshape(T, E)
            _, idx = lax.top_k(masked, TOPK)
            w = jnp.take_along_axis(scores, idx, axis=1)
            w = w / (w.sum(-1, keepdims=True) + 1e-06) * ROUTE_SCALE
            return (w, idx)
        B, S, D = x.shape
        x2 = x.reshape(-1, D)
        T = x2.shape[0]
        weights, indices = _gate(x2, gate_weight, gate_bias)
        cw = jnp.zeros((T, E), x.dtype).at[jnp.arange(T)[:, None], indices].add(weights)
        h1 = jnp.einsum('td,eid->tei', x2, w1)
        h3 = jnp.einsum('td,eid->tei', x2, w3)
        h = jax.nn.silu(h1) * h3
        y = jnp.einsum('tei,edi,te->td', h, w2, cw)
        z = jax.nn.silu(x2 @ sw1.T) * (x2 @ sw3.T) @ sw2.T
        return (y + z).reshape(B, S, D)
    h = _L0_tok_ref(x, L0_tok_conv_w0, L0_tok_ln_g0, L0_tok_ln_b0, L0_tok_conv_w1, L0_tok_ln_g1, L0_tok_ln_b1, L0_tok_conv_w2, L0_tok_ln_g2, L0_tok_ln_b2, L0_tok_conv_w3, L0_tok_ln_g3, L0_tok_ln_b3, L0_tok_conv_w4, L0_tok_ln_g4, L0_tok_ln_b4, L0_tok_conv_w5, L0_tok_ln_g5, L0_tok_ln_b5, L0_tok_conv_w6, L0_tok_ln_g6, L0_tok_ln_b6, L0_tok_fln_g, L0_tok_fln_b, L0_tok_proj_w, L0_tok_proj_b)
    h = h + _L0_attn_ref(_layernorm(h, axis=-1), L0_attn_w_qkv, L0_attn_w_proj, L0_attn_b_proj)
    h = h + _L0_ffn_ref(_layernorm(h, axis=-1), L0_ffn_gate_weight, L0_ffn_gate_bias, L0_ffn_w1, L0_ffn_w2, L0_ffn_w3, L0_ffn_sw1, L0_ffn_sw2, L0_ffn_sw3)
    return h

_drawn_inputs = setup_inputs


def setup_inputs(seed=0):
    import zlib

    import numpy as np

    out = dict(_drawn_inputs(seed))
    spreads = {'L0_tok_ln_g0': (1.0, 0.2),
     'L0_tok_ln_b0': (0.0, 0.1),
     'L0_tok_ln_g1': (1.0, 0.2),
     'L0_tok_ln_b1': (0.0, 0.1),
     'L0_tok_ln_g2': (1.0, 0.2),
     'L0_tok_ln_b2': (0.0, 0.1),
     'L0_tok_ln_g3': (1.0, 0.2),
     'L0_tok_ln_b3': (0.0, 0.1),
     'L0_tok_ln_g4': (1.0, 0.2),
     'L0_tok_ln_b4': (0.0, 0.1),
     'L0_tok_ln_g5': (1.0, 0.2),
     'L0_tok_ln_b5': (0.0, 0.1),
     'L0_tok_ln_g6': (1.0, 0.2),
     'L0_tok_ln_b6': (0.0, 0.1),
     'L0_tok_fln_g': (1.0, 0.2),
     'L0_tok_fln_b': (0.0, 0.1),
     'L0_tok_proj_b': (0.0, 0.1),
     'L0_ffn_gate_bias': (0.0, 0.1)}
    factors = {'L0_attn_b_proj': 3.928}
    for name, (base, spread) in spreads.items():
        noise = np.random.default_rng([zlib.crc32(name.encode()), seed]).standard_normal(out[name].shape)
        drawn = base * np.exp(spread * noise) if base else spread * noise
        out[name] = jnp.asarray(drawn.astype(out[name].dtype))
    for name, factor in factors.items():
        out[name] = (out[name] * factor).astype(out[name].dtype)
    return out
```

```python
import math
from contextlib import ExitStack

import numpy as np
import concourse.bass as bass
from concourse import mybir

f32 = mybir.dt.float32
f16 = mybir.dt.float16
i32 = mybir.dt.int32
ACT = mybir.ActivationFunctionType
ALU = mybir.AluOpType
AX = mybir.AxisListType

CH = 128
BATCH, POS = 8, 374
POS_PAD = 375
TAPS = [10, 3, 3, 3, 3, 2, 2]
STEP0 = 4096
LAYER_COLS = [STEP0 >> l for l in range(6)]
STEPS = -(-(BATCH * POS_PAD * 64 + 1) // STEP0)
LAG = 5
BN = 6
EPS_SUM = CH * 1e-5
ROOT_CH = math.sqrt(CH)
QUAD, HALF = 4, 2
COLS = 512
XROWS = HALF * TAPS[0] * QUAD
SROWS = 3 * TAPS[0] * QUAD
X_LEN = STEP0 * (STEPS + 2) + 8

MAGIC = float(0x5F1FFFF9)
NEWTON1 = (-0.703952253, 0.703952253 * 2.38924456)
NEWTON2 = (-0.5 * (1 + 3.2e-7), 1.5 * (1 + 3.2e-7))

G0, G1, G2, G3 = range(4)
FIRST = {G0: 1, G1: 1, G2: 1, G3: 2}
LAST = {G0: STEPS, G1: STEPS, G2: STEPS, G3: STEPS + 3}
UNITS = [(G0, 0), (G0, 1), ("L0", 0), ("L0", 1), ("L0", 2), ("L0", 3), (G1, 0), (G1, 1),
         (G3, 0), (G3, 1), ("L0", 4), ("L0", 5), ("L0", 6), ("L0", 7), (G2, 0), (G2, 1)]
BANK = [0, 1, 2, 0, 1, 2, 0, 1, 2, 0, 1, 2, 0, 1, 2, 1]
STAGE = [u % 4 for u in range(16)]
TILES = {G0: [(1, t) for t in range(8)], G1: [(1, t) for t in range(8, 16)],
         G2: [(2, t) for t in range(8)],
         G3: [(3, t) for t in range(4)] + [(4, 0), (4, 1), (5, 0)]}
YPAIR = {G0: 0, G1: 1, G3: 0, G2: 1}
NORM_OPS = 12
GRAM_OPS = 8


def first_step(kind):
    return 0 if kind == "L0" else FIRST[kind]


def last_step(kind):
    return STEPS - 1 if kind == "L0" else LAST[kind]


def unit_count(u, s):
    return s - first_step(UNITS[u][0]) + 1


def active(kind, s):
    return not isinstance(s, int) or first_step(kind) <= s <= last_step(kind)


def previous_user(place, u, s):
    at = s
    for _ in range(3):
        order = range(u - 1, -1, -1) if at is s else range(15, -1, -1)
        for v in order:
            if place[v] == place[u] and active(UNITS[v][0], at):
                return v, at
        at = at - 1
        if isinstance(at, int) and at < 0:
            return None
    return None


def conv_tower(nc, x5, w0t, wconv, gb, consts, keep, dump=None):
    ident_d, mask_d, chunk_d = consts
    ident, gains, gain_s, WH, WL, H5, loads = keep
    ctx = ExitStack()
    with ctx:
        def sb(name, shape, dt=f32):
            return ctx.enter_context(nc.sbuf_tensor(name, shape, dt))

        def ps(name, shape):
            return ctx.enter_context(nc.psum_tensor(name, shape, f32))

        def sem(name):
            return ctx.enter_context(nc.semaphore(name))

        mask = sb("same_chunk_mask", [XROWS, XROWS])
        chunk_sum = sb("chunk_sum", [XROWS, 8])
        W = sb("conv_w", [128, 16, CH])
        Wsum = sb("conv_w_sum", [128, 16])
        w0 = sb("w0", [TAPS[0], CH])
        w0sum = sb("w0_sum", [TAPS[0], 1])
        w0hl = sb("w0_high_low", [TAPS[0], 2, CH], f16)
        w0x = sb("w0_expanded", [128, XROWS])
        gram = sb("gram", [XROWS, XROWS])
        W0P = sb("w0_stacked", [SROWS, QUAD, CH], f16)
        X = sb("windows", [XROWS, COLS])
        Q = sb("window_products", [XROWS, COLS])
        XN = sb("windows_scaled", [XROWS, COLS])
        RX = sb("window_scales", [128, 4 * XROWS])
        XHL = sb("windows_high_low", [XROWS, 2, COLS], f16)
        S = sb("windows_stacked", [SROWS, HALF, COLS], f16)
        H = [sb(f"act{l}", [128, 2, LAYER_COLS[l] + 2], f16) for l in range(5)]
        H.append(H5)
        zeros = sb("zeros", [128, 2, 1], f16)
        A = [sb(f"gelu{k}", [128, COLS]) for k in range(4)]
        T = [sb(f"scaled{k}", [128, 8, CH]) for k in range(2)]
        stats = sb("stats", [128, 4, BN])
        rs = {k: [sb(f"rsqrt_{k}_{n}", [128, w]) for n in range(4)] for k, w in (("g", 8), ("x", 32))}

        Y = [ps(f"Y{k}", [128, 8, CH]) for k in range(2)]
        E = [ps(f"E{k}", [128, COLS]) for k in range(3)]
        GB = ps("gram_bank", [128, COLS])

        consts_in = sem("consts_in")
        weights_ready = sem("weights_ready")
        w0_centred = sem("w0_centred")
        w0_turned = sem("w0_turned")
        w0_expanded = sem("w0_expanded")
        gram_raw = sem("gram_raw")
        gram_ready = sem("gram_ready")
        w0_stacked = sem("w0_stacked")
        w0p_zero = sem("w0p_zero")
        act_zero = sem("act_zero")
        setup = sem("setup_link")
        x_in = sem("x_in")
        later_in = sem("later_in")
        z_ready = sem("z_ready")
        q_ready = sem("q_ready")
        v_ready = sem("v_ready")
        rx_ready = sem("rx_ready")
        r_ready = sem("r_ready")
        xn_done = sem("xn_done")
        xhl_done = sem("xhl_done")
        s_in = sem("s_in")
        xhigh = sem("xhigh_done")
        gram_link = sem("gram_link")
        link = {g: sem(f"norm_link{g}") for g in range(4)}
        y_ready = {g: sem(f"y_ready{g}") for g in range(4)}
        scaled = {g: sem(f"scaled{g}") for g in range(4)}
        e_ready = [sem(f"e_ready{u}") for u in range(16)]
        gelu_done = [sem(f"gelu_done{u}") for u in range(16)]
        high_done = [sem(f"high_done{u}") for u in range(16)]
        low_done = [sem(f"low_done{u}") for u in range(16)]
        halo = [sem(f"halo{l}") for l in range(5)]

        block = ctx.enter_context(nc.Block())
        LOOP = (3, STEPS)

        def run_steps(eng, step):
            for s in range(0, LOOP[0]):
                step(s)
            with eng.Fori(LOOP[0], LOOP[1], 1) as s:
                step(s)
            for s in range(LOOP[1], STEPS + 4):
                step(s)

        def unit_target(u):
            kind, k = UNITS[u]
            if kind == "L0":
                return [(0, 1 + COLS * k, 0, COLS)]
            if kind == G0:
                return [(1, 1 + COLS * k, 0, COLS)]
            if kind == G1:
                return [(1, 1 + 1024 + COLS * k, 0, COLS)]
            if kind == G2:
                return [(2, 1 + COLS * k, 0, COLS)]
            if k == 0:
                return [(3, 1, 0, COLS)]
            return [(4, 1, 0, 256), (5, None, 256, 128)]

        def act_cols(layer, part, col, n, s):
            if layer < 5:
                return H[layer][:, part, col:col + n]
            if isinstance(s, int):
                return H[5][:, part, (s - 2) * 128:(s - 2) * 128 + 128]
            return H[5][:, part, bass.ds((s - 2) * 128, 128)]

        @block.sync
        def _(sp):
            sp.dma_start(w0[:], w0t).then_inc(consts_in, 16)
            sp.dma_start(ident[:], ident_d).then_inc(consts_in, 16)
            sp.dma_start(mask[:], mask_d).then_inc(consts_in, 16)
            sp.dma_start(chunk_sum[:], chunk_d).then_inc(consts_in, 16)
            sp.dma_start(gains[:], gb).then_inc(consts_in, 16)
            sp.dma_start(W[:], wconv).then_inc(consts_in, 16)

            def load_windows(g, first=None):
                for j in range(HALF):
                    for k5 in range(2):
                        p = j * 40 + k5 * 20
                        if first is None:
                            start = (g + 1) * STEP0 + j * 2048 + k5
                            src = x5[:, start:start + 2048]
                        else:
                            src = x5[:, bass.ds(first[2 * j + k5], 2048)]
                        sp.dma_start(X[p:p + 20, :], src.rearrange("k (q n) -> k q n", q=QUAD)).then_inc(x_in, 16)

            def stack_windows(g):
                for part, row in ((0, 0), (1, 40), (0, 80)):
                    for j in range(HALF):
                        sp.dma_start(S[row:row + 40, j, :], XHL[j * 40:j * 40 + 40, part, :]).then_inc(s_in, 16)

            load_windows(-1)
            for dst, src in loads:
                sp.dma_start(dst, src).then_inc(later_in, 16)
            sp.wait_ge(w0_centred, 1)
            sp.wait_ge(w0p_zero, 1)
            for g, part in enumerate((0, 0, 1)):
                for q in range(QUAD):
                    r = g * 40 + q
                    sp.dma_start(W0P[r:r + 37:4, q, :], w0hl[:, part, :]).then_inc(w0_stacked, 16)
            sp.wait_ge(xhl_done, 1)
            stack_windows(-1)
            sp.wait_ge(xn_done, 1)
            load_windows(0)

            def step(s):
                if not active("L0", s):
                    return
                first = None
                done, read = s + 2, unit_count(13, s)
                if not isinstance(s, int):
                    done, read = sp.snap(done), sp.snap(read)
                    first = [sp.snap((s + 2) * STEP0 + j * 2048 + k5) for j in range(HALF) for k5 in range(2)]
                sp.wait_ge(xn_done, done)
                load_windows(s + 1, first)
                sp.wait_ge(e_ready[13], read)
                sp.wait_ge(xhl_done, done)
                stack_windows(s)
            run_steps(sp, step)
            sp.wait_ge(x_in, 64 * (STEPS + 2))
            sp.wait_ge(s_in, 96 * (STEPS + 1))
            sp.wait_ge(later_in, 16 * len(loads))
            if dump is not None:
                sp.wait_ge(low_done[9], unit_count(9, STEPS + 3))
                sp.dma_start(dump, H[5][:]).then_inc(x_in, 16)
                sp.wait_ge(x_in, 64 * (STEPS + 2) + 16)

        @block.tensor
        def _(pe):
            pe.wait_ge(consts_in, 96)
            pe.wait_ge(w0_centred, 1)
            nc.tensor.transpose(GB[:, 0:TAPS[0]], w0[:], ident[0:TAPS[0], 0:TAPS[0]]).then_inc(w0_turned, 1)
            pe.wait_ge(w0_expanded, 1)
            nc.tensor.matmul(GB[0:XROWS, 0:XROWS], w0x[:], w0x[:], start=True, stop=True).then_inc(gram_raw, 1)
            pe.wait_ge(gram_ready, 1)

            def gram_z(g):
                pe.wait_ge(x_in, 64 * (g + 2))
                if not (isinstance(g, int) and g < 0):
                    pe.wait_ge(xn_done, g + 1)
                nc.tensor.matmul(GB[0:XROWS, :], gram[:], X[:], start=True, stop=True).then_inc(z_ready, 1)

            def gram_v(g):
                pe.wait_ge(q_ready, g + 2)
                for n in range(4):
                    last = nc.tensor.matmul(GB[:, n * 8:n * 8 + 8], Q[:, n * 128:n * 128 + 128], chunk_sum[:],
                                            start=True, stop=True)
                last.then_inc(v_ready, 1)

            def gram_r(g):
                pe.wait_ge(rx_ready, g + 2)
                for n in range(4):
                    last = nc.tensor.matmul(GB[0:XROWS, n * 128:n * 128 + 128], RX[:, n * XROWS:(n + 1) * XROWS],
                                            ident[:], start=True, stop=True)
                last.then_inc(r_ready, 1)

            gram_z(-1)
            gram_v(-1)
            gram_r(-1)
            pe.wait_ge(weights_ready, 1)
            pe.wait_ge(w0_stacked, 16 * 12)
            pe.wait_ge(act_zero, 2)

            def conv(g, s):
                if g in (G0, G1):
                    if not isinstance(s, int) or s > FIRST[G3 if g == G0 else G2]:
                        prev = G3 if g == G0 else G2
                        pe.wait_ge(scaled[prev], 2 * (s - FIRST[prev]))
                    u = 5 if g == G0 else 13
                    pe.wait_ge(low_done[u], unit_count(u, s - 1))
                    if isinstance(s, int) and s == 1:
                        pe.wait_ge(halo[0], 1)
                    else:
                        pe.wait_ge(halo[0], s)
                elif g == G2:
                    pe.wait_ge(low_done[7], unit_count(7, s))
                else:
                    for u in (15, 9):
                        if not isinstance(s, int):
                            pe.wait_ge(low_done[u], unit_count(u, s - 1))
                        elif active(UNITS[u][0], s - 1):
                            pe.wait_ge(low_done[u], unit_count(u, s - 1))
                for n, (layer, t) in enumerate(TILES[g]):
                    taps = TAPS[layer]
                    w = 3 * (layer - 1) if layer < 6 else 14
                    src = H[layer - 1]
                    k = 0
                    for tap in range(taps):
                        c = 256 * t + tap
                        for part, wt in ((0, WH), (0, WL), (1, WH)):
                            last = nc.tensor.matmul(Y[YPAIR[g]][:, n, :], src[:, part, c:c + 255:2], wt[:, w + tap, :],
                                                    start=(k == 0), stop=(k == 3 * taps - 1))
                            k += 1
                last.then_inc(y_ready[g], 1)

            def wait_bank(u, s):
                prev = previous_user(BANK, u, s)
                if prev:
                    pe.wait_ge(gelu_done[prev[0]], unit_count(prev[0], prev[1]))

            def turn(g, s):
                for b in range(2):
                    u = UNITS.index((g, b))
                    pe.wait_ge(scaled[g], 2 * (s - FIRST[g]) + b + 1)
                    wait_bank(u, s)
                    for t in range(4):
                        if 4 * b + t < len(TILES[g]):
                            last = nc.tensor.transpose(E[BANK[u]][:, t * 128:t * 128 + 128],
                                                       T[YPAIR[g]][:, 4 * b + t, :], ident[:])
                    last.then_inc(e_ready[u], 1)

            def layer0(j, s):
                if j == 0:
                    pe.wait_ge(s_in, 96 * (s + 1))
                for q in range(QUAD):
                    u = UNITS.index(("L0", 4 * j + q))
                    wait_bank(u, s)
                    nc.tensor.matmul(E[BANK[u]][:], W0P[:, q, :], S[:, j, :], start=True, stop=True)\
                        .then_inc(e_ready[u], 1)

            def step(s):
                if active(G0, s):
                    conv(G0, s)
                    conv(G1, s)
                if active("L0", s):
                    gram_z(s)
                if active(G0, s):
                    turn(G0, s)
                if active("L0", s):
                    layer0(0, s)
                if active(G1, s):
                    turn(G1, s)
                if active("L0", s):
                    gram_v(s)
                if active(G3, s):
                    conv(G3, s)
                if active(G2, s):
                    conv(G2, s)
                if active(G3, s):
                    turn(G3, s)
                if active("L0", s):
                    layer0(1, s)
                    gram_r(s)
                if active(G2, s):
                    turn(G2, s)
            run_steps(pe, step)

        def rsqrt_ops(tiles, source, n):
            x, y0, a, y1 = (t[:, 0:n] for t in tiles)
            v = nc.vector
            yield lambda: v.tensor_scalar(x, source, 0.0, EPS_SUM, ALU.max, ALU.add)
            yield lambda: v.tensor_scalar(y0.bitcast(i32), x.bitcast(i32), -0.5, MAGIC, ALU.mult, ALU.add)
            yield lambda: v.tensor_tensor(a, y0, y0, ALU.mult)
            yield lambda: v.scalar_tensor_tensor(a, a, NEWTON1[0], x, ALU.mult, ALU.mult)
            yield lambda: v.scalar_tensor_tensor(y0, a, NEWTON1[1], y0, ALU.add, ALU.mult)
            yield lambda: v.tensor_tensor(a, y0, y0, ALU.mult)
            yield lambda: v.scalar_tensor_tensor(a, a, NEWTON2[0], x, ALU.mult, ALU.mult)
            yield lambda: v.scalar_tensor_tensor(y1, a, NEWTON2[1], y0, ALU.add, ALU.mult)

        @block.vector
        def _(dve):
            done = [0]

            def chained(ins):
                done[0] += 1
                ins.then_inc(setup, 1)
                dve.wait_ge(setup, done[0])

            nc.vector.memset(W0P[:].rearrange("p q c -> p (q c)").bitcast(f32), 0.0).then_inc(w0p_zero, 1)
            dve.wait_ge(consts_in, 96)
            chained(nc.vector.reduce_sum(w0sum[:], w0[:], AX.X))
            chained(nc.vector.tensor_scalar(w0sum[:], w0sum[:], -1.0 / CH, None, ALU.mult))
            chained(nc.vector.tensor_tensor(w0[:], w0[:], w0sum[:].to_broadcast([TAPS[0], CH]), ALU.add))
            chained(nc.vector.tensor_copy(w0hl[:, 0, :], w0[:]))
            nc.vector.tensor_tensor(w0hl[:, 1, :], w0[:], w0hl[:, 0, :], ALU.subtract).then_inc(w0_centred, 1)
            dve.wait_ge(w0_turned, 1)
            nc.vector.tensor_copy(
                w0x[:].rearrange("p (j k q) -> p j k q", j=HALF, q=QUAD),
                GB[:, 0:TAPS[0]].unsqueeze(1).unsqueeze(3).to_broadcast([128, HALF, TAPS[0], QUAD]),
            ).then_inc(w0_expanded, 1)
            dve.wait_ge(gram_raw, 1)
            nc.vector.tensor_tensor(gram[:], GB[0:XROWS, 0:XROWS], mask[:], ALU.mult).then_inc(gram_ready, 1)
            chained(nc.vector.tensor_scalar(gain_s[:], gains[:, 0:8], ROOT_CH, None, ALU.mult))
            chained(nc.vector.reduce_sum(Wsum[:], W[:], AX.X))
            chained(nc.vector.tensor_scalar(Wsum[:], Wsum[:], -1.0 / CH, None, ALU.mult))
            chained(nc.vector.tensor_tensor(W[:], W[:], Wsum[:].unsqueeze(2).to_broadcast([128, 16, CH]), ALU.add))
            chained(nc.vector.tensor_copy(WH[:], W[:]))
            nc.vector.tensor_tensor(WL[:], W[:], WH[:], ALU.subtract).then_inc(weights_ready, 1)

            def gram_q(g):
                dve.wait_ge(z_ready, g + 2)
                nc.vector.tensor_tensor(Q[:], GB[0:XROWS, :], X[:], ALU.mult).then_inc(q_ready, 1)

            def gram_rsqrt(g):
                dve.wait_ge(v_ready, g + 2)
                base = GRAM_OPS * (g + 1)
                for n, op in enumerate(rsqrt_ops(rs["x"], GB[:, 0:32], 32)):
                    if n:
                        dve.wait_ge(gram_link, base + n)
                    op().then_inc(gram_link, 1)
                dve.wait_ge(gram_link, base + GRAM_OPS)
                r = rs["x"][3][:].rearrange("p (a q) -> p a q", q=QUAD).unsqueeze(2)
                nc.vector.tensor_copy(RX[:].rearrange("p (a k q) -> p a k q", k=TAPS[0], q=QUAD),
                                      r.to_broadcast([128, 4 * HALF, TAPS[0], QUAD])).then_inc(rx_ready, 1)

            def gram_scale(g):
                dve.wait_ge(r_ready, g + 2)
                if not (isinstance(g, int) and g < 0):
                    dve.wait_ge(s_in, 96 * (g + 1))
                nc.vector.tensor_tensor(XN[:], GB[0:XROWS, :], X[:], ALU.mult).then_inc(xn_done, 1)
                dve.wait_ge(xn_done, g + 2)
                nc.vector.tensor_copy(XHL[:, 0, :], XN[:]).then_inc(xhigh, 1)
                dve.wait_ge(xhigh, g + 2)
                nc.vector.tensor_tensor(XHL[:, 1, :], XN[:], XHL[:, 0, :], ALU.subtract).then_inc(xhl_done, 1)

            def norm(g, s):
                dve.wait_ge(y_ready[g], s - FIRST[g] + 1)
                tiles = len(TILES[g])
                y = Y[YPAIR[g]]
                base = NORM_OPS * (s - FIRST[g])
                for p in range(4):
                    if 2 * p + 1 < tiles:
                        pair = y[:, 2 * p:2 * p + 2, :].rearrange("p t c -> p c t")
                    else:
                        pair = y[:, 2 * p, :].unsqueeze(2).to_broadcast([128, CH, 2])
                    nc.vector.bn_stats(stats[:, p, :], pair).then_inc(link[g], 1)
                squares = stats[:].rearrange("p a (t x) -> p (a t) x", x=3)[:, :, 2]
                for n, op in enumerate(rsqrt_ops(rs["g"], squares, 8)):
                    dve.wait_ge(link[g], base + 4 + n)
                    op().then_inc(link[g], 1)
                dve.wait_ge(link[g], base + 12)
                r = rs["g"][3]
                for b in range(2):
                    n = min(4, tiles - 4 * b)
                    u = UNITS.index((g, b))
                    before = {G0: (G3, -1), G3: (G0, 0), G1: (G2, -1), G2: (G1, 0)}[g]
                    at = s + before[1]
                    if not isinstance(s, int) or first_step(before[0]) <= at:
                        if isinstance(at, int):
                            at = min(at, last_step(before[0]))
                        v = UNITS.index((before[0], b))
                        dve.wait_ge(e_ready[v], unit_count(v, at))
                    nc.vector.tensor_tensor(T[YPAIR[g]][:, 4 * b:4 * b + n, :], y[:, 4 * b:4 * b + n, :],
                                            r[:, 4 * b:4 * b + n].unsqueeze(2).to_broadcast([128, n, CH]),
                                            ALU.mult).then_inc(scaled[g], 1)

            gram_q(-1)
            gram_rsqrt(-1)
            gram_scale(-1)

            def step(s):
                if active(G0, s):
                    norm(G0, s)
                if active("L0", s):
                    gram_q(s)
                if active(G1, s):
                    norm(G1, s)
                if active("L0", s):
                    gram_rsqrt(s)
                if active(G3, s):
                    norm(G3, s)
                if active(G2, s):
                    norm(G2, s)
                if active("L0", s):
                    gram_scale(s)
            run_steps(dve, step)

        @block.scalar
        def _(act):
            act.wait_ge(consts_in, 96)
            act.wait_ge(weights_ready, 1)
            act.wait_ge(act_zero, 2)

            def gelu(u, s):
                act.wait_ge(e_ready[u], unit_count(u, s))
                prev = previous_user(STAGE, u, s)
                if prev:
                    act.wait_ge(low_done[prev[0]], unit_count(prev[0], prev[1]))
                for layer, _, c, n in unit_target(u):
                    ins = nc.scalar.activation(A[STAGE[u]][:, c:c + n], E[BANK[u]][:, c:c + n], ACT.Gelu,
                                               scale=gain_s[:, layer:layer + 1], bias=gains[:, 8 + layer:9 + layer])
                ins.then_inc(gelu_done[u], 1)

            def high(u, s):
                act.wait_ge(gelu_done[u], unit_count(u, s))
                kind = UNITS[u][0]
                reader = {0: (G0, 0), 1: (G0, 0)}
                if kind == "L0":
                    g = G0 if UNITS[u][1] < 4 else G1
                    if not isinstance(s, int) or s >= 1:
                        act.wait_ge(y_ready[g], s - FIRST[g] + 1)
                elif kind in (G0, G1):
                    if not isinstance(s, int) or s > 1:
                        act.wait_ge(y_ready[G2], s - FIRST[G2])
                elif kind == G2:
                    if not isinstance(s, int) or s >= 2:
                        act.wait_ge(y_ready[G3], s - FIRST[G3] + 1)
                else:
                    act.wait_ge(y_ready[G3], s - FIRST[G3] + 1)
                for l, v in ((0, 13), (1, 7), (2, 15), (3, 8), (4, 9)):
                    if u == v:
                        act.wait_ge(halo[l], s - first_step(kind) + 1)
                for layer, col, c, n in unit_target(u):
                    ins = nc.scalar.activation(act_cols(layer, 0, col, n, s), A[STAGE[u]][:, c:c + n], ACT.Copy)
                ins.then_inc(high_done[u], 1)

            def step(s):
                pending = None
                for u in range(16):
                    if active(UNITS[u][0], s):
                        gelu(u, s)
                        if pending is not None:
                            high(pending, s)
                        pending = u
                    if u in (7, 15) and pending is not None:
                        high(pending, s)
                        pending = None
            run_steps(act, step)

        @block.gpsimd
        def _(pool):
            for l in range(5):
                flat = H[l][:].bitcast(f32)
                ins = nc.gpsimd.memset(flat, 0.0)
            ins.then_inc(act_zero, 1)
            nc.gpsimd.memset(zeros[:], 0.0).then_inc(act_zero, 1)
            pool.wait_ge(act_zero, 2)

            def keep_halo(l, s, g, at, kind):
                if at is not None:
                    pool.wait_ge(y_ready[g], at)
                n = LAYER_COLS[l]
                nc.gpsimd.tensor_tensor(H[l][:, :, 0:1], H[l][:, :, n:n + 1], zeros[:], ALU.add).then_inc(halo[l], 1)

            def low(u, s):
                pool.wait_ge(high_done[u], unit_count(u, s))
                for layer, col, c, n in unit_target(u):
                    ins = nc.gpsimd.tensor_tensor(act_cols(layer, 1, col, n, s), A[STAGE[u]][:, c:c + n],
                                                  act_cols(layer, 0, col, n, s), ALU.subtract)
                ins.then_inc(low_done[u], 1)

            def step(s):
                sym = not isinstance(s, int)
                for u in range(16):
                    kind = UNITS[u][0]
                    if not active(kind, s):
                        continue
                    if u == 0:
                        keep_halo(1, s, G2, s - 1 if sym or s > 1 else None, kind)
                    if u == 10:
                        keep_halo(0, s, G0, s if sym or s >= 1 else None, kind)
                    if u == 8:
                        keep_halo(3, s, G3, s - 1, kind)
                        keep_halo(4, s, G3, s - 1, kind)
                    if u == 14:
                        keep_halo(2, s, G3, s - 1 if sym or s >= 2 else None, kind)
                    low(u, s)
            run_steps(pool, step)



D = 192
TP = POS_PAD // 3
THIRDS = 3
HEADS, HD = 12, 16
EXPERTS, INTER = 8, 128
D2 = D - 128
PAIRS = BATCH * (BATCH + 1) // 2
POOL_Q = (1, 3, 4, 6, 7)


def tokens_part(nc, keep, wt, out):
    ident, gains, gain_s, WH, WL, H5 = keep
    ctx = ExitStack()
    with ctx:
        def sb(name, shape, dt=f32):
            return ctx.enter_context(nc.sbuf_tensor(name, shape, dt))

        def sem(name):
            return ctx.enter_context(nc.semaphore(name))

        B = [ctx.enter_context(nc.psum_tensor(f"bank{k}", [128, COLS], f32)) for k in range(8)]
        ones = sb("ones", [1, 128])
        TA = sb("token_rows", [TP, 8, 128])
        h6 = sb("h6", [128, 8 * TP])
        z = h6
        h0 = [sb(f"resid{k}", [TP, 8, D]) for k in range(2)]
        xn = sb("xn", [TP, 8, D])
        XT1 = sb("xt1", [128, 8 * TP])
        XT2 = sb("xt2", [D2, 8 * TP])
        YT1 = [sb(f"yt1_{k}", [128, 8 * TP]) for k in range(2)]
        YT2 = [sb(f"yt2_{k}", [D2, 8 * TP]) for k in range(2)]
        KV = sb("kv", [TP, 8, 2 * D])
        q0 = sb("q0", [TP, D])
        vn = sb("vn", [TP, 8, D])
        prod = sb("prod", [TP, PAIRS, D])
        prod0 = xn
        PQ = [prod[:, 8 * k:8 * k + 8, :] for k in range(4)]
        sv = sb("sv", [TP, PAIRS, HEADS])
        s0 = sb("s0", [TP, 8, HEADS])
        m0 = sb("m0", [TP, HEADS])
        EX = sb("ex", [TP, 64, HEADS])
        Z = sb("zsum", [TP, 8, HEADS])
        RZ = sb("rz", [TP, 8, HEADS])
        O = vn
        n2 = sb("n2", [TP, 96])
        stats = sb("tstats", [TP, 4, BN])
        rt = [sb(f"t_rsqrt{n}", [TP, 96]) for n in range(4)]
        sc = sb("sc", [TP, 8, EXPERTS])
        sb_ = sb("sbias", [TP, 8, EXPERTS])
        gs = sb("gs", [TP, 8, 4])
        gk = sb("gk", [TP, 8, 4])
        gc = sb("gc", [TP, 8, 8])
        ek = sb("ek", [TP, 8, EXPERTS])
        em = sb("em", [TP, 8, EXPERTS])
        cw = sb("cw", [TP, 8, EXPERTS])
        wsum = sb("wsum", [TP, 8])
        cwT = [sb(f"cwt{k}", [EXPERTS, 8 * TP]) for k in range(2)]
        sl = [sb(f"silu{k}", [128, 4 * TP]) for k in range(2)]
        U = sb("hidden", [128, EXPERTS + 1, 4 * TP])

        names = ("y6 t6 e6 h6 fl_in fl_t fl_e z pj h0 x_t xt_e xt kv kv_s vn_r prod_p prod_v sv s0 ex0in ex en pqm_p pqm_v "
                 "pq_free o ot_e ot op h1 yn yt_e yt gate sig cw cwt_e cwt ones f1 f3 fc silu gated hid fo res").split()
        S = {n: sem("s_" + n) for n in names}
        link = sem("token_link")
        out_left = [sem(f"out_left{i}") for i in range(THIRDS)]
        block = ctx.enter_context(nc.Block())
        NFE = EXPERTS + 1

        def tile_cols(t):
            return slice((t % 4) * TP, (t % 4 + 1) * TP)

        @block.tensor
        def _(pe):
            pe.wait_ge(S["ones"], 1)

            def turn(src, banks, width, rows, sem_):
                for t in range(8):
                    last = nc.tensor.transpose(B[banks[t // 4]][0:width, tile_cols(t)], src(t), ident[0:rows, 0:rows])
                    if t % 4 == 3:
                        last.then_inc(sem_, 1)

            def front(i):
                if i:
                    pe.wait_ge(S["cwt"], 2 * i)
                for t in range(8):
                    base = 2 * (t * POS_PAD + TP * i) + 257
                    k = 0
                    for tap in range(2):
                        for part, w in ((0, WH), (0, WL), (1, WH)):
                            c = base + tap
                            last = nc.tensor.matmul(B[t // 4][0:TP, t % 4 * 128:t % 4 * 128 + 128],
                                                    H5[:, part, c:c + 2 * TP - 1:2], w[:, 14 + tap, :],
                                                    start=(k == 0), stop=(k == 5))
                            k += 1
                    if t % 4 == 3:
                        last.then_inc(S["y6"], 1)
                pe.wait_ge(S["t6"], 2 * i + 2)
                turn(lambda t: TA[:, t, :], (2, 3), 128, TP, S["e6"])
                pe.wait_ge(S["h6"], 2 * i + 2)
                for t in range(8):
                    last = nc.tensor.transpose(B[t // 4][0:TP, t % 4 * 128:t % 4 * 128 + 128], h6[:, t * TP:(t + 1) * TP], ident[:])
                    if t % 4 == 3:
                        last.then_inc(S["fl_in"], 1)
                pe.wait_ge(S["fl_t"], i + 1)
                turn(lambda t: TA[:, t, :], (2, 3), 128, TP, S["fl_e"])
                pe.wait_ge(S["z"], 2 * i + 2)
                for t in range(8):
                    o = B[t // 2][0:TP, t % 2 * D:t % 2 * D + D]
                    nc.tensor.matmul(o, z[:, t * TP:(t + 1) * TP], wt["proj"][:], start=True, stop=False)
                    last = nc.tensor.matmul(o, ones[:, 0:TP], wt["proj_b"][:], start=False, stop=True)
                    if t % 2:
                        last.then_inc(S["pj"], 1)
                pe.wait_ge(S["x_t"], 2 * i + 1)
                turn(lambda t: xn[:, t, 0:128], (0, 1), 128, TP, S["xt_e"])
                turn(lambda t: xn[:, t, 128:D], (2, 3), D2, TP, S["xt_e"])
                pe.wait_ge(S["xt"], 8 * i + 4)
                for t in range(8):
                    b = B[t % 4]
                    if t >= 4:
                        pe.wait_ge(S["kv_s"], 9 * i + t - 3)
                    c = slice(t * TP, (t + 1) * TP)
                    nc.tensor.matmul(b[0:TP, 0:2 * D], XT1[:, c], wt["qkv1"][:, D:3 * D], start=True, stop=False)
                    nc.tensor.matmul(b[0:TP, 0:2 * D], XT2[:, c], wt["qkv2"][:, D:3 * D], start=False, stop=True).then_inc(S["kv"], 1)
                pe.wait_ge(S["kv_s"], 9 * i + 5)
                c = slice(0, TP)
                nc.tensor.matmul(B[0][0:TP, 0:D], XT1[:, c], wt["qkv1"][:, 0:D], start=True, stop=False)
                nc.tensor.matmul(B[0][0:TP, 0:D], XT2[:, c], wt["qkv2"][:, 0:D], start=False, stop=True).then_inc(S["kv"], 1)
                pe.wait_ge(S["kv_s"], 9 * i + 9)
                pe.wait_ge(S["o"], 8 * i + 8)
                turn(lambda t: O[:, t, 0:128], (0, 1), 128, TP, S["ot_e"])
                turn(lambda t: O[:, t, 128:D], (2, 3), D2, TP, S["ot_e"])
                pe.wait_ge(S["xt"], 8 * i + 8)
                for t in range(8):
                    o = B[t // 2][0:TP, t % 2 * D:t % 2 * D + D]
                    c = slice(t * TP, (t + 1) * TP)
                    nc.tensor.matmul(o, XT1[:, c], wt["op1"][:], start=True, stop=False)
                    nc.tensor.matmul(o, XT2[:, c], wt["op2"][:], start=False, stop=False)
                    last = nc.tensor.matmul(o, ones[:, 0:TP], wt["op_b"][:], start=False, stop=True)
                    if t % 2:
                        last.then_inc(S["op"], 1)
                pe.wait_ge(S["x_t"], 2 * i + 2)
                turn(lambda t: xn[:, t, 0:128], (0, 1), 128, TP, S["yt_e"])
                turn(lambda t: xn[:, t, 128:D], (2, 3), D2, TP, S["yt_e"])
                pe.wait_ge(S["yt"], 4 * i + 4)
                for t in range(8):
                    c = slice(t * TP, (t + 1) * TP)
                    o = B[0][0:TP, t * 8:t * 8 + 8]
                    nc.tensor.matmul(o, YT1[i % 2][:, c], wt["gate1"][:], start=True, stop=False)
                    last = nc.tensor.matmul(o, YT2[i % 2][:, c], wt["gate2"][:], start=False, stop=True)
                last.then_inc(S["gate"], 1)
                pe.wait_ge(S["cw"], i + 1)
                turn(lambda t: cw[:, t, :], (1, 2), EXPERTS, TP, S["cwt_e"])

            def back(i):
                pe.wait_ge(S["cwt"], 2 * i + 2)
                for hh in range(2):
                    c = slice(hh * 4 * TP, (hh + 1) * 4 * TP)
                    for e in range(NFE):
                        n = (2 * i + hh) * NFE + e
                        nsc = (2 * i + hh) * EXPERTS + e
                        if n:
                            pe.wait_ge(S["silu"], n)
                        nc.tensor.matmul(B[4][:, 0:4 * TP], wt["w1a"][:, e, :], YT1[i % 2][:, c], start=True, stop=False)
                        nc.tensor.matmul(B[4][:, 0:4 * TP], wt["w1b"][:, e, :], YT2[i % 2][:, c], start=False, stop=True).then_inc(S["f1"], 1)
                        if n:
                            pe.wait_ge(S["gated"], n)
                        nc.tensor.matmul(B[5][:, 0:4 * TP], wt["w3a"][:, e, :], YT1[i % 2][:, c], start=True, stop=False)
                        nc.tensor.matmul(B[5][:, 0:4 * TP], wt["w3b"][:, e, :], YT2[i % 2][:, c], start=False, stop=True).then_inc(S["f3"], 1)
                        if e < EXPERTS:
                            if n:
                                pe.wait_ge(S["hid"], n)
                            nc.tensor.matmul(B[6][:, 0:4 * TP], wt["pick"][:, e, :], cwT[i % 2][:, c], start=True, stop=True).then_inc(S["fc"], 1)
                    pe.wait_ge(S["hid"], (2 * i + hh + 1) * NFE)
                    for t in range(4):
                        m = (2 * i + hh) * 4 + t
                        if m:
                            pe.wait_ge(S["res"], m)
                        for e in range(NFE):
                            last = nc.tensor.matmul(B[7][0:TP, 0:D], U[:, e, t * TP:(t + 1) * TP], wt["w2"][:, e, :],
                                                    start=(e == 0), stop=(e == NFE - 1))
                        last.then_inc(S["fo"], 1)

            for i in range(THIRDS):
                front(i)
                back(i)

        @block.scalar
        def _(act):
            A = nc.scalar.activation

            def copies(dst, banks, rows, sem_in, base, sem_out):
                for b in range(2):
                    act.wait_ge(sem_in, base + b + 1)
                    A(dst[:, b * 4 * TP:(b + 1) * 4 * TP], B[banks[b]][0:rows, 0:4 * TP], ACT.Copy).then_inc(sem_out, 1)

            def front(i):
                for b in range(2):
                    act.wait_ge(S["e6"], 2 * i + b + 1)
                    A(h6[:, b * 4 * TP:(b + 1) * 4 * TP], B[2 + b][:, 0:4 * TP], ACT.Gelu,
                      scale=gain_s[:, 6:7], bias=gains[:, 14:15]).then_inc(S["h6"], 1)
                for b in range(2):
                    act.wait_ge(S["fl_e"], 2 * i + b + 1)
                    A(z[:, b * 4 * TP:(b + 1) * 4 * TP], B[2 + b][:, 0:4 * TP], ACT.Identity,
                      scale=gain_s[:, 7:8], bias=gains[:, 15:16]).then_inc(S["z"], 1)
                if i > 1:
                    act.wait_ge(out_left[i - 2], 16 * 8)
                for b in range(4):
                    act.wait_ge(S["pj"], 4 * i + b + 1)
                    A(h0[i % 2][:, 2 * b:2 * b + 2, :], B[b][0:TP, 0:2 * D].rearrange("p (t d) -> p t d", t=2), ACT.Copy).then_inc(S["h0"], 1)
                copies(XT1, (0, 1), 128, S["xt_e"], 4 * i, S["xt"])
                copies(XT2, (2, 3), D2, S["xt_e"], 4 * i + 2, S["xt"])
                for t in range(8):
                    act.wait_ge(S["kv"], 9 * i + t + 1)
                    A(KV[:, t, :], B[t % 4][0:TP, 0:2 * D], ACT.Copy).then_inc(S["kv_s"], 1)
                act.wait_ge(S["kv"], 9 * i + 9)
                A(q0[:], B[0][0:TP, 0:D], ACT.Copy).then_inc(S["kv_s"], 1)
                act.wait_ge(S["sv"], i + 1)
                off = 0
                for d in range(8):
                    if d < 7:
                        A(EX[:, 9 + d:9 + d + 9 * (6 - d) + 1:9, :], sv[:, off + 1:off + 8 - d, :], ACT.Exp, scale=0.25)
                    if d:
                        A(EX[:, 8 * d:8 * d + 9 * (7 - d) + 1:9, :], sv[:, off:off + 8 - d, :], ACT.Exp, scale=0.25)
                    off += 8 - d
                act.wait_ge(S["ex0in"], i + 1)
                A(EX[:, 0:8, :], s0[:], ACT.Exp, scale=0.25).then_inc(S["ex"], 1)
                copies(XT1, (0, 1), 128, S["ot_e"], 4 * i, S["xt"])
                copies(XT2, (2, 3), D2, S["ot_e"], 4 * i + 2, S["xt"])
                copies(YT1[i % 2], (0, 1), 128, S["yt_e"], 4 * i, S["yt"])
                copies(YT2[i % 2], (2, 3), D2, S["yt_e"], 4 * i + 2, S["yt"])
                act.wait_ge(S["gate"], i + 1)
                A(sc[:], B[0][0:TP, 0:64].rearrange("p (t e) -> p t e", t=8), ACT.Sigmoid).then_inc(S["sig"], 1)
                copies(cwT[i % 2], (1, 2), EXPERTS, S["cwt_e"], 2 * i, S["cwt"])

            def back(i):
                for hh in range(2):
                    for e in range(NFE):
                        n = (2 * i + hh) * NFE + e
                        act.wait_ge(S["f1"], n + 1)
                        if n > 1:
                            act.wait_ge(S["gated"], n - 1)
                        A(sl[n % 2][:], B[4][:, 0:4 * TP], ACT.Silu).then_inc(S["silu"], 1)

            for i in range(THIRDS):
                front(i)
                back(i)

        @block.vector
        def _(dve):
            v = nc.vector
            count = [0]

            def chained(ins):
                count[0] += 1
                ins.then_inc(link, 1)
                dve.wait_ge(link, count[0])

            def rsqrt(source, n, low, eps, factor=1.0):
                x, y0, a, y1 = (t[:, 0:n] for t in rt)
                chained(v.tensor_scalar(x, source, low, eps, ALU.max, ALU.add))
                chained(v.tensor_scalar(y0.bitcast(i32), x.bitcast(i32), -0.5, MAGIC, ALU.mult, ALU.add))
                chained(v.tensor_tensor(a, y0, y0, ALU.mult))
                chained(v.scalar_tensor_tensor(a, a, NEWTON1[0], x, ALU.mult, ALU.mult))
                chained(v.scalar_tensor_tensor(y0, a, NEWTON1[1], y0, ALU.add, ALU.mult))
                chained(v.tensor_tensor(a, y0, y0, ALU.mult))
                chained(v.scalar_tensor_tensor(a, a, NEWTON2[0] * factor, x, ALU.mult, ALU.mult))
                chained(v.scalar_tensor_tensor(y1, a, NEWTON2[1] * factor, y0, ALU.add, ALU.mult))
                return y1

            halves = stats[:].rearrange("p a (t x) -> p (a t) x", x=3)
            mean, squares = halves[:, :, 1], halves[:, :, 2]

            def token_norm(src, n, dst, done):
                for p in range(4):
                    chained(v.bn_stats(stats[:, p, :], src[:, 2 * p:2 * p + 2, :].rearrange("p t c -> p c t")))
                r = rsqrt(squares, 8, 0.0, n * 1e-5, math.sqrt(n))
                for t in range(8):
                    last = v.tensor_scalar(dst[:, t, :], src[:, t, :], halves[:, t, 1:2], r[:, t:t + 1], ALU.subtract, ALU.mult)
                last.then_inc(done, 1)

            def front(i):
                for b in range(2):
                    dve.wait_ge(S["y6"], 2 * i + b + 1)
                    for p in range(2):
                        q = 2 * b + p
                        chained(v.bn_stats(stats[:, q, :], B[b][0:TP, p * 256:p * 256 + 256].rearrange("p (t c) -> p c t", t=2)))
                r = rsqrt(squares, 8, 0.0, EPS_SUM)
                for b in range(2):
                    v.tensor_tensor(TA[:, 4 * b:4 * b + 4, :], B[b][0:TP, :].rearrange("p (t c) -> p t c", t=4),
                                    r[:, 4 * b:4 * b + 4].unsqueeze(2).to_broadcast([TP, 4, 128]), ALU.mult).then_inc(S["t6"], 1)
                for b in range(2):
                    dve.wait_ge(S["fl_in"], 2 * i + b + 1)
                    for p in range(2):
                        q = 2 * b + p
                        chained(v.bn_stats(stats[:, q, :], B[b][0:TP, p * 256:p * 256 + 256].rearrange("p (t c) -> p c t", t=2)))
                r = rsqrt(squares, 8, 0.0, EPS_SUM)
                for t in range(8):
                    last = v.tensor_scalar(TA[:, t, :], B[t // 4][0:TP, t % 4 * 128:t % 4 * 128 + 128], halves[:, t, 1:2],
                                           r[:, t:t + 1], ALU.subtract, ALU.mult)
                last.then_inc(S["fl_t"], 1)
                dve.wait_ge(S["h0"], 4 * i + 4)
                token_norm(h0[i % 2], D, xn, S["x_t"])
                dve.wait_ge(S["kv_s"], 9 * i + 9)
                V = KV[:, :, D:2 * D]
                Vh = V.rearrange("p b (h d) -> p b h d", h=HEADS)
                chained(v.tensor_tensor(prod0[:], V, V, ALU.mult))
                chained(v.reduce_sum(n2[:], prod0[:].rearrange("p b (h d) -> p (b h) d", h=HEADS), AX.X))
                r = rsqrt(n2[:], 96, 1e-12, 0.0)
                rb = r.rearrange("p (b h) -> p b h", b=8).unsqueeze(3).to_broadcast([TP, 8, HEADS, HD])
                v.tensor_tensor(vn[:].rearrange("p b (h d) -> p b h d", h=HEADS), Vh, rb, ALU.mult).then_inc(S["vn_r"], 1)
                chained(v.tensor_tensor(prod0[:], KV[:, :, 0:D], q0[:].unsqueeze(1).to_broadcast([TP, 8, D]), ALU.mult))
                chained(v.reduce_sum(s0[:], prod0[:].rearrange("p b (h d) -> p b h d", h=HEADS), AX.X))
                chained(v.reduce_max(m0[:], s0[:].rearrange("p k h -> p h k"), AX.X))
                v.tensor_tensor(s0[:], s0[:], m0[:].unsqueeze(1).to_broadcast([TP, 8, HEADS]), ALU.subtract).then_inc(S["ex0in"], 1)
                dve.wait_ge(S["vn_r"], i + 1)
                off = 0
                for d in range(3):
                    last = v.tensor_tensor(prod[:, off:off + 8 - d, :], vn[:, 0:8 - d, :], vn[:, d:8, :], ALU.mult)
                    off += 8 - d
                chained(last)
                dve.wait_ge(S["prod_p"], i + 1)
                v.reduce_sum(sv[:], prod[:].rearrange("p a (h d) -> p a h d", h=HEADS), AX.X).then_inc(S["sv"], 1)
                dve.wait_ge(S["ex"], i + 1)
                EQ = EX[:].rearrange("p (q k) h -> p q k h", q=8)
                chained(v.reduce_sum(Z[:], EQ.rearrange("p q k h -> p q h k"), AX.X))
                chained(v.reciprocal(RZ[:], Z[:]))
                v.tensor_tensor(EQ, EQ, RZ[:].unsqueeze(2).to_broadcast([TP, 8, 8, HEADS]), ALU.mult).then_inc(S["en"], 1)
                dve.wait_ge(S["en"], i + 1)
                pool_n = 0
                own = 0
                for q in [0, 1, 3, 2, 4, 6, 5, 7]:
                    if q in POOL_Q:
                        pool_n += 1
                        dve.wait_ge(S["pqm_p"], len(POOL_Q) * i + pool_n)
                        src = PQ[2 + (len(POOL_Q) * i + pool_n - 1) % 2]
                    else:
                        src = PQ[own % 2]
                        w = EQ[:, q, :, :].unsqueeze(3).to_broadcast([TP, 8, HEADS, HD])
                        chained(v.tensor_tensor(src.rearrange("p b (h d) -> p b h d", h=HEADS), Vh, w, ALU.mult))
                        own += 1
                    ins = v.reduce_sum(O[:, q, :], src.rearrange("p k x -> p x k"), AX.X).then_inc(S["o"], 1)
                for b in range(4):
                    dve.wait_ge(S["op"], 4 * i + b + 1)
                    r2 = h0[i % 2][:, 2 * b:2 * b + 2, :]
                    chained(v.tensor_tensor(r2, B[b][0:TP, 0:2 * D].rearrange("p (t d) -> p t d", t=2), r2, ALU.add))
                token_norm(h0[i % 2], D, xn, S["x_t"])
                dve.wait_ge(S["sig"], i + 1)
                chained(v.tensor_tensor(sb_[:], sc[:], wt["gate_b"][:].unsqueeze(1).to_broadcast([TP, 8, EXPERTS]), ALU.add))
                two = sb_[:].rearrange("p t (g k) -> p t g k", k=2)
                chained(v.tensor_tensor(gs[:], two[:, :, :, 0], two[:, :, :, 1], ALU.add))

                def rank(x, k, n):
                    chained(v.memset(k[:], 0.0))
                    for d in range(1, n):
                        c = gc[:, :, 0:n - d]
                        chained(v.tensor_tensor(c, x[:, :, 0:n - d], x[:, :, d:n], ALU.is_ge))
                        chained(v.tensor_tensor(k[:, :, d:n], k[:, :, d:n], c, ALU.add))
                        chained(v.scalar_tensor_tensor(k[:, :, 0:n - d], k[:, :, 0:n - d], 1.0, c, ALU.add, ALU.subtract))

                rank(gs, gk, 4)
                chained(v.tensor_scalar(gk[:], gk[:], 1.5, None, ALU.is_lt))
                chained(v.tensor_scalar(gs[:], gk[:], -1.0, 1e30, ALU.add, ALU.mult))
                gb4 = lambda a: a[:].unsqueeze(3).to_broadcast([TP, 8, 4, 2])
                e4 = em[:].rearrange("p t (g k) -> p t g k", k=2)
                chained(v.tensor_tensor(e4, two, gb4(gk), ALU.mult))
                chained(v.tensor_tensor(e4, e4, gb4(gs), ALU.add))
                rank(em, ek, 8)
                chained(v.tensor_scalar(ek[:], ek[:], 1.5, None, ALU.is_lt))
                chained(v.tensor_tensor(cw[:], ek[:], sc[:], ALU.mult))
                chained(v.reduce_sum(wsum[:], cw[:], AX.X))
                chained(v.tensor_scalar(wsum[:], wsum[:], 1e-6, None, ALU.add))
                chained(v.reciprocal(wsum[:], wsum[:]))
                v.tensor_tensor(cw[:], cw[:], wsum[:].unsqueeze(2).to_broadcast([TP, 8, EXPERTS]), ALU.mult).then_inc(S["cw"], 1)

            def back(i):
                for hh in range(2):
                    for e in range(NFE):
                        n = (2 * i + hh) * NFE + e
                        dve.wait_ge(S["silu"], n + 1)
                        dve.wait_ge(S["f3"], n + 1)
                        if e == 0 and n:
                            dve.wait_ge(S["fo"], (2 * i + hh) * 4)
                        g = U[:, e, :]
                        v.tensor_tensor(g, sl[n % 2][:], B[5][:, 0:4 * TP], ALU.mult).then_inc(S["gated"], 1)
                        dve.wait_ge(S["gated"], n + 1)
                        if e < EXPERTS:
                            dve.wait_ge(S["fc"], (2 * i + hh) * EXPERTS + e + 1)
                            v.tensor_tensor(g, g, B[6][:, 0:4 * TP], ALU.mult).then_inc(S["hid"], 1)
                        else:
                            v.tensor_copy(wsum[:, 0:1], wsum[:, 1:2]).then_inc(S["hid"], 1)
                    for t in range(4):
                        m = (2 * i + hh) * 4 + t
                        dve.wait_ge(S["fo"], m + 1)
                        tt = hh * 4 + t
                        v.tensor_tensor(h0[i % 2][:, tt, :], B[7][0:TP, 0:D], h0[i % 2][:, tt, :], ALU.add).then_inc(S["res"], 1)

            v.memset(ones[:], 1.0).then_inc(S["ones"], 1)
            for i in range(THIRDS):
                front(i)
                back(i)

        @block.gpsimd
        def _(pool):
            for i in range(THIRDS):
                pool.wait_ge(S["vn_r"], i + 1)
                off = 21
                for d in range(3, 8):
                    last = nc.gpsimd.tensor_tensor(prod[:, off:off + 8 - d, :], vn[:, 0:8 - d, :], vn[:, d:8, :], ALU.mult)
                    off += 8 - d
                last.then_inc(S["prod_p"], 1)
                pool.wait_ge(S["en"], i + 1)
                EQ = EX[:].rearrange("p (q k) h -> p q k h", q=8)
                Vh = KV[:, :, D:2 * D].rearrange("p b (h d) -> p b h d", h=HEADS)
                for n, q in enumerate(POOL_Q):
                    m = len(POOL_Q) * i + n
                    if n >= 2:
                        order = [0, 1, 3, 2, 4, 6, 5, 7]
                        pool.wait_ge(S["o"], 8 * i + order.index(POOL_Q[n - 2]) + 1)
                    w = EQ[:, q, :, :].unsqueeze(3).to_broadcast([TP, 8, HEADS, HD])
                    nc.gpsimd.tensor_tensor(PQ[2 + m % 2].rearrange("p b (h d) -> p b h d", h=HEADS), Vh, w, ALU.mult).then_inc(S["pqm_p"], 1)

        @block.sync
        def _(sp):
            for i in range(THIRDS):
                rows = TP if i < THIRDS - 1 else POS - TP * (THIRDS - 1)
                for t in range(8):
                    sp.wait_ge(S["res"], 8 * i + t + 1)
                    sp.dma_start(out[t, i * TP:i * TP + rows, :], h0[i % 2][0:rows, t, :]).then_inc(out_left[i], 16)
            for left in out_left:
                sp.wait_ge(left, 16 * 8)


WEIGHTS = {
    "proj": [128, D], "proj_b": [1, D], "qkv1": [128, 3 * D], "qkv2": [D2, 3 * D],
    "op1": [128, D], "op2": [D2, D], "op_b": [1, D], "gate1": [128, EXPERTS], "gate2": [D2, EXPERTS],
    "gate_b": [TP, EXPERTS], "w1a": [128, 9, INTER], "w1b": [D2, 9, INTER], "w3a": [128, 9, INTER],
    "w3b": [D2, 9, INTER], "w2": [INTER, 9, D], "pick": [EXPERTS, EXPERTS, 128],
}


def audio_tower(nc, d, out):
    ctx = ExitStack()
    with ctx:
        def sb(name, shape, dt=f32):
            return ctx.enter_context(nc.sbuf_tensor(name, shape, dt))
        ident = sb("ident", [128, 128])
        gains = sb("gains", [128, 16])
        gain_s = sb("gain_scaled", [128, 8])
        WH = sb("conv_w_high", [128, 16, CH], f16)
        WL = sb("conv_w_low", [128, 16, CH], f16)
        H5 = sb("act5", [128, 2, (STEPS + 2) * 128], f16)
        wt = {n: sb("w_" + n, shape) for n, shape in WEIGHTS.items()}
        src = {
            "proj": d["proj"], "proj_b": d["proj_b"], "qkv1": d["wqkv"][0:128, :], "qkv2": d["wqkv"][128:D, :],
            "op1": d["wo"][0:128, :], "op2": d["wo"][128:D, :], "op_b": d["wo_b"],
            "gate1": d["gate"][0:128, :], "gate2": d["gate"][128:D, :], "gate_b": d["gate_b"],
            "w1a": d["w1"][0:128], "w1b": d["w1"][128:D], "w3a": d["w3"][0:128], "w3b": d["w3"][128:D],
            "w2": d["w2"], "pick": d["pick"],
        }
        loads = [(wt[n][:], src[n]) for n in WEIGHTS]
        keep = (ident, gains, gain_s, WH, WL, H5)
        conv_tower(nc, d["x5"], d["w0t"], d["wconv"], d["gb"], (d["ident"], d["mask"], d["chunk_sum"]), (*keep, loads))
        tokens_part(nc, keep, wt, out)


def layout(inputs):
    f = lambda name: np.asarray(inputs[name])
    x = np.zeros(5 * X_LEN, np.float32)
    flat = f("x").reshape(-1)
    x[5:5 + flat.size] = flat
    x5 = np.ascontiguousarray(x.reshape(X_LEN, 5).T)
    t = "L0_tok_"
    w0t = np.ascontiguousarray(f(t + "conv_w0")[:, 0, :].T)
    wconv = np.concatenate([f(f"{t}conv_w{l}").transpose(1, 2, 0) for l in range(1, 7)], axis=1)
    gb = np.stack([f(f"{t}ln_g{l}") for l in range(7)] + [f(t + "fln_g")] + [f(f"{t}ln_b{l}") for l in range(7)]
                  + [f(t + "fln_b")], axis=1)
    rows = np.arange(XROWS)
    chunk = rows // 40 * 4 + rows % 4
    n = "L0_ffn_"
    both = lambda a, b, axes: np.concatenate([f(n + a), f(n + b)[None]], axis=0).transpose(axes)
    pick = np.zeros((EXPERTS, EXPERTS, 128), np.float32)
    pick[np.arange(EXPERTS), np.arange(EXPERTS)] = 1.0
    made = {
        "x5": x5, "w0t": w0t, "wconv": wconv, "gb": gb,
        "ident": np.eye(128, dtype=np.float32),
        "mask": (chunk[:, None] == chunk[None, :]).astype(np.float32),
        "chunk_sum": (chunk[:, None] == np.arange(8)[None, :]).astype(np.float32),
        "proj": f(t + "proj_w"), "proj_b": f(t + "proj_b")[None],
        "wqkv": f("L0_attn_w_qkv").T, "wo": f("L0_attn_w_proj").T, "wo_b": f("L0_attn_b_proj")[None],
        "gate": f(n + "gate_weight").T, "gate_b": np.broadcast_to(f(n + "gate_bias")[None], (TP, EXPERTS)),
        "w1": both("w1", "sw1", (2, 0, 1)), "w3": both("w3", "sw3", (2, 0, 1)), "w2": both("w2", "sw2", (2, 0, 1)),
        "pick": pick,
    }
    return {k: np.ascontiguousarray(a) for k, a in made.items()}


def kernel(**inputs):
    import concourse.bacc as bacc
    from concourse.bass_utils import run_bass_kernel_spmd

    arrays = {f"in_{k}": a for k, a in layout(inputs).items()}
    nc = bacc.Bacc("TRN2", target_bir_lowering=False, num_devices=1)
    d = {k[3:]: nc.dram_tensor(k, a.shape, mybir.dt.from_np(a.dtype), kind="ExternalInput").ap() for k, a in arrays.items()}
    out = nc.dram_tensor("out", (BATCH, POS, D), f32, kind="ExternalOutput").ap()
    audio_tower(nc, d, out)
    r = run_bass_kernel_spmd(nc, [arrays], core_ids=[0])
    return r.results[0]["out"]
```

```python
import math
from contextlib import ExitStack

import numpy as np
import concourse.bass as bass
from concourse import mybir

f32 = mybir.dt.float32
f16 = mybir.dt.float16
i32 = mybir.dt.int32
ACT = mybir.ActivationFunctionType
ALU = mybir.AluOpType
AX = mybir.AxisListType

CH = 128
BATCH, POS = 8, 374
POS_PAD = 375
TAPS = [10, 3, 3, 3, 3, 2, 2]
STEP0 = 4096
LAYER_COLS = [STEP0 >> l for l in range(6)]
STEPS = -(-(BATCH * POS_PAD * 64 + 1) // STEP0)
LAG = 5
BN = 6
EPS_SUM = CH * 1e-5
ROOT_CH = math.sqrt(CH)
QUAD, HALF = 4, 2
COLS = 512
XROWS = HALF * TAPS[0] * QUAD
SROWS = 3 * TAPS[0] * QUAD
X_LEN = STEP0 * (STEPS + 2) + 8

MAGIC = float(0x5F1FFFF9)
NEWTON1 = (-0.703952253, 0.703952253 * 2.38924456)
NEWTON2 = (-0.5 * (1 + 3.2e-7), 1.5 * (1 + 3.2e-7))

G0, G1, G2, G3 = range(4)
FIRST = {G0: 1, G1: 1, G2: 1, G3: 2}
LAST = {G0: STEPS, G1: STEPS, G2: STEPS, G3: STEPS + 3}
UNITS = [("L0", 6), ("L0", 7), (G2, 0), (G2, 1), ("L0", 0), ("L0", 1), (G0, 0), ("L0", 2),
         (G0, 1), ("L0", 3), (G1, 0), (G1, 1), ("L0", 4), ("L0", 5), (G3, 0), (G3, 1)]
BEHIND = [1] * 4 + [0] * 12
UNIT = {kind: u for u, kind in enumerate(UNITS)}
BANK = [0, 1, 2, 0, 1, 2, 0, 1, 2, 0, 1, 2, 0, 1, 2, 1]
STAGE = [u % 4 for u in range(16)]
TILES = {G0: [(1, t) for t in range(8)], G1: [(1, t) for t in range(8, 16)],
         G2: [(2, t) for t in range(8)],
         G3: [(3, t) for t in range(4)] + [(4, 0), (4, 1), (5, 0)]}
YPAIR = {G0: 0, G1: 1, G3: 0, G2: 1}
NORM_OPS = 12
GRAM_OPS = 8


def first_step(kind):
    return 0 if kind == "L0" else FIRST[kind]


def last_step(kind):
    return STEPS - 1 if kind == "L0" else LAST[kind]


def unit_count(u, s):
    return s - first_step(UNITS[u][0]) + 1


def active(kind, s):
    return not isinstance(s, int) or first_step(kind) <= s <= last_step(kind)


def previous_user(place, u, n):
    at = n
    for _ in range(4):
        order = range(u - 1, -1, -1) if at is n else range(15, -1, -1)
        for v in order:
            if place[v] == place[u] and active(UNITS[v][0], at - BEHIND[v]):
                return v, at - BEHIND[v]
        at = at - 1
        if isinstance(at, int) and at < 0:
            return None
    return None


def conv_tower(nc, x5, w0t, wconv, gb, consts, keep, dump=None):
    ident_d, mask_d, chunk_d = consts
    ident, gains, gain_s, WH, WL, H5, loads, splits = keep
    ctx = ExitStack()
    with ctx:
        def sb(name, shape, dt=f32):
            return ctx.enter_context(nc.sbuf_tensor(name, shape, dt))

        def ps(name, shape):
            return ctx.enter_context(nc.psum_tensor(name, shape, f32))

        def sem(name):
            return ctx.enter_context(nc.semaphore(name))

        mask = sb("same_chunk_mask", [XROWS, XROWS])
        chunk_sum = sb("chunk_sum", [XROWS, 8])
        W = sb("conv_w", [128, 16, CH])
        Wsum = sb("conv_w_sum", [128, 16])
        w0 = sb("w0", [TAPS[0], CH])
        w0sum = sb("w0_sum", [TAPS[0], 1])
        w0hl = sb("w0_high_low", [TAPS[0], 2, CH], f16)
        w0x = sb("w0_expanded", [128, XROWS])
        gram = sb("gram", [XROWS, XROWS])
        W0P = sb("w0_stacked", [SROWS, QUAD, CH], f16)
        X = sb("windows", [XROWS, COLS])
        Q = sb("window_products", [XROWS, COLS])
        XN = sb("windows_scaled", [XROWS, COLS])
        RX = sb("window_scales", [128, 4 * XROWS])
        XHL = sb("windows_high_low", [XROWS, 2, COLS], f16)
        raw = [sb(f"raw_{n}", list(hi.shape)) for n, (_, hi, _) in enumerate(splits)]
        S = sb("windows_stacked", [SROWS, HALF, COLS], f16)
        H = [sb(f"act{l}", [128, 2, LAYER_COLS[l] + 2], f16) for l in range(5)]
        H.append(H5)
        zeros = sb("zeros", [128, 2, 1], f16)
        A = [sb(f"gelu{k}", [128, COLS]) for k in range(4)]
        T = [sb(f"scaled{k}", [128, 8, CH]) for k in range(2)]
        stats = sb("stats", [128, 4, BN])
        rs = {k: [sb(f"rsqrt_{k}_{n}", [128, w]) for n in range(4)] for k, w in (("g", 8), ("x", 32))}

        Y = [ps(f"Y{k}", [128, 8, CH]) for k in range(2)]
        E = [ps(f"E{k}", [128, COLS]) for k in range(3)]
        GB = ps("gram_bank", [128, COLS])

        consts_in = sem("consts_in")
        weights_ready = sem("weights_ready")
        w0_centred = sem("w0_centred")
        w0_turned = sem("w0_turned")
        w0_expanded = sem("w0_expanded")
        gram_raw = sem("gram_raw")
        gram_ready = sem("gram_ready")
        w0_stacked = sem("w0_stacked")
        w0p_zero = sem("w0p_zero")
        act_zero = sem("act_zero")
        setup = sem("setup_link")
        x_in = sem("x_in")
        later_in = sem("later_in")
        raw_in = sem("raw_in")
        split_high = sem("split_high")
        split_low = sem("split_low")
        z_ready = sem("z_ready")
        q_ready = sem("q_ready")
        v_ready = sem("v_ready")
        rx_ready = sem("rx_ready")
        r_ready = sem("r_ready")
        xn_done = sem("xn_done")
        xhl_done = sem("xhl_done")
        s_in = [sem(f"s_in{j}") for j in range(HALF)]
        xhigh = sem("xhigh_done")
        gram_link = sem("gram_link")
        link = {g: sem(f"norm_link{g}") for g in range(4)}
        y_ready = {g: sem(f"y_ready{g}") for g in range(4)}
        scaled = {g: sem(f"scaled{g}") for g in range(4)}
        e_ready = [sem(f"e_ready{u}") for u in range(16)]
        gelu_done = [sem(f"gelu_done{u}") for u in range(16)]
        high_done = [sem(f"high_done{u}") for u in range(16)]
        low_done = [sem(f"low_done{u}") for u in range(16)]
        halo = [sem(f"halo{l}") for l in range(5)]

        block = ctx.enter_context(nc.Block())
        LOOP = (3, STEPS)

        def run_steps(eng, step):
            for s in range(0, LOOP[0]):
                step(s)
            with eng.Fori(LOOP[0], LOOP[1], 1) as s:
                step(s)
            for s in range(LOOP[1], STEPS + 4):
                step(s)

        def unit_target(u):
            kind, k = UNITS[u]
            if kind == "L0":
                return [(0, 1 + COLS * k, 0, COLS)]
            if kind == G0:
                return [(1, 1 + COLS * k, 0, COLS)]
            if kind == G1:
                return [(1, 1 + 1024 + COLS * k, 0, COLS)]
            if kind == G2:
                return [(2, 1 + COLS * k, 0, COLS)]
            if k == 0:
                return [(3, 1, 0, COLS)]
            return [(4, 1, 0, 256), (5, None, 256, 128)]

        def act_cols(layer, part, col, n, s):
            if layer < 5:
                return H[layer][:, part, col:col + n]
            if isinstance(s, int):
                return H[5][:, part, (s - 2) * 128:(s - 2) * 128 + 128]
            return H[5][:, part, bass.ds((s - 2) * 128, 128)]

        @block.sync
        def _(sp):
            sp.dma_start(w0[:], w0t).then_inc(consts_in, 16)
            sp.dma_start(ident[:], ident_d).then_inc(consts_in, 16)
            sp.dma_start(mask[:], mask_d).then_inc(consts_in, 16)
            sp.dma_start(chunk_sum[:], chunk_d).then_inc(consts_in, 16)
            sp.dma_start(gains[:], gb).then_inc(consts_in, 16)
            sp.dma_start(W[:], wconv).then_inc(consts_in, 16)

            def load_windows(g, first=None):
                for j in range(HALF):
                    for k5 in range(2):
                        p = j * 40 + k5 * 20
                        if first is None:
                            start = (g + 1) * STEP0 + j * 2048 + k5
                            src = x5[:, start:start + 2048]
                        else:
                            src = x5[:, bass.ds(first[2 * j + k5], 2048)]
                        sp.dma_start(X[p:p + 20, :], src.rearrange("k (q n) -> k q n", q=QUAD)).then_inc(x_in, 16)

            def stack_windows(j):
                for part, row in ((0, 0), (1, 40), (0, 80)):
                    sp.dma_start(S[row:row + 40, j, :], XHL[j * 40:j * 40 + 40, part, :]).then_inc(s_in[j], 16)

            load_windows(-1)
            for w, (srcs, _, _) in zip(raw, splits):
                for row, src in srcs:
                    sp.dma_start(w[row:row + src.shape[0]], src).then_inc(raw_in, 16)
            for dst, src in loads:
                sp.dma_start(dst, src).then_inc(later_in, 16)
            sp.wait_ge(w0_centred, 1)
            sp.wait_ge(w0p_zero, 1)
            for g, part in enumerate((0, 0, 1)):
                for q in range(QUAD):
                    r = g * 40 + q
                    sp.dma_start(W0P[r:r + 37:4, q, :], w0hl[:, part, :]).then_inc(w0_stacked, 16)
            sp.wait_ge(xhl_done, 1)
            stack_windows(0)
            sp.wait_ge(xn_done, 1)
            load_windows(0)

            def step(n):
                sym = not isinstance(n, int)
                if sym or 0 <= n <= STEPS:
                    if sym or n >= 1:
                        sp.wait_ge(e_ready[UNIT["L0", 7]], n)
                    stack_windows(1)
                if not active("L0", n):
                    return
                first = None
                if sym:
                    first = [sp.snap((n + 2) * STEP0 + j * 2048 + k5) for j in range(HALF) for k5 in range(2)]
                sp.wait_ge(xn_done, n + 2)
                load_windows(n + 1, first)
                sp.wait_ge(e_ready[UNIT["L0", 3]], n + 1)
                sp.wait_ge(xhl_done, n + 2)
                stack_windows(0)
            run_steps(sp, step)
            sp.wait_ge(x_in, 64 * (STEPS + 2))
            for j in range(HALF):
                sp.wait_ge(s_in[j], 48 * (STEPS + 1))
            sp.wait_ge(later_in, 16 * len(loads))
            if dump is not None:
                sp.wait_ge(low_done[UNIT[G3, 1]], unit_count(UNIT[G3, 1], STEPS + 3))
                sp.dma_start(dump, H[5][:]).then_inc(x_in, 16)
                sp.wait_ge(x_in, 64 * (STEPS + 2) + 16)

        @block.tensor
        def _(pe):
            pe.wait_ge(consts_in, 96)
            pe.wait_ge(w0_centred, 1)
            nc.tensor.transpose(GB[:, 0:TAPS[0]], w0[:], ident[0:TAPS[0], 0:TAPS[0]]).then_inc(w0_turned, 1)
            pe.wait_ge(w0_expanded, 1)
            nc.tensor.matmul(GB[0:XROWS, 0:XROWS], w0x[:], w0x[:], start=True, stop=True).then_inc(gram_raw, 1)
            pe.wait_ge(gram_ready, 1)

            def gram_z(g):
                pe.wait_ge(x_in, 64 * (g + 2))
                if not (isinstance(g, int) and g < 0):
                    pe.wait_ge(xn_done, g + 1)
                nc.tensor.matmul(GB[0:XROWS, :], gram[:], X[:], start=True, stop=True).then_inc(z_ready, 1)

            def gram_v(g):
                pe.wait_ge(q_ready, g + 2)
                for n in range(4):
                    last = nc.tensor.matmul(GB[:, n * 8:n * 8 + 8], Q[:, n * 128:n * 128 + 128], chunk_sum[:],
                                            start=True, stop=True)
                last.then_inc(v_ready, 1)

            def gram_r(g):
                pe.wait_ge(rx_ready, g + 2)
                for n in range(4):
                    last = nc.tensor.matmul(GB[0:XROWS, n * 128:n * 128 + 128], RX[:, n * XROWS:(n + 1) * XROWS],
                                            ident[:], start=True, stop=True)
                last.then_inc(r_ready, 1)

            gram_z(-1)
            gram_v(-1)
            gram_r(-1)
            pe.wait_ge(weights_ready, 1)
            pe.wait_ge(w0_stacked, 16 * 12)
            pe.wait_ge(act_zero, 2)

            def conv(g, s, first=0, count=8):
                sym = not isinstance(s, int)
                if first == 0:
                    before, at = {G0: (G3, s - 1), G1: (G2, s - 1), G3: (G0, s), G2: (G1, s)}[g]
                    if sym or first_step(before) <= at:
                        if not sym:
                            at = min(at, last_step(before))
                        pe.wait_ge(scaled[before], 2 * (at - FIRST[before] + 1))
                if g == G0 and first == 0:
                    pe.wait_ge(halo[0], s)
                for n, (layer, t) in list(enumerate(TILES[g]))[first:first + count]:
                    at = s if g == G2 else s - 1
                    v = {1: UNIT["L0", t // 2], 2: UNIT[(G0, G1)[t // 4 % 2], t // 2 % 2],
                         3: UNIT[G2, t // 2 % 2], 4: UNIT[G3, 0], 5: UNIT[G3, 1]}[layer]
                    if t % 2 == 0 and (sym or active(UNITS[v][0], at)):
                        pe.wait_ge(low_done[v], unit_count(v, at))
                    taps = TAPS[layer]
                    w = 3 * (layer - 1)
                    src = H[layer - 1]
                    k = 0
                    for tap in range(taps):
                        c = 256 * t + tap
                        for part, wt in ((0, WH), (0, WL), (1, WH)):
                            last = nc.tensor.matmul(Y[YPAIR[g]][:, n, :], src[:, part, c:c + 255:2], wt[:, w + tap, :],
                                                    start=(k == 0), stop=(k == 3 * taps - 1))
                            k += 1
                if first + count >= len(TILES[g]):
                    last.then_inc(y_ready[g], 1)

            def wait_bank(u, n):
                prev = previous_user(BANK, u, n)
                if prev:
                    pe.wait_ge(gelu_done[prev[0]], unit_count(prev[0], prev[1]))

            def turn(g, b, n):
                u = UNIT[g, b]
                s = n - BEHIND[u]
                if not active(g, s):
                    return
                pe.wait_ge(scaled[g], 2 * (s - FIRST[g]) + b + 1)
                wait_bank(u, n)
                for t in range(4):
                    if 4 * b + t < len(TILES[g]):
                        last = nc.tensor.transpose(E[BANK[u]][:, t * 128:t * 128 + 128],
                                                   T[YPAIR[g]][:, 4 * b + t, :], ident[:])
                last.then_inc(e_ready[u], 1)

            def layer0(c, n):
                u = UNIT["L0", c]
                s = n - BEHIND[u]
                if not active("L0", s):
                    return
                if c % 4 == 0:
                    pe.wait_ge(s_in[c // 4], 48 * (s + 1))
                wait_bank(u, n)
                nc.tensor.matmul(E[BANK[u]][:], W0P[:, c % 4, :], S[:, c // 4, :], start=True, stop=True)\
                    .then_inc(e_ready[u], 1)

            def step(n):
                if active(G0, n):
                    conv(G0, n, 0, 4)
                layer0(6, n)
                if active(G0, n):
                    conv(G0, n, 4, 4)
                layer0(7, n)
                turn(G2, 0, n)
                turn(G2, 1, n)
                if active(G1, n):
                    conv(G1, n, 0, 4)
                layer0(0, n)
                if active(G1, n):
                    conv(G1, n, 4, 4)
                layer0(1, n)
                turn(G0, 0, n)
                layer0(2, n)
                turn(G0, 1, n)
                layer0(3, n)
                if active(G3, n):
                    conv(G3, n)
                turn(G1, 0, n)
                turn(G1, 1, n)
                if active("L0", n):
                    gram_z(n)
                layer0(4, n)
                layer0(5, n)
                turn(G3, 0, n)
                turn(G3, 1, n)
                if active("L0", n):
                    gram_v(n)
                if active(G2, n):
                    conv(G2, n, 0, 4)
                if active("L0", n):
                    gram_r(n)
                if active(G2, n):
                    conv(G2, n, 4, 4)
            run_steps(pe, step)

        def rsqrt_ops(tiles, source, n):
            x, y0, a, y1 = (t[:, 0:n] for t in tiles)
            v = nc.vector
            yield lambda: v.tensor_scalar(x, source, 0.0, EPS_SUM, ALU.max, ALU.add)
            yield lambda: v.tensor_scalar(y0.bitcast(i32), x.bitcast(i32), -0.5, MAGIC, ALU.mult, ALU.add)
            yield lambda: v.tensor_tensor(a, y0, y0, ALU.mult)
            yield lambda: v.scalar_tensor_tensor(a, a, NEWTON1[0], x, ALU.mult, ALU.mult)
            yield lambda: v.scalar_tensor_tensor(y0, a, NEWTON1[1], y0, ALU.add, ALU.mult)
            yield lambda: v.tensor_tensor(a, y0, y0, ALU.mult)
            yield lambda: v.scalar_tensor_tensor(a, a, NEWTON2[0], x, ALU.mult, ALU.mult)
            yield lambda: v.scalar_tensor_tensor(y1, a, NEWTON2[1], y0, ALU.add, ALU.mult)

        @block.vector
        def _(dve):
            done = [0]

            def chained(ins):
                done[0] += 1
                ins.then_inc(setup, 1)
                dve.wait_ge(setup, done[0])

            nc.vector.memset(W0P[:].rearrange("p q c -> p (q c)").bitcast(f32), 0.0).then_inc(w0p_zero, 1)
            dve.wait_ge(consts_in, 96)
            chained(nc.vector.reduce_sum(w0sum[:], w0[:], AX.X))
            chained(nc.vector.tensor_scalar(w0sum[:], w0sum[:], -1.0 / CH, None, ALU.mult))
            chained(nc.vector.tensor_tensor(w0[:], w0[:], w0sum[:].to_broadcast([TAPS[0], CH]), ALU.add))
            chained(nc.vector.tensor_copy(w0hl[:, 0, :], w0[:]))
            nc.vector.tensor_tensor(w0hl[:, 1, :], w0[:], w0hl[:, 0, :], ALU.subtract).then_inc(w0_centred, 1)
            dve.wait_ge(w0_turned, 1)
            nc.vector.tensor_copy(
                w0x[:].rearrange("p (j k q) -> p j k q", j=HALF, q=QUAD),
                GB[:, 0:TAPS[0]].unsqueeze(1).unsqueeze(3).to_broadcast([128, HALF, TAPS[0], QUAD]),
            ).then_inc(w0_expanded, 1)
            dve.wait_ge(gram_raw, 1)
            nc.vector.tensor_tensor(gram[:], GB[0:XROWS, 0:XROWS], mask[:], ALU.mult).then_inc(gram_ready, 1)
            chained(nc.vector.tensor_scalar(gain_s[:], gains[:, 0:8], ROOT_CH, None, ALU.mult))
            chained(nc.vector.reduce_sum(Wsum[:], W[:], AX.X))
            chained(nc.vector.tensor_scalar(Wsum[:], Wsum[:], -1.0 / CH, None, ALU.mult))
            chained(nc.vector.tensor_tensor(W[:], W[:], Wsum[:].unsqueeze(2).to_broadcast([128, 16, CH]), ALU.add))
            chained(nc.vector.tensor_copy(WH[:], W[:]))
            nc.vector.tensor_tensor(WL[:], W[:], WH[:], ALU.subtract).then_inc(weights_ready, 1)

            def gram_q(g):
                dve.wait_ge(z_ready, g + 2)
                nc.vector.tensor_tensor(Q[:], GB[0:XROWS, :], X[:], ALU.mult).then_inc(q_ready, 1)

            def gram_rsqrt(g):
                dve.wait_ge(v_ready, g + 2)
                base = GRAM_OPS * (g + 1)
                for n, op in enumerate(rsqrt_ops(rs["x"], GB[:, 0:32], 32)):
                    if n:
                        dve.wait_ge(gram_link, base + n)
                    op().then_inc(gram_link, 1)
                dve.wait_ge(gram_link, base + GRAM_OPS)
                r = rs["x"][3][:].rearrange("p (a q) -> p a q", q=QUAD).unsqueeze(2)
                nc.vector.tensor_copy(RX[:].rearrange("p (a k q) -> p a k q", k=TAPS[0], q=QUAD),
                                      r.to_broadcast([128, 4 * HALF, TAPS[0], QUAD])).then_inc(rx_ready, 1)

            def gram_scale(g):
                dve.wait_ge(r_ready, g + 2)
                if not (isinstance(g, int) and g < 0):
                    for j in range(HALF):
                        dve.wait_ge(s_in[j], 48 * (g + 1))
                nc.vector.tensor_tensor(XN[:], GB[0:XROWS, :], X[:], ALU.mult).then_inc(xn_done, 1)
                dve.wait_ge(xn_done, g + 2)
                nc.vector.tensor_copy(XHL[:, 0, :], XN[:]).then_inc(xhigh, 1)
                dve.wait_ge(xhigh, g + 2)
                nc.vector.tensor_tensor(XHL[:, 1, :], XN[:], XHL[:, 0, :], ALU.subtract).then_inc(xhl_done, 1)

            def norm(g, s):
                dve.wait_ge(y_ready[g], s - FIRST[g] + 1)
                tiles = len(TILES[g])
                y = Y[YPAIR[g]]
                base = NORM_OPS * (s - FIRST[g])
                for p in range(4):
                    if 2 * p + 1 < tiles:
                        pair = y[:, 2 * p:2 * p + 2, :].rearrange("p t c -> p c t")
                    else:
                        pair = y[:, 2 * p, :].unsqueeze(2).to_broadcast([128, CH, 2])
                    nc.vector.bn_stats(stats[:, p, :], pair).then_inc(link[g], 1)
                squares = stats[:].rearrange("p a (t x) -> p (a t) x", x=3)[:, :, 2]
                for n, op in enumerate(rsqrt_ops(rs["g"], squares, 8)):
                    dve.wait_ge(link[g], base + 4 + n)
                    op().then_inc(link[g], 1)
                dve.wait_ge(link[g], base + 12)
                r = rs["g"][3]
                for b in range(2):
                    n = min(4, tiles - 4 * b)
                    before = {G0: (G3, -1), G3: (G0, 0), G1: (G2, -1), G2: (G1, 0)}[g]
                    at = s + before[1]
                    if not isinstance(s, int) or first_step(before[0]) <= at:
                        if isinstance(at, int):
                            at = min(at, last_step(before[0]))
                        v = UNIT[before[0], b]
                        dve.wait_ge(e_ready[v], unit_count(v, at))
                    nc.vector.tensor_tensor(T[YPAIR[g]][:, 4 * b:4 * b + n, :], y[:, 4 * b:4 * b + n, :],
                                            r[:, 4 * b:4 * b + n].unsqueeze(2).to_broadcast([128, n, CH]),
                                            ALU.mult).then_inc(scaled[g], 1)

            gram_q(-1)
            gram_rsqrt(-1)
            gram_scale(-1)

            def step(n):
                if active(G2, n - 1):
                    norm(G2, n - 1)
                if active(G0, n):
                    norm(G0, n)
                if active(G1, n):
                    norm(G1, n)
                if active(G3, n):
                    norm(G3, n)
                if active("L0", n):
                    gram_q(n)
                    gram_rsqrt(n)
                    gram_scale(n)
            run_steps(dve, step)

        @block.scalar
        def _(act):
            act.wait_ge(consts_in, 96)
            act.wait_ge(raw_in, 16 * sum(len(srcs) for srcs, _, _ in splits))
            for w, (_, hi, _) in zip(raw, splits):
                nc.scalar.activation(hi[:], w[:], ACT.Copy).then_inc(split_high, 1)
            act.wait_ge(weights_ready, 1)
            act.wait_ge(act_zero, 2)

            def gelu(u, n):
                s = n - BEHIND[u]
                act.wait_ge(e_ready[u], unit_count(u, s))
                prev = previous_user(STAGE, u, n)
                if prev:
                    act.wait_ge(low_done[prev[0]], unit_count(prev[0], prev[1]))
                for layer, _, c, cols in unit_target(u):
                    ins = nc.scalar.activation(A[STAGE[u]][:, c:c + cols], E[BANK[u]][:, c:c + cols], ACT.Gelu,
                                               scale=gain_s[:, layer:layer + 1], bias=gains[:, 8 + layer:9 + layer])
                ins.then_inc(gelu_done[u], 1)

            def high(u, n):
                s = n - BEHIND[u]
                sym = not isinstance(s, int)
                act.wait_ge(gelu_done[u], unit_count(u, s))
                kind, part = UNITS[u]
                reader, at = {"L0": (G0 if part < 4 else G1, s), G0: (G2, s - 1), G1: (G2, s - 1),
                              G2: (G3, s), G3: (G3, s)}[kind]
                if sym or at >= FIRST[reader]:
                    act.wait_ge(y_ready[reader], at - FIRST[reader] + 1)
                for l, last in enumerate([("L0", 7), (G1, 1), (G2, 1), (G3, 0), (G3, 1)]):
                    if (kind, part) == last and (sym or l != 2 or s >= FIRST[G3]):
                        act.wait_ge(halo[l], s - (FIRST[G3] if l == 2 else first_step(kind)) + 1)
                for layer, col, c, cols in unit_target(u):
                    ins = nc.scalar.activation(act_cols(layer, 0, col, cols, s), A[STAGE[u]][:, c:c + cols], ACT.Copy)
                ins.then_inc(high_done[u], 1)

            def step(n):
                for u in range(16):
                    if active(UNITS[u][0], n - BEHIND[u]):
                        gelu(u, n)
                    v, at = (u - 1, n) if u else (15, n - 1)
                    if active(UNITS[v][0], at - BEHIND[v]):
                        high(v, at)
            run_steps(act, step)
            high(15, STEPS + 3)

        @block.gpsimd
        def _(pool):
            for l in range(5):
                flat = H[l][:].bitcast(f32)
                ins = nc.gpsimd.memset(flat, 0.0)
            ins.then_inc(act_zero, 1)
            nc.gpsimd.memset(zeros[:], 0.0).then_inc(act_zero, 1)
            pool.wait_ge(act_zero, 2)

            pool.wait_ge(raw_in, 16 * sum(len(srcs) for srcs, _, _ in splits))
            for n, (w, (_, hi, lo)) in enumerate(zip(raw, splits)):
                p = lo.shape[0]
                pool.wait_ge(split_high, n + 1)
                nc.gpsimd.tensor_tensor(lo[:], w[0:p], hi[0:p], ALU.subtract).then_inc(split_low, 1)

            def keep_halo(l, g, count, s):
                if count is not None:
                    pool.wait_ge(y_ready[g], count)
                u = UNIT[[("L0", 7), (G1, 1), (G2, 1), (G3, 0), (G3, 1)][l]]
                if active(UNITS[u][0], s):
                    pool.wait_ge(low_done[u], unit_count(u, s))
                n = LAYER_COLS[l]
                nc.gpsimd.tensor_tensor(H[l][:, :, 0:1], H[l][:, :, n:n + 1], zeros[:], ALU.add).then_inc(halo[l], 1)

            def low(u, s):
                pool.wait_ge(high_done[u], unit_count(u, s))
                for layer, col, c, cols in unit_target(u):
                    ins = nc.gpsimd.tensor_tensor(act_cols(layer, 1, col, cols, s), A[STAGE[u]][:, c:c + cols],
                                                  act_cols(layer, 0, col, cols, s), ALU.subtract)
                ins.then_inc(low_done[u], 1)

            def step(n):
                sym = not isinstance(n, int)
                for u, kind in enumerate(UNITS):
                    s = n - BEHIND[u]
                    if not active(kind[0], s):
                        continue
                    if kind == ("L0", 0):
                        keep_halo(0, G0, n if sym or n >= 1 else None, n - 1)
                    if kind == (G0, 0):
                        keep_halo(1, G2, n - 1 if sym or n > 1 else None, n - 1)
                    if kind == (G3, 0):
                        for l in (2, 3, 4) if sym or n <= STEPS else (3, 4):
                            keep_halo(l, G3, n - 1, n - 1)
                    low(u, s)
            run_steps(pool, step)



D = 192
TP = POS_PAD // 3
THIRDS = 3
HEADS, HD = 12, 16
EXPERTS, INTER = 8, 128
D2 = D - 128
PAIRS = BATCH * (BATCH + 1) // 2
POOL_Q = (1, 3, 4, 6, 7)


FRONT = ["conv", "conv_turn", "final_in", "final_turn", "proj", "x_turn", "kv_a", "kv_b", "v_norm", "q_scores",
         "vv_scores", "vv_sum_a", "vv_sum_b", "exp", "weights", "mix_a", "mix_b", "mix_c", "mix_d",
         "o_turn", "o_proj", "y_turn", "router", "rank_groups", "rank_experts", "weights_turn"]
BACK = [("expert", h, e) for h in (0,) for e in range(9)] + [("sum", 0, 0), ("sum", 0, 1)] \
    + [("expert", 1, e) for e in range(9)] + [("sum", 1, 0), ("sum", 1, 1)]


def merged(i):
    front = [(i, name) for name in FRONT] if i < THIRDS else []
    back = [(i - 1, *stage) for stage in BACK] if i else []
    while front or back:
        if front:
            yield ("front", *front.pop(0))
        if back:
            yield ("back", *back.pop(0))


MIX = [(0, 1), (3, 2), (4, 6), (5, 7)]
MIX_ORDER = [q for pair in MIX for q in pair]
SUM_SPLIT = 21


def tokens_part(nc, keep, wt, out):
    ident, gains, gain_s, WH, WL, H5 = keep
    ctx = ExitStack()
    with ctx:
        def sb(name, shape, dt=f32):
            return ctx.enter_context(nc.sbuf_tensor(name, shape, dt))

        def sem(name):
            return ctx.enter_context(nc.semaphore(name))

        B = [ctx.enter_context(nc.psum_tensor(f"bank{k}", [128, COLS], f32)) for k in range(8)]
        ones = sb("ones", [1, 128])
        TA = sb("token_rows", [TP, 8, 128])
        h6 = sb("h6", [128, 8 * TP])
        z = h6
        h0 = [sb(f"resid{k}", [TP, 8, D]) for k in range(2)]
        xn = sb("xn", [TP, 8, D])
        XT1 = sb("xt1", [128, 8 * TP])
        XT2 = sb("xt2", [D2, 8 * TP])
        YH = [sb(f"y_high{k}", [128, 8 * TP], f16) for k in range(2)]
        YL = [sb(f"y_low{k}", [128, 8 * TP], f16) for k in range(2)]
        YS = [sb(f"y_rest{k}", [128, 8 * TP], f16) for k in range(2)]
        KV = sb("kv", [TP, 8, 2 * D])
        q0 = sb("q0", [TP, D])
        vn = sb("vn", [TP, 8, D])
        prod = sb("prod", [TP, PAIRS, D])
        prod0 = xn
        PQ = [prod[:, 8 * k:8 * k + 8, :] for k in range(4)]
        sv = sb("sv", [TP, PAIRS, HEADS])
        s0 = sb("s0", [TP, 8, HEADS])
        m0 = sb("m0", [TP, HEADS])
        EX = sb("ex", [TP, 64, HEADS])
        Z = sb("zsum", [TP, 8, HEADS])
        RZ = sb("rz", [TP, 8, HEADS])
        O = vn
        n2 = sb("n2", [TP, 96])
        stats = sb("tstats", [TP, 4, BN])
        rt = [sb(f"t_rsqrt{n}", [TP, 96]) for n in range(4)]
        sc = sb("sc", [TP, 8, EXPERTS])
        biased = sb("biased", [TP, 8, EXPERTS])
        gs = sb("gs", [TP, 8, 4])
        gk = sb("gk", [TP, 8, 4])
        gc = sb("gc", [TP, 8, 8])
        ek = sb("ek", [TP, 8, EXPERTS])
        em = sb("em", [TP, 8, EXPERTS])
        cw = sb("cw", [TP, 8, EXPERTS])
        wsum = sb("wsum", [TP, 8])
        mark = sb("mark", [128, 2])
        cwT = [sb(f"cwt{k}", [EXPERTS, 8 * TP]) for k in range(2)]
        sl = [sb(f"silu{k}", [128, 4 * TP]) for k in range(2)]
        U = sb("hidden", [128, EXPERTS + 1, 4 * TP])

        names = ("y6 t6 e6 h6 fl_in fl_t fl_e z pj h0 x_t xt_e xt kv kv_s vn_r prod_p sv ex0in ex en pqm_p "
                 "o ot_e op yt_e yh yl gate sig cw cwt_e cwt ones f1 f3 fc silu gated hid fo res").split()
        S = {n: sem("s_" + n) for n in names}
        link = sem("token_link")
        out_left = [sem(f"out_left{i}") for i in range(THIRDS)]
        block = ctx.enter_context(nc.Block())
        NFE = EXPERTS + 1
        N4 = 4 * TP

        def tile_cols(t):
            return slice((t % 4) * TP, (t % 4 + 1) * TP)

        def run(front, back):
            for i in range(THIRDS + 1):
                for stage in merged(i):
                    if stage[0] == "front":
                        front(*stage[1:])
                    else:
                        back(*stage[1:])

        @block.tensor
        def _(pe):
            pe.wait_ge(S["ones"], 1)

            def turn(src, banks, width, rows, sem_):
                for t in range(8):
                    last = nc.tensor.transpose(B[banks[t // 4]][0:width, tile_cols(t)], src(t), ident[0:rows, 0:rows])
                    if t % 4 == 3:
                        last.then_inc(sem_, 1)

            def front(i, name):
                if name == "conv":
                    if i:
                        pe.wait_ge(S["cwt"], 2 * i)
                    for t in range(8):
                        base = 2 * (t * POS_PAD + TP * i) + 257
                        k = 0
                        for tap in range(2):
                            for part, w in ((0, WH), (0, WL), (1, WH)):
                                c = base + tap
                                last = nc.tensor.matmul(B[t // 4][0:TP, t % 4 * 128:t % 4 * 128 + 128],
                                                        H5[:, part, c:c + 2 * TP - 1:2], w[:, 14 + tap, :],
                                                        start=(k == 0), stop=(k == 5))
                                k += 1
                        if t % 4 == 3:
                            last.then_inc(S["y6"], 1)
                elif name == "conv_turn":
                    pe.wait_ge(S["t6"], 2 * i + 2)
                    turn(lambda t: TA[:, t, :], (2, 3), 128, TP, S["e6"])
                elif name == "final_in":
                    pe.wait_ge(S["h6"], 2 * i + 2)
                    for t in range(8):
                        last = nc.tensor.transpose(B[t // 4][0:TP, t % 4 * 128:t % 4 * 128 + 128],
                                                   h6[:, t * TP:(t + 1) * TP], ident[:])
                        if t % 4 == 3:
                            last.then_inc(S["fl_in"], 1)
                elif name == "final_turn":
                    pe.wait_ge(S["fl_t"], i + 1)
                    turn(lambda t: TA[:, t, :], (2, 3), 128, TP, S["fl_e"])
                elif name == "proj":
                    pe.wait_ge(S["z"], 2 * i + 2)
                    for t in range(8):
                        o = B[t // 2][0:TP, t % 2 * D:t % 2 * D + D]
                        nc.tensor.matmul(o, z[:, t * TP:(t + 1) * TP], wt["proj"][:], start=True, stop=False)
                        last = nc.tensor.matmul(o, ones[:, 0:TP], wt["proj_b"][:], start=False, stop=True)
                        if t % 2:
                            last.then_inc(S["pj"], 1)
                elif name == "x_turn":
                    pe.wait_ge(S["x_t"], 2 * i + 1)
                    turn(lambda t: xn[:, t, 0:128], (0, 1), 128, TP, S["xt_e"])
                    turn(lambda t: xn[:, t, 128:D], (2, 3), D2, TP, S["xt_e"])
                elif name in ("kv_a", "kv_b"):
                    if name == "kv_a":
                        pe.wait_ge(S["xt"], 8 * i + 4)
                    for t in range(4) if name == "kv_a" else range(4, 8):
                        b = B[t % 4]
                        if t >= 4:
                            pe.wait_ge(S["kv_s"], 9 * i + t - 3)
                        c = slice(t * TP, (t + 1) * TP)
                        nc.tensor.matmul(b[0:TP, 0:2 * D], XT1[:, c], wt["qkv1"][:, D:3 * D], start=True, stop=False)
                        nc.tensor.matmul(b[0:TP, 0:2 * D], XT2[:, c], wt["qkv2"][:, D:3 * D], start=False, stop=True)\
                            .then_inc(S["kv"], 1)
                    if name == "kv_b":
                        pe.wait_ge(S["kv_s"], 9 * i + 5)
                        c = slice(0, TP)
                        nc.tensor.matmul(B[0][0:TP, 0:D], XT1[:, c], wt["qkv1"][:, 0:D], start=True, stop=False)
                        nc.tensor.matmul(B[0][0:TP, 0:D], XT2[:, c], wt["qkv2"][:, 0:D], start=False, stop=True)\
                            .then_inc(S["kv"], 1)
                elif name == "o_turn":
                    pe.wait_ge(S["kv_s"], 9 * i + 9)
                    pe.wait_ge(S["o"], 8 * i + 8)
                    turn(lambda t: O[:, t, 0:128], (0, 1), 128, TP, S["ot_e"])
                    turn(lambda t: O[:, t, 128:D], (2, 3), D2, TP, S["ot_e"])
                elif name == "o_proj":
                    pe.wait_ge(S["xt"], 8 * i + 8)
                    for t in range(8):
                        o = B[t // 2][0:TP, t % 2 * D:t % 2 * D + D]
                        c = slice(t * TP, (t + 1) * TP)
                        nc.tensor.matmul(o, XT1[:, c], wt["op1"][:], start=True, stop=False)
                        nc.tensor.matmul(o, XT2[:, c], wt["op2"][:], start=False, stop=False)
                        last = nc.tensor.matmul(o, ones[:, 0:TP], wt["op_b"][:], start=False, stop=True)
                        if t % 2:
                            last.then_inc(S["op"], 1)
                elif name == "y_turn":
                    pe.wait_ge(S["x_t"], 2 * i + 2)
                    turn(lambda t: xn[:, t, 0:128], (0, 1), 128, TP, S["yt_e"])
                    turn(lambda t: xn[:, t, 128:D], (2, 3), D2, TP, S["yt_e"])
                elif name == "router":
                    pe.wait_ge(S["yl"], 4 * i + 4)
                    yh, yl, ys = YH[i % 2], YL[i % 2], YS[i % 2]
                    for t in range(8):
                        c = slice(t * TP, (t + 1) * TP)
                        o = B[0][0:TP, t * 8:t * 8 + 8]
                        nc.tensor.matmul(o, yh[:, c], wt["gateah"][:], start=True, stop=False)
                        nc.tensor.matmul(o, yh[:, c], wt["gateal"][:], start=False, stop=False)
                        nc.tensor.matmul(o, yl[:, c], wt["gateah"][:], start=False, stop=False)
                        nc.tensor.matmul(o, ys[:, c], wt["gatebh"][:], start=False, stop=False)
                        last = nc.tensor.matmul(o, ys[0:D2, c], wt["gatebl"][:], start=False, stop=True)
                    last.then_inc(S["gate"], 1)
                elif name == "weights_turn":
                    pe.wait_ge(S["cw"], i + 1)
                    turn(lambda t: cw[:, t, :], (1, 2), EXPERTS, TP, S["cwt_e"])

            def back(i, name, hh, e):
                if name == "expert":
                    c = slice(hh * N4, (hh + 1) * N4)
                    n = (2 * i + hh) * NFE + e
                    yh, yl, ys = YH[i % 2][:, c], YL[i % 2][:, c], YS[i % 2][:, c]
                    if n == 0 or (hh == 0 and e == 0):
                        pe.wait_ge(S["cwt"], 2 * i + 2)
                    for bank, w, done, free in ((4, "w1", "f1", "silu"), (5, "w3", "f3", "gated")):
                        if n:
                            pe.wait_ge(S[free], n)
                        o = B[bank][:, 0:N4]
                        nc.tensor.matmul(o, wt[w + "ah"][:, e, :], yh, start=True, stop=False)
                        nc.tensor.matmul(o, wt[w + "ah"][:, e, :], yl, start=False, stop=False)
                        nc.tensor.matmul(o, wt[w + "al"][:, e, :], yh, start=False, stop=False)
                        nc.tensor.matmul(o, wt[w + "bh"][:, e, :], ys, start=False, stop=False)
                        nc.tensor.matmul(o, wt[w + "bl"][:, e, :], YS[i % 2][0:D2, c], start=False, stop=True)\
                            .then_inc(S[done], 1)
                    if e < EXPERTS:
                        if n:
                            pe.wait_ge(S["hid"], n)
                        nc.tensor.matmul(B[6][:, 0:N4], wt["pick"][:, e, :], cwT[i % 2][:, c], start=True, stop=True)\
                            .then_inc(S["fc"], 1)
                else:
                    if e == 0:
                        pe.wait_ge(S["hid"], (2 * i + hh + 1) * NFE)
                    for t in (2 * e, 2 * e + 1):
                        m = (2 * i + hh) * 4 + t
                        if m:
                            pe.wait_ge(S["res"], m)
                        for x in range(NFE):
                            last = nc.tensor.matmul(B[7][0:TP, 0:D], U[:, x, t * TP:(t + 1) * TP], wt["w2"][:, x, :],
                                                    start=(x == 0), stop=(x == NFE - 1))
                        last.then_inc(S["fo"], 1)

            run(front, back)

        @block.scalar
        def _(act):
            A = nc.scalar.activation

            def copies(dst, banks, rows, sem_in, base, sem_out):
                for b in range(2):
                    act.wait_ge(sem_in, base + b + 1)
                    A(dst[0:rows, b * N4:(b + 1) * N4], B[banks[b]][0:rows, 0:N4], ACT.Copy).then_inc(sem_out, 1)

            def front(i, name):
                if name == "conv_turn":
                    for b in range(2):
                        act.wait_ge(S["e6"], 2 * i + b + 1)
                        A(h6[:, b * N4:(b + 1) * N4], B[2 + b][:, 0:N4], ACT.Gelu,
                          scale=gain_s[:, 6:7], bias=gains[:, 14:15]).then_inc(S["h6"], 1)
                elif name == "final_turn":
                    for b in range(2):
                        act.wait_ge(S["fl_e"], 2 * i + b + 1)
                        A(z[:, b * N4:(b + 1) * N4], B[2 + b][:, 0:N4], ACT.Identity,
                          scale=gain_s[:, 7:8], bias=gains[:, 15:16]).then_inc(S["z"], 1)
                elif name == "proj":
                    if i > 1:
                        act.wait_ge(out_left[i - 2], 16 * 8)
                    for b in range(4):
                        act.wait_ge(S["pj"], 4 * i + b + 1)
                        A(h0[i % 2][:, 2 * b:2 * b + 2, :], B[b][0:TP, 0:2 * D].rearrange("p (t d) -> p t d", t=2),
                          ACT.Copy).then_inc(S["h0"], 1)
                elif name == "x_turn":
                    copies(XT1, (0, 1), 128, S["xt_e"], 4 * i, S["xt"])
                    copies(XT2, (2, 3), D2, S["xt_e"], 4 * i + 2, S["xt"])
                elif name in ("kv_a", "kv_b"):
                    for t in range(4) if name == "kv_a" else range(4, 8):
                        act.wait_ge(S["kv"], 9 * i + t + 1)
                        A(KV[:, t, :], B[t % 4][0:TP, 0:2 * D], ACT.Copy).then_inc(S["kv_s"], 1)
                    if name == "kv_b":
                        act.wait_ge(S["kv"], 9 * i + 9)
                        A(q0[:], B[0][0:TP, 0:D], ACT.Copy).then_inc(S["kv_s"], 1)
                elif name == "exp":
                    act.wait_ge(S["sv"], 2 * i + 2)
                    off = 0
                    for d in range(8):
                        if d < 7:
                            A(EX[:, 9 + d:9 + d + 9 * (6 - d) + 1:9, :], sv[:, off + 1:off + 8 - d, :], ACT.Exp, scale=0.25)
                        if d:
                            A(EX[:, 8 * d:8 * d + 9 * (7 - d) + 1:9, :], sv[:, off:off + 8 - d, :], ACT.Exp, scale=0.25)
                        off += 8 - d
                    act.wait_ge(S["ex0in"], i + 1)
                    A(EX[:, 0:8, :], s0[:], ACT.Exp, scale=0.25).then_inc(S["ex"], 1)
                elif name == "o_turn":
                    copies(XT1, (0, 1), 128, S["ot_e"], 4 * i, S["xt"])
                    copies(XT2, (2, 3), D2, S["ot_e"], 4 * i + 2, S["xt"])
                elif name == "y_turn":
                    copies(YH[i % 2], (0, 1), 128, S["yt_e"], 4 * i, S["yh"])
                    copies(YS[i % 2], (2, 3), D2, S["yt_e"], 4 * i + 2, S["yh"])
                elif name == "router":
                    act.wait_ge(S["gate"], i + 1)
                    A(sc[:], B[0][0:TP, 0:64].rearrange("p (t e) -> p t e", t=8), ACT.Sigmoid).then_inc(S["sig"], 1)
                elif name == "weights_turn":
                    copies(cwT[i % 2], (1, 2), EXPERTS, S["cwt_e"], 2 * i, S["cwt"])

            def back(i, name, hh, e):
                if name == "expert":
                    n = (2 * i + hh) * NFE + e
                    act.wait_ge(S["f1"], n + 1)
                    if n > 1:
                        act.wait_ge(S["gated"], n - 1)
                    A(sl[n % 2][:], B[4][:, 0:N4], ACT.Silu).then_inc(S["silu"], 1)

            run(front, back)

        @block.vector
        def _(dve):
            v = nc.vector
            count = [0]

            def chained(ins):
                count[0] += 1
                ins.then_inc(link, 1)
                dve.wait_ge(link, count[0])

            def rsqrt(source, n, low, eps, factor=1.0):
                x, y0, a, y1 = (t[:, 0:n] for t in rt)
                chained(v.tensor_scalar(x, source, low, eps, ALU.max, ALU.add))
                chained(v.tensor_scalar(y0.bitcast(i32), x.bitcast(i32), -0.5, MAGIC, ALU.mult, ALU.add))
                chained(v.tensor_tensor(a, y0, y0, ALU.mult))
                chained(v.scalar_tensor_tensor(a, a, NEWTON1[0], x, ALU.mult, ALU.mult))
                chained(v.scalar_tensor_tensor(y0, a, NEWTON1[1], y0, ALU.add, ALU.mult))
                chained(v.tensor_tensor(a, y0, y0, ALU.mult))
                chained(v.scalar_tensor_tensor(a, a, NEWTON2[0] * factor, x, ALU.mult, ALU.mult))
                chained(v.scalar_tensor_tensor(y1, a, NEWTON2[1] * factor, y0, ALU.add, ALU.mult))
                return y1

            halves = stats[:].rearrange("p a (t x) -> p (a t) x", x=3)
            squares = halves[:, :, 2]

            def token_norm(src, n, dst, done):
                for p in range(4):
                    chained(v.bn_stats(stats[:, p, :], src[:, 2 * p:2 * p + 2, :].rearrange("p t c -> p c t")))
                r = rsqrt(squares, 8, 0.0, n * 1e-5, math.sqrt(n))
                for t in range(8):
                    last = v.tensor_scalar(dst[:, t, :], src[:, t, :], halves[:, t, 1:2], r[:, t:t + 1],
                                           ALU.subtract, ALU.mult)
                last.then_inc(done, 1)

            def bank_stats(sem_in, base):
                for b in range(2):
                    dve.wait_ge(sem_in, base + b + 1)
                    for p in range(2):
                        chained(v.bn_stats(stats[:, 2 * b + p, :],
                                           B[b][0:TP, p * 256:p * 256 + 256].rearrange("p (t c) -> p c t", t=2)))
                return rsqrt(squares, 8, 0.0, EPS_SUM)

            def rank(x, k, n):
                chained(v.memset(k[:], 0.0))
                for d in range(1, n):
                    c = gc[:, :, 0:n - d]
                    chained(v.tensor_tensor(c, x[:, :, 0:n - d], x[:, :, d:n], ALU.is_ge))
                    chained(v.tensor_tensor(k[:, :, d:n], k[:, :, d:n], c, ALU.add))
                    chained(v.scalar_tensor_tensor(k[:, :, 0:n - d], k[:, :, 0:n - d], 1.0, c, ALU.add, ALU.subtract))

            V = KV[:, :, D:2 * D]
            Vh = V.rearrange("p b (h d) -> p b h d", h=HEADS)
            EQ = EX[:].rearrange("p (q k) h -> p q k h", q=8)

            def front(i, name):
                if name == "conv":
                    r = bank_stats(S["y6"], 2 * i)
                    for b in range(2):
                        v.tensor_tensor(TA[:, 4 * b:4 * b + 4, :], B[b][0:TP, :].rearrange("p (t c) -> p t c", t=4),
                                        r[:, 4 * b:4 * b + 4].unsqueeze(2).to_broadcast([TP, 4, 128]), ALU.mult)\
                            .then_inc(S["t6"], 1)
                elif name == "final_in":
                    r = bank_stats(S["fl_in"], 2 * i)
                    for t in range(8):
                        last = v.tensor_scalar(TA[:, t, :], B[t // 4][0:TP, t % 4 * 128:t % 4 * 128 + 128],
                                               halves[:, t, 1:2], r[:, t:t + 1], ALU.subtract, ALU.mult)
                    last.then_inc(S["fl_t"], 1)
                elif name == "proj":
                    dve.wait_ge(S["h0"], 4 * i + 4)
                    token_norm(h0[i % 2], D, xn, S["x_t"])
                elif name == "v_norm":
                    dve.wait_ge(S["kv_s"], 9 * i + 9)
                    chained(v.tensor_tensor(prod0[:], V, V, ALU.mult))
                    chained(v.reduce_sum(n2[:], prod0[:].rearrange("p b (h d) -> p (b h) d", h=HEADS), AX.X))
                    r = rsqrt(n2[:], 96, 1e-12, 0.0)
                    rb = r.rearrange("p (b h) -> p b h", b=8).unsqueeze(3).to_broadcast([TP, 8, HEADS, HD])
                    v.tensor_tensor(vn[:].rearrange("p b (h d) -> p b h d", h=HEADS), Vh, rb, ALU.mult)\
                        .then_inc(S["vn_r"], 1)
                elif name == "q_scores":
                    chained(v.tensor_tensor(prod0[:], KV[:, :, 0:D], q0[:].unsqueeze(1).to_broadcast([TP, 8, D]), ALU.mult))
                    chained(v.reduce_sum(s0[:], prod0[:].rearrange("p b (h d) -> p b h d", h=HEADS), AX.X))
                    chained(v.reduce_max(m0[:], s0[:].rearrange("p k h -> p h k"), AX.X))
                    v.tensor_tensor(s0[:], s0[:], m0[:].unsqueeze(1).to_broadcast([TP, 8, HEADS]), ALU.subtract)\
                        .then_inc(S["ex0in"], 1)
                elif name == "vv_scores":
                    dve.wait_ge(S["vn_r"], i + 1)
                    off = 0
                    for d in range(3):
                        last = v.tensor_tensor(prod[:, off:off + 8 - d, :], vn[:, 0:8 - d, :], vn[:, d:8, :], ALU.mult)
                        off += 8 - d
                    chained(last)
                elif name in ("vv_sum_a", "vv_sum_b"):
                    a, b = (0, SUM_SPLIT) if name == "vv_sum_a" else (SUM_SPLIT, PAIRS)
                    if name == "vv_sum_b":
                        dve.wait_ge(S["prod_p"], i + 1)
                    v.reduce_sum(sv[:, a:b, :], prod[:, a:b, :].rearrange("p a (h d) -> p a h d", h=HEADS), AX.X)\
                        .then_inc(S["sv"], 1)
                elif name == "weights":
                    dve.wait_ge(S["ex"], i + 1)
                    chained(v.reduce_sum(Z[:], EQ.rearrange("p q k h -> p q h k"), AX.X))
                    chained(v.reciprocal(RZ[:], Z[:]))
                    v.tensor_tensor(EQ, EQ, RZ[:].unsqueeze(2).to_broadcast([TP, 8, 8, HEADS]), ALU.mult)\
                        .then_inc(S["en"], 1)
                elif name.startswith("mix"):
                    k = "abcd".index(name[-1])
                    if k == 0:
                        dve.wait_ge(S["en"], i + 1)
                    for q in MIX[k]:
                        if q in POOL_Q:
                            m = len(POOL_Q) * i + POOL_Q.index(q)
                            dve.wait_ge(S["pqm_p"], m + 1)
                            src = PQ[2 + m % 2]
                        else:
                            src = PQ[MIX_ORDER.index(q) % 2]
                            w = EQ[:, q, :, :].unsqueeze(3).to_broadcast([TP, 8, HEADS, HD])
                            chained(v.tensor_tensor(src.rearrange("p b (h d) -> p b h d", h=HEADS), Vh, w, ALU.mult))
                        v.reduce_sum(O[:, q, :], src.rearrange("p k x -> p x k"), AX.X).then_inc(S["o"], 1)
                elif name == "o_proj":
                    for b in range(4):
                        dve.wait_ge(S["op"], 4 * i + b + 1)
                        r2 = h0[i % 2][:, 2 * b:2 * b + 2, :]
                        chained(v.tensor_tensor(r2, B[b][0:TP, 0:2 * D].rearrange("p (t d) -> p t d", t=2), r2, ALU.add))
                    token_norm(h0[i % 2], D, xn, S["x_t"])
                elif name == "y_turn":
                    for n, (bank, dst, hi, rows) in enumerate(((0, YL, YH, 0), (1, YL, YH, 0), (2, YS, YS, D2), (3, YS, YS, D2))):
                        b = n % 2
                        c = slice(b * N4, (b + 1) * N4)
                        dve.wait_ge(S["yh"], 4 * i + n + 1)
                        p = D2 if rows else 128
                        v.tensor_tensor(dst[i % 2][rows:rows + p, c], B[bank][0:p, 0:N4], hi[i % 2][0:p, c], ALU.subtract)\
                            .then_inc(S["yl"], 1)
                elif name == "rank_groups":
                    dve.wait_ge(S["sig"], i + 1)
                    chained(v.tensor_tensor(biased[:], sc[:], wt["gate_b"][:].unsqueeze(1).to_broadcast([TP, 8, EXPERTS]), ALU.add))
                    two = biased[:].rearrange("p t (g k) -> p t g k", k=2)
                    chained(v.tensor_tensor(gs[:], two[:, :, :, 0], two[:, :, :, 1], ALU.add))
                    rank(gs, gk, 4)
                    chained(v.tensor_scalar(gk[:], gk[:], 1.5, None, ALU.is_lt))
                    chained(v.tensor_scalar(gs[:], gk[:], -1.0, 1e30, ALU.add, ALU.mult))
                    e4 = em[:].rearrange("p t (g k) -> p t g k", k=2)
                    chained(v.tensor_tensor(e4, two, gk[:].unsqueeze(3).to_broadcast([TP, 8, 4, 2]), ALU.mult))
                    chained(v.tensor_tensor(e4, e4, gs[:].unsqueeze(3).to_broadcast([TP, 8, 4, 2]), ALU.add))
                elif name == "rank_experts":
                    rank(em, ek, 8)
                    chained(v.tensor_scalar(ek[:], ek[:], 1.5, None, ALU.is_lt))
                    chained(v.tensor_tensor(cw[:], ek[:], sc[:], ALU.mult))
                    chained(v.reduce_sum(wsum[:], cw[:], AX.X))
                    chained(v.tensor_scalar(wsum[:], wsum[:], 1e-6, None, ALU.add))
                    chained(v.reciprocal(wsum[:], wsum[:]))
                    v.tensor_tensor(cw[:], cw[:], wsum[:].unsqueeze(2).to_broadcast([TP, 8, EXPERTS]), ALU.mult)\
                        .then_inc(S["cw"], 1)

            def back(i, name, hh, e):
                if name == "expert":
                    n = (2 * i + hh) * NFE + e
                    dve.wait_ge(S["silu"], n + 1)
                    dve.wait_ge(S["f3"], n + 1)
                    if e == 0 and n:
                        dve.wait_ge(S["fo"], (2 * i + hh) * 4)
                    g = U[:, e, :]
                    last = v.tensor_tensor(g, sl[n % 2][:], B[5][:, 0:N4], ALU.mult).then_inc(S["gated"], 1)
                    dve.wait_ge(S["gated"], n + 1)
                    if e < EXPERTS:
                        dve.wait_ge(S["fc"], (2 * i + hh) * EXPERTS + e + 1)
                        v.tensor_tensor(g, g, B[6][:, 0:N4], ALU.mult).then_inc(S["hid"], 1)
                    else:
                        v.tensor_copy(mark[:, 0:1], mark[:, 1:2]).then_inc(S["hid"], 1)
                else:
                    for t in (2 * e, 2 * e + 1):
                        m = (2 * i + hh) * 4 + t
                        dve.wait_ge(S["fo"], m + 1)
                        tt = hh * 4 + t
                        v.tensor_tensor(h0[i % 2][:, tt, :], B[7][0:TP, 0:D], h0[i % 2][:, tt, :], ALU.add)\
                            .then_inc(S["res"], 1)

            v.memset(mark[:], 0.0)
            v.memset(ones[:], 1.0).then_inc(S["ones"], 1)
            dve.wait_ge(S["ones"], 1)
            run(front, back)

        @block.gpsimd
        def _(pool):
            for i in range(THIRDS):
                pool.wait_ge(S["vn_r"], i + 1)
                off = 21
                for d in range(3, 8):
                    last = nc.gpsimd.tensor_tensor(prod[:, off:off + 8 - d, :], vn[:, 0:8 - d, :], vn[:, d:8, :], ALU.mult)
                    off += 8 - d
                last.then_inc(S["prod_p"], 1)
                pool.wait_ge(S["en"], i + 1)
                EQ = EX[:].rearrange("p (q k) h -> p q k h", q=8)
                Vh = KV[:, :, D:2 * D].rearrange("p b (h d) -> p b h d", h=HEADS)
                for n, q in enumerate(POOL_Q):
                    m = len(POOL_Q) * i + n
                    if n >= 2:
                        pool.wait_ge(S["o"], 8 * i + MIX_ORDER.index(POOL_Q[n - 2]) + 1)
                    w = EQ[:, q, :, :].unsqueeze(3).to_broadcast([TP, 8, HEADS, HD])
                    nc.gpsimd.tensor_tensor(PQ[2 + m % 2].rearrange("p b (h d) -> p b h d", h=HEADS), Vh, w, ALU.mult)\
                        .then_inc(S["pqm_p"], 1)

        @block.sync
        def _(sp):
            for i in range(THIRDS):
                rows = TP if i < THIRDS - 1 else POS - TP * (THIRDS - 1)
                for t in range(8):
                    sp.wait_ge(S["res"], 8 * i + t + 1)
                    sp.dma_start(out[t, i * TP:i * TP + rows, :], h0[i % 2][0:rows, t, :]).then_inc(out_left[i], 16)
            for left in out_left:
                sp.wait_ge(left, 16 * 8)


WEIGHTS = {
    "proj": [128, D], "proj_b": [1, D], "qkv1": [128, 3 * D], "qkv2": [D2, 3 * D],
    "op1": [128, D], "op2": [D2, D], "op_b": [1, D], "gate_b": [TP, EXPERTS], "w2": [INTER, 9, D],
    "pick": [EXPERTS, EXPERTS, 128],
}
SPLIT = {"gate": [EXPERTS], "w1": [9, INTER], "w3": [9, INTER]}


def audio_tower(nc, d, out):
    ctx = ExitStack()
    with ctx:
        def sb(name, shape, dt=f32):
            return ctx.enter_context(nc.sbuf_tensor(name, shape, dt))
        ident = sb("ident", [128, 128])
        gains = sb("gains", [128, 16])
        gain_s = sb("gain_scaled", [128, 8])
        WH = sb("conv_w_high", [128, 16, CH], f16)
        WL = sb("conv_w_low", [128, 16, CH], f16)
        H5 = sb("act5", [128, 2, (STEPS + 2) * 128], f16)
        wt = {n: sb("w_" + n, shape) for n, shape in WEIGHTS.items()}
        src = {
            "proj": d["proj"], "proj_b": d["proj_b"], "qkv1": d["wqkv"][0:128, :], "qkv2": d["wqkv"][128:D, :],
            "op1": d["wo"][0:128, :], "op2": d["wo"][128:D, :], "op_b": d["wo_b"],
            "gate_b": d["gate_b"], "w2": d["w2"], "pick": d["pick"],
        }
        loads = [(wt[n][:], src[n]) for n in WEIGHTS]
        splits = []
        for n, shape in SPLIT.items():
            for part, rows in (("a", 128), ("b", D2)):
                hi = sb(f"w_{n}{part}_high", [128, *shape], f16)
                lo = sb(f"w_{n}{part}_low", [rows, *shape], f16)
                wt[f"{n}{part}h"], wt[f"{n}{part}l"] = hi, lo
                top, rest = d[n][0:128], d[n][128:D]
                splits.append(([(0, top)] if part == "a" else [(0, rest), (D2, rest)], hi, lo))
        keep = (ident, gains, gain_s, WH, WL, H5)
        conv_tower(nc, d["x5"], d["w0t"], d["wconv"], d["gb"], (d["ident"], d["mask"], d["chunk_sum"]), (*keep, loads, splits))
        tokens_part(nc, keep, wt, out)


def layout(inputs):
    f = lambda name: np.asarray(inputs[name])
    x = np.zeros(5 * X_LEN, np.float32)
    flat = f("x").reshape(-1)
    x[5:5 + flat.size] = flat
    x5 = np.ascontiguousarray(x.reshape(X_LEN, 5).T)
    t = "L0_tok_"
    w0t = np.ascontiguousarray(f(t + "conv_w0")[:, 0, :].T)
    wconv = np.concatenate([f(f"{t}conv_w{l}").transpose(1, 2, 0) for l in range(1, 7)], axis=1)
    gb = np.stack([f(f"{t}ln_g{l}") for l in range(7)] + [f(t + "fln_g")] + [f(f"{t}ln_b{l}") for l in range(7)]
                  + [f(t + "fln_b")], axis=1)
    rows = np.arange(XROWS)
    chunk = rows // 40 * 4 + rows % 4
    n = "L0_ffn_"
    both = lambda a, b, axes: np.concatenate([f(n + a), f(n + b)[None]], axis=0).transpose(axes)
    pick = np.zeros((EXPERTS, EXPERTS, 128), np.float32)
    pick[np.arange(EXPERTS), np.arange(EXPERTS)] = 1.0
    made = {
        "x5": x5, "w0t": w0t, "wconv": wconv, "gb": gb,
        "ident": np.eye(128, dtype=np.float32),
        "mask": (chunk[:, None] == chunk[None, :]).astype(np.float32),
        "chunk_sum": (chunk[:, None] == np.arange(8)[None, :]).astype(np.float32),
        "proj": f(t + "proj_w"), "proj_b": f(t + "proj_b")[None],
        "wqkv": f("L0_attn_w_qkv").T, "wo": f("L0_attn_w_proj").T, "wo_b": f("L0_attn_b_proj")[None],
        "gate": f(n + "gate_weight").T, "gate_b": np.broadcast_to(f(n + "gate_bias")[None], (TP, EXPERTS)),
        "w1": both("w1", "sw1", (2, 0, 1)), "w3": both("w3", "sw3", (2, 0, 1)), "w2": both("w2", "sw2", (2, 0, 1)),
        "pick": pick,
    }
    return {k: np.ascontiguousarray(a) for k, a in made.items()}


def kernel(**inputs):
    import concourse.bacc as bacc
    from concourse.bass_utils import run_bass_kernel_spmd

    arrays = {f"in_{k}": a for k, a in layout(inputs).items()}
    nc = bacc.Bacc("TRN2", target_bir_lowering=False, num_devices=1)
    d = {k[3:]: nc.dram_tensor(k, a.shape, mybir.dt.from_np(a.dtype), kind="ExternalInput").ap() for k, a in arrays.items()}
    out = nc.dram_tensor("out", (BATCH, POS, D), f32, kind="ExternalOutput").ap()
    audio_tower(nc, d, out)
    r = run_bass_kernel_spmd(nc, [arrays], core_ids=[0])
    return r.results[0]["out"]
```

```python
import math
from contextlib import ExitStack

import numpy as np
import concourse.bass as bass
from concourse import mybir

f32 = mybir.dt.float32
f16 = mybir.dt.float16
i32 = mybir.dt.int32
ACT = mybir.ActivationFunctionType
ALU = mybir.AluOpType
AX = mybir.AxisListType

CH = 128
BATCH, POS = 8, 374
POS_PAD = 375
TAPS = [10, 3, 3, 3, 3, 2, 2]
STEP0 = 4096
LAYER_COLS = [STEP0 >> l for l in range(6)]
STEPS = -(-(BATCH * POS_PAD * 64 + 1) // STEP0)
BN = 6
EPS_SUM = CH * 1e-5
ROOT_CH = math.sqrt(CH)
QUAD, HALF = 4, 2
COLS = 512
XROWS = HALF * TAPS[0] * QUAD
SROWS = 3 * TAPS[0] * QUAD
X_LEN = STEP0 * (STEPS + 2) + 8

MAGIC = float(0x5F1FFFF9)
NEWTON1 = (-0.703952253, 0.703952253 * 2.38924456)
NEWTON2 = (-0.5 * (1 + 3.2e-7), 1.5 * (1 + 3.2e-7))

G0, G1, G2, G3 = range(4)
FIRST = {G0: 1, G1: 1, G2: 1, G3: 2}
LAST = {G0: STEPS, G1: STEPS, G2: STEPS, G3: STEPS + 3}
UNITS = [("L0", 6), ("L0", 7), (G2, 0), (G2, 1), ("L0", 0), ("L0", 1), (G0, 0), ("L0", 2), (G0, 1), ("L0", 3),
         (G1, 0), ("L0", 4), (G1, 1), ("L0", 5), (G3, 0), (G3, 1)]
BEHIND = [1] * 4 + [0] * 12
UNIT = {kind: u for u, kind in enumerate(UNITS)}
BANK = [0, 1, 2, 0, 1, 2, 0, 1, 2, 0, 1, 2, 0, 1, 2, 1]
STAGE = [u % 4 for u in range(16)]
VECTOR_CASTS = [[], [UNIT[G2, 1]], [], [], [UNIT[G3, 0]]]
VECTOR_HIGH = [u for place in VECTOR_CASTS for u in place]
TILES = {G0: [(1, t) for t in range(8)], G1: [(1, t) for t in range(8, 16)],
         G2: [(2, t) for t in range(8)],
         G3: [(3, t) for t in range(4)] + [(4, 0), (4, 1), (5, 0)]}
YPAIR = {G0: 0, G1: 1, G3: 0, G2: 1}
NORM_OPS = 12
GRAM_OPS = 8


def first_step(kind):
    return 0 if kind == "L0" else FIRST[kind]


def last_step(kind):
    return STEPS - 1 if kind == "L0" else LAST[kind]


def unit_count(u, s):
    return s - first_step(UNITS[u][0]) + 1


def active(kind, s):
    return not isinstance(s, int) or first_step(kind) <= s <= last_step(kind)


def previous_user(place, u, n):
    at = n
    for _ in range(4):
        order = range(u - 1, -1, -1) if at is n else range(15, -1, -1)
        for v in order:
            if place[v] == place[u] and active(UNITS[v][0], at - BEHIND[v]):
                return v, at - BEHIND[v]
        at = at - 1
        if isinstance(at, int) and at < 0:
            return None
    return None


def conv_tower(nc, x5, w0t, wconv, gb, consts, keep):
    ident_d, mask_d, chunk_d = consts
    ident, gains, gain_s, WH, WL, H5, loads, splits = keep
    ctx = ExitStack()
    with ctx:
        def sb(name, shape, dt=f32):
            return ctx.enter_context(nc.sbuf_tensor(name, shape, dt))

        def ps(name, shape):
            return ctx.enter_context(nc.psum_tensor(name, shape, f32))

        def sem(name):
            return ctx.enter_context(nc.semaphore(name))

        mask = sb("same_chunk_mask", [XROWS, XROWS])
        chunk_sum = sb("chunk_sum", [XROWS, 8])
        W = sb("conv_w", [128, 16, CH])
        Wsum = sb("conv_w_sum", [128, 16])
        w0 = sb("w0", [TAPS[0], CH])
        w0sum = sb("w0_sum", [TAPS[0], 1])
        w0hl = sb("w0_high_low", [TAPS[0], 2, CH], f16)
        w0x = sb("w0_expanded", [128, XROWS])
        gram = sb("gram", [XROWS, XROWS])
        W0P = sb("w0_stacked", [SROWS, QUAD, CH], f16)
        X = sb("windows", [XROWS, COLS])
        Q = sb("window_products", [XROWS, COLS])
        XN = sb("windows_scaled", [XROWS, COLS])
        RX = sb("window_scales", [128, 4 * XROWS])
        XHL = sb("windows_high_low", [XROWS, 2, COLS], f16)
        raw = [sb(f"raw_{n}", list(hi.shape)) for n, (_, hi, _) in enumerate(splits)]
        S = sb("windows_stacked", [SROWS, HALF, COLS], f16)
        H = [sb(f"act{l}", [128, 2, LAYER_COLS[l] + 2], f16) for l in range(5)]
        H.append(H5)
        zeros = sb("zeros", [128, 2, 1], f16)
        A = [sb(f"gelu{k}", [128, COLS]) for k in range(4)]
        T = [sb(f"scaled{k}", [128, 8, CH]) for k in range(2)]
        stats = sb("stats", [128, 4, BN])
        rs = {k: [sb(f"rsqrt_{k}_{n}", [128, w]) for n in range(4)] for k, w in (("g", 8), ("x", 32))}

        Y = [ps(f"Y{k}", [128, 8, CH]) for k in range(2)]
        E = [ps(f"E{k}", [128, COLS]) for k in range(3)]
        GB = ps("gram_bank", [128, COLS])

        consts_in = sem("consts_in")
        w_in = sem("w_in")
        weights_ready = sem("weights_ready")
        gains_ready = sem("gains_ready")
        w0_centred = sem("w0_centred")
        w0_turned = sem("w0_turned")
        w0_expanded = sem("w0_expanded")
        w0_stacked = sem("w0_stacked")
        act_zero = sem("act_zero")
        setup = sem("setup_link")
        x_in = sem("x_in")
        later_in = sem("later_in")
        raw_in = sem("raw_in")
        split_high = sem("split_high")
        z_ready = sem("z_ready")
        q_ready = sem("q_ready")
        v_ready = sem("v_ready")
        rx_ready = sem("rx_ready")
        r_ready = sem("r_ready")
        xn_done = sem("xn_done")
        xhl_done = sem("xhl_done")
        s_in = [sem(f"s_in{j}") for j in range(HALF)]
        xhigh = sem("xhigh_done")
        gram_link = sem("gram_link")
        link = {g: sem(f"norm_link{g}") for g in range(4)}
        y_ready = {g: sem(f"y_ready{g}") for g in range(4)}
        scaled = {g: sem(f"scaled{g}") for g in range(4)}
        e_ready = [sem(f"e_ready{u}") for u in range(16)]
        gelu_done = [sem(f"gelu_done{u}") for u in range(16)]
        high_done = [sem(f"high_done{u}") for u in range(16)]
        low_done = [sem(f"low_done{u}") for u in range(16)]
        halo = [sem(f"halo{l}") for l in range(5)]

        block = ctx.enter_context(nc.Block())
        LOOP = (3, STEPS)

        def run_steps(eng, step, extra=None, after=0):
            for s in range(0, LOOP[0]):
                step(s)
                if extra and s == after:
                    extra()
            with eng.Fori(LOOP[0], LOOP[1], 1) as s:
                step(s)
            for s in range(LOOP[1], STEPS + 4):
                step(s)

        def unit_target(u):
            kind, k = UNITS[u]
            if kind == "L0":
                return [(0, 1 + COLS * k, 0, COLS)]
            if kind == G0:
                return [(1, 1 + COLS * k, 0, COLS)]
            if kind == G1:
                return [(1, 1 + 1024 + COLS * k, 0, COLS)]
            if kind == G2:
                return [(2, 1 + COLS * k, 0, COLS)]
            if k == 0:
                return [(3, 1, 0, COLS)]
            return [(4, 1, 0, 256), (5, None, 256, 128)]

        def act_cols(layer, part, col, n, s):
            if layer < 5:
                return H[layer][:, part, col:col + n]
            if isinstance(s, int):
                return H[5][:, part, (s - 2) * 128:(s - 2) * 128 + 128]
            return H[5][:, part, bass.ds((s - 2) * 128, 128)]

        def high_half(eng, u, n):
            s = n - BEHIND[u]
            sym = not isinstance(s, int)
            eng.wait_ge(gelu_done[u], unit_count(u, s))
            kind, part = UNITS[u]
            reader, at = {"L0": (G0 if part < 4 else G1, s), G0: (G2, s - 1), G1: (G2, s - 1),
                          G2: (G3, s), G3: (G3, s)}[kind]
            if sym or at >= FIRST[reader]:
                eng.wait_ge(y_ready[reader], at - FIRST[reader] + 1)
            for l, last in enumerate([("L0", 7), (G1, 1), (G2, 1), (G3, 0), (G3, 1)]):
                if (kind, part) == last and (sym or l != 2 or s >= FIRST[G3]):
                    eng.wait_ge(halo[l], s - (FIRST[G3] if l == 2 else first_step(kind)) + 1)
            for layer, col, c, cols in unit_target(u):
                dst, src = act_cols(layer, 0, col, cols, s), A[STAGE[u]][:, c:c + cols]
                if u in VECTOR_HIGH:
                    ins = nc.vector.tensor_copy(dst, src)
                else:
                    ins = nc.scalar.activation(dst, src, ACT.Copy)
            ins.then_inc(high_done[u], 1)

        @block.sync
        def _(sp):
            for dst, src in ((w0, w0t), (gains, gb), (ident, ident_d), (mask, mask_d), (chunk_sum, chunk_d)):
                sp.dma_start(dst[:], src).then_inc(consts_in, 16)

            def load_windows(g, first=None):
                for j in range(HALF):
                    for k5 in range(2):
                        p = j * 40 + k5 * 20
                        if first is None:
                            start = (g + 1) * STEP0 + j * 2048 + k5
                            src = x5[:, start:start + 2048]
                        else:
                            src = x5[:, bass.ds(first[2 * j + k5], 2048)]
                        sp.dma_start(X[p:p + 20, :], src.rearrange("k (q n) -> k q n", q=QUAD)).then_inc(x_in, 16)

            def stack_windows(j):
                for part, row in ((0, 0), (1, 40), (0, 80)):
                    sp.dma_start(S[row:row + 40, j, :], XHL[j * 40:j * 40 + 40, part, :]).then_inc(s_in[j], 16)

            load_windows(-1)
            sp.wait_ge(w0_centred, 2)
            for g, part in enumerate((0, 0, 1)):
                for q in range(QUAD):
                    r = g * 40 + q
                    sp.dma_start(W0P[r:r + 37:4, q, :], w0hl[:, part, :]).then_inc(w0_stacked, 16)
            sp.dma_start(W[:], wconv).then_inc(w_in, 16)
            sp.wait_ge(xhl_done, 1)
            stack_windows(0)
            sp.wait_ge(xn_done, 1)
            load_windows(0)

            def step(n):
                sym = not isinstance(n, int)
                if sym or 0 <= n <= STEPS:
                    if sym or n >= 1:
                        sp.wait_ge(e_ready[UNIT["L0", 7]], n)
                    stack_windows(1)
                if not active("L0", n):
                    return
                first = None
                if sym:
                    first = [sp.snap((n + 2) * STEP0 + j * 2048 + k5) for j in range(HALF) for k5 in range(2)]
                sp.wait_ge(xn_done, n + 2)
                load_windows(n + 1, first)
                sp.wait_ge(e_ready[UNIT["L0", 3]], n + 1)
                sp.wait_ge(xhl_done, n + 2)
                stack_windows(0)

            def load_later():
                for w, (srcs, _, _) in zip(raw, splits):
                    for row, src in srcs:
                        sp.dma_start(w[row:row + src.shape[0]], src).then_inc(raw_in, 16)
                for dst, src in loads:
                    sp.dma_start(dst, src).then_inc(later_in, 16)
            run_steps(sp, step, load_later, 1)
            sp.wait_ge(x_in, 64 * (STEPS + 2))
            for j in range(HALF):
                sp.wait_ge(s_in[j], 48 * (STEPS + 1))
            sp.wait_ge(later_in, 16 * len(loads))

        @block.tensor
        def _(pe):
            pe.wait_ge(consts_in, 80)
            pe.wait_ge(w0_centred, 2)
            nc.tensor.transpose(GB[:, 0:TAPS[0]], w0[:], ident[0:TAPS[0], 0:TAPS[0]]).then_inc(w0_turned, 1)
            pe.wait_ge(w0_expanded, 1)
            nc.tensor.matmul(GB[0:XROWS, 0:XROWS], w0x[:], w0x[:], start=True, stop=True).then_inc(w0_turned, 1)
            pe.wait_ge(w0_expanded, 2)

            def gram_z(g):
                pe.wait_ge(x_in, 64 * (g + 2))
                if not (isinstance(g, int) and g < 0):
                    pe.wait_ge(xn_done, g + 1)
                nc.tensor.matmul(GB[0:XROWS, :], gram[:], X[:], start=True, stop=True).then_inc(z_ready, 1)

            def gram_v(g):
                pe.wait_ge(q_ready, g + 2)
                for n in range(4):
                    last = nc.tensor.matmul(GB[:, n * 8:n * 8 + 8], Q[:, n * 128:n * 128 + 128], chunk_sum[:],
                                            start=True, stop=True)
                last.then_inc(v_ready, 1)

            def gram_r(g):
                pe.wait_ge(rx_ready, g + 2)
                for n in range(4):
                    last = nc.tensor.transpose(GB[0:XROWS, n * 128:n * 128 + 128], RX[:, n * XROWS:(n + 1) * XROWS],
                                               ident[:])
                last.then_inc(r_ready, 1)

            gram_z(-1)
            gram_v(-1)
            gram_r(-1)
            pe.wait_ge(w0_stacked, 16 * 12)
            pe.wait_ge(act_zero, 2)

            def conv(g, s, first=0, count=8):
                sym = not isinstance(s, int)
                if g == G0 and not sym and s == FIRST[G0]:
                    pe.wait_ge(weights_ready, 1)
                if first == 0:
                    before, at = {G0: (G3, s - 1), G1: (G2, s - 1), G3: (G0, s), G2: (G1, s)}[g]
                    if sym or first_step(before) <= at:
                        if not sym:
                            at = min(at, last_step(before))
                        pe.wait_ge(scaled[before], 2 * (at - FIRST[before] + 1))
                if g == G0 and first == 0:
                    pe.wait_ge(halo[0], s)
                for n, (layer, t) in list(enumerate(TILES[g]))[first:first + count]:
                    at = s if g == G2 else s - 1
                    v = {1: UNIT["L0", t // 2], 2: UNIT[(G0, G1)[t // 4 % 2], t // 2 % 2],
                         3: UNIT[G2, t // 2 % 2], 4: UNIT[G3, 0], 5: UNIT[G3, 1]}[layer]
                    if t % 2 == 0 and (sym or active(UNITS[v][0], at)):
                        pe.wait_ge(low_done[v], unit_count(v, at))
                    taps = TAPS[layer]
                    w = 3 * (layer - 1)
                    src = H[layer - 1]
                    k = 0
                    for tap in range(taps):
                        c = 256 * t + tap
                        for part, wt in ((0, WH), (0, WL), (1, WH)):
                            last = nc.tensor.matmul(Y[YPAIR[g]][:, n, :], src[:, part, c:c + 255:2], wt[:, w + tap, :],
                                                    start=(k == 0), stop=(k == 3 * taps - 1))
                            k += 1
                if first + count >= len(TILES[g]):
                    last.then_inc(y_ready[g], 1)

            def wait_bank(u, n):
                prev = previous_user(BANK, u, n)
                if prev:
                    pe.wait_ge(gelu_done[prev[0]], unit_count(prev[0], prev[1]))

            def turn(g, b, n):
                u = UNIT[g, b]
                s = n - BEHIND[u]
                if not active(g, s):
                    return
                pe.wait_ge(scaled[g], 2 * (s - FIRST[g]) + b + 1)
                wait_bank(u, n)
                for t in range(4):
                    if 4 * b + t < len(TILES[g]):
                        last = nc.tensor.transpose(E[BANK[u]][:, t * 128:t * 128 + 128],
                                                   T[YPAIR[g]][:, 4 * b + t, :], ident[:])
                last.then_inc(e_ready[u], 1)

            def layer0(c, n):
                u = UNIT["L0", c]
                s = n - BEHIND[u]
                if not active("L0", s):
                    return
                if c % 4 == 0:
                    pe.wait_ge(s_in[c // 4], 48 * (s + 1))
                wait_bank(u, n)
                nc.tensor.matmul(E[BANK[u]][:], W0P[:, c % 4, :], S[:, c // 4, :], start=True, stop=True)\
                    .then_inc(e_ready[u], 1)

            def step(n):
                if active(G0, n):
                    conv(G0, n, 0, 4)
                layer0(6, n)
                if active(G0, n):
                    conv(G0, n, 4, 3)
                layer0(7, n)
                if active(G0, n):
                    conv(G0, n, 7, 1)
                turn(G2, 0, n)
                if active(G1, n):
                    conv(G1, n, 0, 1)
                turn(G2, 1, n)
                if active(G1, n):
                    conv(G1, n, 1, 2)
                layer0(0, n)
                if active(G1, n):
                    conv(G1, n, 3, 3)
                layer0(1, n)
                turn(G0, 0, n)
                if active(G1, n):
                    conv(G1, n, 6, 2)
                layer0(2, n)
                if active(G3, n):
                    conv(G3, n, 0, 4)
                turn(G0, 1, n)
                if active("L0", n):
                    gram_z(n)
                if active(G3, n):
                    conv(G3, n, 4, 1)
                layer0(3, n)
                if active(G3, n):
                    conv(G3, n, 5, 2)
                turn(G1, 0, n)
                layer0(4, n)
                turn(G1, 1, n)
                if active("L0", n):
                    gram_v(n)
                layer0(5, n)
                if active(G2, n):
                    conv(G2, n, 0, 2)
                turn(G3, 0, n)
                turn(G3, 1, n)
                if active(G2, n):
                    conv(G2, n, 2, 2)
                if active("L0", n):
                    gram_r(n)
                if active(G2, n):
                    conv(G2, n, 4, 4)
            run_steps(pe, step)

        def rsqrt_ops(tiles, source, n):
            x, y0, a, y1 = (t[:, 0:n] for t in tiles)
            v = nc.vector
            yield lambda: v.tensor_scalar(x, source, 0.0, EPS_SUM, ALU.max, ALU.add)
            yield lambda: v.tensor_scalar(y0.bitcast(i32), x.bitcast(i32), -0.5, MAGIC, ALU.mult, ALU.add)
            yield lambda: v.tensor_tensor(a, y0, y0, ALU.mult)
            yield lambda: v.scalar_tensor_tensor(a, a, NEWTON1[0], x, ALU.mult, ALU.mult)
            yield lambda: v.scalar_tensor_tensor(y0, a, NEWTON1[1], y0, ALU.add, ALU.mult)
            yield lambda: v.tensor_tensor(a, y0, y0, ALU.mult)
            yield lambda: v.scalar_tensor_tensor(a, a, NEWTON2[0], x, ALU.mult, ALU.mult)
            yield lambda: v.scalar_tensor_tensor(y1, a, NEWTON2[1], y0, ALU.add, ALU.mult)

        @block.vector
        def _(dve):
            done = [0]

            def chained(ins):
                done[0] += 1
                ins.then_inc(setup, 1)
                dve.wait_ge(setup, done[0])

            nc.vector.memset(W0P[:].rearrange("p q c -> p (q c)").bitcast(f32), 0.0).then_inc(w0_centred, 1)
            dve.wait_ge(consts_in, 80)
            nc.vector.tensor_scalar(gain_s[:], gains[:, 0:8], ROOT_CH, None, ALU.mult).then_inc(gains_ready, 1)
            chained(nc.vector.reduce_sum(w0sum[:], w0[:], AX.X))
            chained(nc.vector.tensor_scalar(w0sum[:], w0sum[:], -1.0 / CH, None, ALU.mult))
            chained(nc.vector.tensor_tensor(w0[:], w0[:], w0sum[:].to_broadcast([TAPS[0], CH]), ALU.add))
            chained(nc.vector.tensor_copy(w0hl[:, 0, :], w0[:]))
            nc.vector.tensor_tensor(w0hl[:, 1, :], w0[:], w0hl[:, 0, :], ALU.subtract).then_inc(w0_centred, 1)
            dve.wait_ge(w0_turned, 1)
            nc.vector.tensor_copy(
                w0x[:].rearrange("p (j k q) -> p j k q", j=HALF, q=QUAD),
                GB[:, 0:TAPS[0]].unsqueeze(1).unsqueeze(3).to_broadcast([128, HALF, TAPS[0], QUAD]),
            ).then_inc(w0_expanded, 1)
            dve.wait_ge(w0_turned, 2)
            nc.vector.tensor_tensor(gram[:], GB[0:XROWS, 0:XROWS], mask[:], ALU.mult).then_inc(w0_expanded, 1)
            def gram_q(g):
                dve.wait_ge(z_ready, g + 2)
                nc.vector.tensor_tensor(Q[:], GB[0:XROWS, :], X[:], ALU.mult).then_inc(q_ready, 1)

            def gram_rsqrt(g):
                dve.wait_ge(v_ready, g + 2)
                base = GRAM_OPS * (g + 1)
                for n, op in enumerate(rsqrt_ops(rs["x"], GB[:, 0:32], 32)):
                    if n:
                        dve.wait_ge(gram_link, base + n)
                    op().then_inc(gram_link, 1)
                dve.wait_ge(gram_link, base + GRAM_OPS)
                r = rs["x"][3][:].rearrange("p (a q) -> p a q", q=QUAD).unsqueeze(2)
                nc.vector.tensor_copy(RX[:].rearrange("p (a k q) -> p a k q", k=TAPS[0], q=QUAD),
                                      r.to_broadcast([128, 4 * HALF, TAPS[0], QUAD])).then_inc(rx_ready, 1)

            def gram_scale(g):
                dve.wait_ge(r_ready, g + 2)
                if not (isinstance(g, int) and g < 0):
                    for j in range(HALF):
                        dve.wait_ge(s_in[j], 48 * (g + 1))
                nc.vector.tensor_tensor(XN[:], GB[0:XROWS, :], X[:], ALU.mult).then_inc(xn_done, 1)
                dve.wait_ge(xn_done, g + 2)
                nc.vector.tensor_copy(XHL[:, 0, :], XN[:]).then_inc(xhigh, 1)
                dve.wait_ge(xhigh, g + 2)
                nc.vector.tensor_tensor(XHL[:, 1, :], XN[:], XHL[:, 0, :], ALU.subtract).then_inc(xhl_done, 1)

            def norm(g, s):
                dve.wait_ge(y_ready[g], s - FIRST[g] + 1)
                tiles = len(TILES[g])
                y = Y[YPAIR[g]]
                base = NORM_OPS * (s - FIRST[g])
                for p in range(4):
                    if 2 * p + 1 < tiles:
                        pair = y[:, 2 * p:2 * p + 2, :].rearrange("p t c -> p c t")
                    else:
                        pair = y[:, 2 * p, :].unsqueeze(2).to_broadcast([128, CH, 2])
                    nc.vector.bn_stats(stats[:, p, :], pair).then_inc(link[g], 1)
                squares = stats[:].rearrange("p a (t x) -> p (a t) x", x=3)[:, :, 2]
                for n, op in enumerate(rsqrt_ops(rs["g"], squares, 8)):
                    dve.wait_ge(link[g], base + 4 + n)
                    op().then_inc(link[g], 1)
                dve.wait_ge(link[g], base + 12)
                r = rs["g"][3]
                for b in range(2):
                    n = min(4, tiles - 4 * b)
                    before = {G0: (G3, -1), G3: (G0, 0), G1: (G2, -1), G2: (G1, 0)}[g]
                    at = s + before[1]
                    if not isinstance(s, int) or first_step(before[0]) <= at:
                        if isinstance(at, int):
                            at = min(at, last_step(before[0]))
                        v = UNIT[before[0], b]
                        dve.wait_ge(e_ready[v], unit_count(v, at))
                    nc.vector.tensor_tensor(T[YPAIR[g]][:, 4 * b:4 * b + n, :], y[:, 4 * b:4 * b + n, :],
                                            r[:, 4 * b:4 * b + n].unsqueeze(2).to_broadcast([128, n, CH]),
                                            ALU.mult).then_inc(scaled[g], 1)

            def cast(place, n):
                for u in VECTOR_CASTS[place]:
                    if active(UNITS[u][0], n - BEHIND[u]):
                        high_half(dve, u, n)

            gram_q(-1)
            gram_rsqrt(-1)
            gram_scale(-1)
            dve.wait_ge(w_in, 16)
            chained(nc.vector.reduce_sum(Wsum[:], W[:], AX.X))
            chained(nc.vector.tensor_scalar(Wsum[:], Wsum[:], -1.0 / CH, None, ALU.mult))
            chained(nc.vector.tensor_tensor(W[:], W[:], Wsum[:].unsqueeze(2).to_broadcast([128, 16, CH]), ALU.add))
            chained(nc.vector.tensor_copy(WH[:], W[:]))
            nc.vector.tensor_tensor(WL[:], W[:], WH[:], ALU.subtract).then_inc(weights_ready, 1)

            def step(n):
                if active(G2, n - 1):
                    norm(G2, n - 1)
                cast(0, n)
                if active(G0, n):
                    norm(G0, n)
                cast(1, n)
                if active(G1, n):
                    norm(G1, n)
                cast(2, n)
                if active("L0", n):
                    gram_q(n)
                if active(G3, n):
                    norm(G3, n)
                cast(3, n)
                if active("L0", n):
                    gram_rsqrt(n)
                    gram_scale(n)
                cast(4, n)
            run_steps(dve, step)

        @block.scalar
        def _(act):
            def high_weights():
                act.wait_ge(raw_in, 16 * sum(len(srcs) for srcs, _, _ in splits))
                for w, (_, hi, _) in zip(raw, splits):
                    nc.scalar.activation(hi[:], w[:], ACT.Copy).then_inc(split_high, 1)

            act.wait_ge(gains_ready, 1)
            act.wait_ge(act_zero, 2)

            def gelu(u, n):
                s = n - BEHIND[u]
                act.wait_ge(e_ready[u], unit_count(u, s))
                prev = previous_user(STAGE, u, n)
                if prev:
                    act.wait_ge(low_done[prev[0]], unit_count(prev[0], prev[1]))
                for layer, _, c, cols in unit_target(u):
                    ins = nc.scalar.activation(A[STAGE[u]][:, c:c + cols], E[BANK[u]][:, c:c + cols], ACT.Gelu,
                                               scale=gain_s[:, layer:layer + 1], bias=gains[:, 8 + layer:9 + layer])
                ins.then_inc(gelu_done[u], 1)

            def step(n):
                for u in range(16):
                    if active(UNITS[u][0], n - BEHIND[u]):
                        gelu(u, n)
                    v, at = (u - 1, n) if u else (15, n - 1)
                    if v not in VECTOR_HIGH and active(UNITS[v][0], at - BEHIND[v]):
                        high_half(act, v, at)
            run_steps(act, step, high_weights, 2)
            high_half(act, 15, STEPS + 3)

        @block.gpsimd
        def _(pool):
            for l in range(5):
                flat = H[l][:].bitcast(f32)
                ins = nc.gpsimd.memset(flat, 0.0)
            ins.then_inc(act_zero, 1)
            nc.gpsimd.memset(zeros[:], 0.0).then_inc(act_zero, 1)
            pool.wait_ge(act_zero, 2)

            def low_weights():
                for n, (w, (_, hi, lo)) in enumerate(zip(raw, splits)):
                    p = lo.shape[0]
                    pool.wait_ge(split_high, n + 1)
                    nc.gpsimd.tensor_tensor(lo[:], w[0:p], hi[0:p], ALU.subtract)

            def keep_halo(l, g, count, s):
                if count is not None:
                    pool.wait_ge(y_ready[g], count)
                u = UNIT[[("L0", 7), (G1, 1), (G2, 1), (G3, 0), (G3, 1)][l]]
                if active(UNITS[u][0], s):
                    pool.wait_ge(low_done[u], unit_count(u, s))
                n = LAYER_COLS[l]
                nc.gpsimd.tensor_tensor(H[l][:, :, 0:1], H[l][:, :, n:n + 1], zeros[:], ALU.add).then_inc(halo[l], 1)

            def low(u, s):
                pool.wait_ge(high_done[u], unit_count(u, s))
                for layer, col, c, cols in unit_target(u):
                    ins = nc.gpsimd.tensor_tensor(act_cols(layer, 1, col, cols, s), A[STAGE[u]][:, c:c + cols],
                                                  act_cols(layer, 0, col, cols, s), ALU.subtract)
                ins.then_inc(low_done[u], 1)

            def step(n):
                sym = not isinstance(n, int)
                for u, kind in enumerate(UNITS):
                    s = n - BEHIND[u]
                    if not active(kind[0], s):
                        continue
                    if kind == ("L0", 0):
                        keep_halo(0, G0, n if sym or n >= 1 else None, n - 1)
                    if kind == (G0, 0):
                        keep_halo(1, G2, n - 1 if sym or n > 1 else None, n - 1)
                    if kind == (G3, 0):
                        for l in (2, 3, 4) if sym or n <= STEPS else (3, 4):
                            keep_halo(l, G3, n - 1, n - 1)
                    low(u, s)
            run_steps(pool, step, low_weights, 2)



D = 192
TP = POS_PAD // 3
THIRDS = 3
BROWS = 33
HEADS, HD = 12, 16
EXPERTS, INTER = 8, 128
D2 = D - 128
PAIRS = BATCH * (BATCH + 1) // 2


START = ["conv", "conv_turn", "final_in", "final_turn"]
PROJECT = ["proj", "kv_a", "kv_b"]
ATTEND = ["v_norm", "q_scores", "vv_scores", "vv_sum_a", "vv_sum_b", "exp", "weights", "mix_a", "mix_b", "mix_c", "mix_d"]
FINISH = ["o_turn", "o_proj", "y_turn", "router", "rank_groups", "rank_experts", "weights_turn"]
FILL = {"v_norm": 2, "q_scores": 2, "vv_scores": 2, "vv_sum_a": 2, "vv_sum_b": 1, "exp": 1, "weights": 1,
        "mix_a": 2, "mix_b": 2, "mix_d": 4, "o_turn": 1, "o_proj": 1}
AHEAD = {"q_scores": ["conv"], "vv_scores": ["conv_turn"], "vv_sum_b": ["final_in"], "mix_b": ["final_turn"],
         "rank_groups": ["proj", "kv_a"], "rank_experts": ["kv_b"]}


def through_experts():
    for h in range(2):
        for e in range(EXPERTS + 1):
            yield "expert", h, e
            if e < EXPERTS:
                yield "share", h, e
        yield "sum", h, 0
        yield "sum", h, 1


def order():
    yield ("front", 0, "conv")
    yield ("front", 0, "join")
    for name in START[1:] + PROJECT:
        yield ("front", 0, name)
    back = []
    for i in range(THIRDS):
        for name in ATTEND + FINISH:
            yield ("front", i, name)
            for _ in range(FILL.get(name, 0)):
                if back:
                    yield back.pop(0)
                while back and back[0][2] == "share":
                    yield back.pop(0)
            if i + 1 < THIRDS:
                for other in AHEAD.get(name, []):
                    yield ("front", i + 1, other)
            if name == "rank_groups":
                yield from back
        back = [("back", i, *stage) for stage in through_experts()]
    yield from back


MIX = [[0, 1], [3, 2], [5, 6], [4, 7]]
MIX_ORDER = [q for pair in MIX for q in pair]
POOL_PAIRS = [3, 3, 4]
POOL_Q = [(1, 3, 6, 4, 7), (5, 6, 4), (6, 4)]


def sum_split(i):
    return sum(8 - d for d in range(POOL_PAIRS[i]))


def pool_count(i):
    return sum(len(q) for q in POOL_Q[:i])


def tokens_part(nc, keep, wt, out):
    ident, gains, gain_s, WH, WL, H5 = keep
    ctx = ExitStack()
    with ctx:
        def sb(name, shape, dt=f32):
            return ctx.enter_context(nc.sbuf_tensor(name, shape, dt))

        def sem(name):
            return ctx.enter_context(nc.semaphore(name))

        B = [ctx.enter_context(nc.psum_tensor(f"bank{k}", [128, COLS], f32)) for k in range(8)]
        ones = sb("ones", [BROWS, TP], f16)
        two = sb("rows_0_and_32", [1, BROWS])
        pbc = sb("proj_b_centred", [1, D])
        p_mean = sb("proj_mean", [128, 1])
        pb_mean = sb("proj_b_mean", [1, 1])
        PB1 = sb("proj_b_turned1", [128, BROWS])
        PB2 = sb("proj_b_turned2", [D2, BROWS])
        M = sb("proj_qkv", [128, 3 * D])
        bias = sb("bias_rows", [BROWS, 5 * D], f16)
        r2 = sb("attn_scale", [TP, 8])
        no_bias = sb("no_bias", [TP, 1])
        turned = sb("turned", [128, 8, 128])
        TA = turned[0:TP]
        h6 = sb("h6", [128, 8 * TP])
        Pc, PT1, PT2 = h6[:, 0:D], h6[:, D:D + 128], h6[0:D2, D + 128:D + 256]
        z = h6
        h0 = [sb(f"resid{k}", [TP, 8, D]) for k in range(THIRDS)]
        xn = sb("xn", [TP, 8, D])
        XT1 = turned[:].rearrange("p t c -> p (t c)")[:, 0:8 * TP]
        XT2 = sb("xt2", [D2, 8 * TP])
        YH = [sb(f"y_high{k}", [128, 8 * TP], f16) for k in range(2)]
        YL = [sb(f"y_low{k}", [128, 8 * TP], f16) for k in range(2)]
        YS = [sb(f"y_rest{k}", [128, 8 * TP], f16) for k in range(2)]
        KV = sb("kv", [TP, 8, 2 * D])
        q0 = sb("q0", [TP, D])
        vn = sb("vn", [TP, 8, D])
        prod = sb("prod", [TP, PAIRS, D])
        prod0 = xn
        PQ = [prod[:, 8 * k:8 * k + 8, :] for k in range(4)]
        sv = sb("sv", [TP, PAIRS, HEADS])
        s0 = sb("s0", [TP, 8, HEADS])
        m0 = sb("m0", [TP, HEADS])
        EX = sb("ex", [TP, 64, HEADS])
        Z = sb("zsum", [TP, 8, HEADS])
        RZ = sb("rz", [TP, 8, HEADS])
        O = vn
        n2 = sb("n2", [TP, 96])
        stats = sb("tstats", [TP, 4, BN])
        rt = [sb(f"t_rsqrt{n}", [TP, 96]) for n in range(4)]
        sc = sb("sc", [TP, 8, EXPERTS])
        biased = sb("biased", [TP, 8, EXPERTS])
        gs = sb("gs", [TP, 8, 4])
        gk = sb("gk", [TP, 8, 4])
        gc = sb("gc", [TP, 8, 8])
        ek = sb("ek", [TP, 8, EXPERTS])
        em = sb("em", [TP, 8, EXPERTS])
        cw = sb("cw", [TP, 8, EXPERTS])
        wsum = sb("wsum", [TP, 8])
        cwh = sb("cw_high", [TP, 8, EXPERTS], f16)
        cw2 = sb("cw_parts", [TP, 8, 2 * EXPERTS])
        cwT = [sb(f"cwt{k}", [2 * EXPERTS, 8 * TP], f16) for k in range(2)]
        sl = [sb(f"silu{k}", [128, 4 * TP]) for k in range(2)]
        share = [sb("expert_weight", [128, 4 * TP])[:], wt["qkv1"][:, 0:4 * TP]]
        ffn = sb("ffn_out", [TP, 2, D])
        U = sb("hidden", [128, EXPERTS + 1, 4 * TP])

        names = ("pc pt made m_s r2 y6 t6 e6 h6 fl_in fl_t fl_e z pj h0 x_t xt kv kv_s vn_r prod_p sv ex0in ex en pqm_p "
                 "o ot_e op yt_e yh yl gate sig cw cwt_e cwt f1 f3 fc silu gated hid fo res h3 share fo_s").split()
        S = {n: sem("s_" + n) for n in names}
        link = sem("token_link")
        out_left = sem("out_left")
        block = ctx.enter_context(nc.Block())
        NFE = EXPERTS + 1
        N4 = 4 * TP

        def tile_cols(t):
            return slice((t % 4) * TP, (t % 4 + 1) * TP)

        def run(front, back):
            for stage in order():
                if stage[0] == "front":
                    front(*stage[1:])
                else:
                    back(*stage[1:])

        @block.tensor
        def _(pe):
            def turn(src, banks, width, rows, sem_):
                for t in range(8):
                    last = nc.tensor.transpose(B[banks[t // 4]][0:width, tile_cols(t)], src(t), ident[0:rows, 0:rows])
                    if t % 4 == 3:
                        last.then_inc(sem_, 1)

            def front(i, name):
                if name == "conv":
                    if i:
                        pe.wait_ge(S["kv_s"], 9 * i)
                    for t in range(8):
                        base = 2 * (t * POS_PAD + TP * i) + 257
                        k = 0
                        for tap in range(2):
                            for part, w in ((0, WH), (0, WL), (1, WH)):
                                c = base + tap
                                last = nc.tensor.matmul(B[t // 4][0:TP, t % 4 * 128:t % 4 * 128 + 128],
                                                        H5[:, part, c:c + 2 * TP - 1:2], w[:, 14 + tap, :],
                                                        start=(k == 0), stop=(k == 5))
                                k += 1
                        if t % 4 == 3:
                            last.then_inc(S["y6"], 1)
                elif name == "join":
                    pe.wait_ge(S["pc"], 2)
                    nc.tensor.transpose(B[4][:, 0:128], Pc[:, 0:128], ident[:])
                    nc.tensor.transpose(B[4][0:D2, 128:256], Pc[:, 128:D], ident[:])
                    nc.tensor.transpose(B[4][:, 256:257], pbc[:, 0:128], ident[0:1, 0:1])
                    nc.tensor.transpose(B[4][0:D2, 257:258], pbc[:, 128:D], ident[0:1, 0:1]).then_inc(S["pt"], 1)
                    pe.wait_ge(S["made"], 4)
                    for o, w1, w2, c in ((B[5][:, 0:2 * D], PT1, PT2, slice(D, 3 * D)), (B[6][:, 0:D], PT1, PT2, slice(0, D)),
                                         (B[4][0:BROWS, 0:2 * D], PB1, PB2, slice(D, 3 * D)),
                                         (B[6][0:BROWS, D:2 * D], PB1, PB2, slice(0, D))):
                        nc.tensor.matmul(o, w1[:], wt["qkv1"][:, c], start=True, stop=False)
                        nc.tensor.matmul(o, w2[:], wt["qkv2"][:, c], start=False, stop=True).then_inc(S["pt"], 1)
                    for o, w in ((B[7][0:BROWS, 0:D], "proj_b"), (B[7][0:BROWS, D:2 * D], "op_b")):
                        nc.tensor.matmul(o, two[:], wt[w][:], start=True, stop=True).then_inc(S["pt"], 1)
                elif name == "conv_turn":
                    pe.wait_ge(S["t6"], 2 * i + 2)
                    turn(lambda t: TA[:, t, :], (2, 3), 128, TP, S["e6"])
                elif name == "final_in":
                    pe.wait_ge(S["h6"], 2 * i + 2)
                    for t in range(8):
                        last = nc.tensor.transpose(B[t // 4][0:TP, t % 4 * 128:t % 4 * 128 + 128],
                                                   h6[:, t * TP:(t + 1) * TP], ident[:])
                        if t % 4 == 3:
                            last.then_inc(S["fl_in"], 1)
                elif name == "final_turn":
                    pe.wait_ge(S["fl_t"], i + 1)
                    turn(lambda t: TA[:, t, :], (2, 3), 128, TP, S["fl_e"])
                elif name == "proj":
                    pe.wait_ge(S["z"], 2 * i + 2)
                    pe.wait_ge(S["made"], 7)
                    if i:
                        pe.wait_ge(S["sig"], i)
                    for t in range(8):
                        o = B[t // 2][0:TP, t % 2 * D:t % 2 * D + D]
                        nc.tensor.matmul(o, z[:, t * TP:(t + 1) * TP], wt["proj"][:], start=True, stop=False)
                        last = nc.tensor.matmul(o, ones[:], bias[:, 3 * D:4 * D], start=False, stop=True)
                        if t % 2:
                            last.then_inc(S["pj"], 1)
                elif name in ("kv_a", "kv_b"):
                    if i == 0 and name == "kv_a":
                        pe.wait_ge(S["m_s"], 2)
                    for t in range(4) if name == "kv_a" else range(4, 8):
                        b = B[t % 4]
                        if t < 4:
                            pe.wait_ge(S["h0"], 4 * i + t + 1)
                        else:
                            pe.wait_ge(S["kv_s"], 9 * i + t - 3)
                        nc.tensor.matmul(b[0:TP, 0:2 * D], z[:, t * TP:(t + 1) * TP], M[:, D:3 * D], start=True, stop=False)
                        nc.tensor.matmul(b[0:TP, 0:2 * D], ones[:], bias[:, D:3 * D], start=False, stop=True)\
                            .then_inc(S["kv"], 1)
                    if name == "kv_b":
                        pe.wait_ge(S["kv_s"], 9 * i + 5)
                        nc.tensor.matmul(B[0][0:TP, 0:D], z[:, 0:TP], M[:, 0:D], start=True, stop=False)
                        nc.tensor.matmul(B[0][0:TP, 0:D], ones[:], bias[:, 0:D], start=False, stop=True)\
                            .then_inc(S["kv"], 1)
                elif name == "o_turn":
                    pe.wait_ge(S["kv_s"], 9 * i + 9)
                    if i + 1 < THIRDS:
                        pe.wait_ge(S["z"], 2 * i + 4)
                    pe.wait_ge(S["o"], 8 * i + 8)
                    turn(lambda t: O[:, t, 0:128], (0, 1), 128, TP, S["ot_e"])
                    turn(lambda t: O[:, t, 128:D], (2, 3), D2, TP, S["ot_e"])
                elif name == "o_proj":
                    pe.wait_ge(S["xt"], 4 * i + 4)
                    for t in range(8):
                        o = B[t // 2][0:TP, t % 2 * D:t % 2 * D + D]
                        c = slice(t * TP, (t + 1) * TP)
                        nc.tensor.matmul(o, XT1[:, c], wt["op1"][:], start=True, stop=False)
                        nc.tensor.matmul(o, XT2[:, c], wt["op2"][:], start=False, stop=False)
                        last = nc.tensor.matmul(o, ones[:], bias[:, 4 * D:5 * D], start=False, stop=True)
                        if t % 2:
                            last.then_inc(S["op"], 1)
                elif name == "y_turn":
                    pe.wait_ge(S["x_t"], i + 1)
                    turn(lambda t: xn[:, t, 0:128], (0, 1), 128, TP, S["yt_e"])
                    turn(lambda t: xn[:, t, 128:D], (2, 3), D2, TP, S["yt_e"])
                elif name == "router":
                    pe.wait_ge(S["yl"], 4 * i + 4)
                    yh, yl, ys = YH[i % 2], YL[i % 2], YS[i % 2]
                    for t in range(8):
                        c = slice(t * TP, (t + 1) * TP)
                        o = B[0][0:TP, t * 8:t * 8 + 8]
                        nc.tensor.matmul(o, yh[:, c], wt["gateah"][:], start=True, stop=False)
                        nc.tensor.matmul(o, yh[:, c], wt["gateal"][:], start=False, stop=False)
                        nc.tensor.matmul(o, yl[:, c], wt["gateah"][:], start=False, stop=False)
                        nc.tensor.matmul(o, ys[:, c], wt["gatebh"][:], start=False, stop=False)
                        last = nc.tensor.matmul(o, ys[0:D2, c], wt["gatebl"][:], start=False, stop=True)
                    last.then_inc(S["gate"], 1)
                elif name == "weights_turn":
                    pe.wait_ge(S["cw"], i + 1)
                    if i:
                        pe.wait_ge(S["share"], 2 * EXPERTS * i)
                        pe.wait_ge(S["fo_s"], 8 * i)
                    turn(lambda t: cw2[:, t, :], (6, 7), 2 * EXPERTS, TP, S["cwt_e"])

            def back(i, name, hh, e):
                if name == "expert":
                    c = slice(hh * N4, (hh + 1) * N4)
                    n = (2 * i + hh) * NFE + e
                    yh, yl, ys = YH[i % 2][:, c], YL[i % 2][:, c], YS[i % 2][:, c]
                    for bank, w, done, free in ((4, "w1", "f1", "silu"), (5, "w3", "f3", "h3")):
                        if n:
                            pe.wait_ge(S[free], n)
                        o = B[bank][:, 0:N4]
                        nc.tensor.matmul(o, wt[w + "ah"][:, e, :], yh, start=True, stop=False)
                        nc.tensor.matmul(o, wt[w + "ah"][:, e, :], yl, start=False, stop=False)
                        nc.tensor.matmul(o, wt[w + "al"][:, e, :], yh, start=False, stop=False)
                        nc.tensor.matmul(o, wt[w + "bh"][:, e, :], ys, start=False, stop=False)
                        nc.tensor.matmul(o, wt[w + "bl"][:, e, :], YS[i % 2][0:D2, c], start=False, stop=True)\
                            .then_inc(S[done], 1)
                elif name == "share":
                    c = slice(hh * N4, (hh + 1) * N4)
                    half = 2 * i + hh
                    m = half * EXPERTS + e
                    if hh == 0 and e == 0:
                        pe.wait_ge(S["cwt"], 2 * i + 2)
                    if m:
                        pe.wait_ge(S["share"], m)
                        if e == 0:
                            pe.wait_ge(S["fo_s"], half * 4)
                    nc.tensor.matmul(B[6][:, 0:N4], wt["pick"][:, e, :], cwT[i % 2][:, c], start=True, stop=True)\
                        .then_inc(S["fc"], 1)
                else:
                    half = 2 * i + hh
                    for t in (2 * e, 2 * e + 1):
                        m = half * 4 + t
                        if t % 2 == 0 and m:
                            pe.wait_ge(S["fo_s"], m - 1)
                        elif t % 2:
                            pe.wait_ge(S["share"], (half + 1) * EXPERTS)
                            if m > 1:
                                pe.wait_ge(S["fo_s"], m - 1)
                        for x in range(NFE):
                            if t == 0 and x < EXPERTS:
                                pe.wait_ge(S["hid"], half * EXPERTS + x + 1)
                            elif t == 0:
                                pe.wait_ge(S["gated"], (half + 1) * NFE)
                            last = nc.tensor.matmul(B[7 - t % 2][0:TP, 0:D], U[:, x, t * TP:(t + 1) * TP], wt["w2"][:, x, :],
                                                    start=(x == 0), stop=(x == NFE - 1))
                        last.then_inc(S["fo"], 1)

            run(front, back)

        @block.scalar
        def _(act):
            A = nc.scalar.activation

            def copies(dst, banks, rows, sem_in, base, sem_out):
                for b in range(2):
                    act.wait_ge(sem_in, base + b + 1)
                    A(dst[0:rows, b * N4:(b + 1) * N4], B[banks[b]][0:rows, 0:N4], ACT.Copy).then_inc(sem_out, 1)

            def front(i, name):
                if name == "join":
                    act.wait_ge(S["pt"], 7)
                    A(M[:, D:3 * D], B[5][:, 0:2 * D], ACT.Copy).then_inc(S["m_s"], 1)
                    A(M[:, 0:D], B[6][:, 0:D], ACT.Copy).then_inc(S["m_s"], 1)
                elif name == "conv_turn":
                    for b in range(2):
                        act.wait_ge(S["e6"], 2 * i + b + 1)
                        A(h6[:, b * N4:(b + 1) * N4], B[2 + b][:, 0:N4], ACT.Gelu,
                          scale=gain_s[:, 6:7], bias=gains[:, 14:15]).then_inc(S["h6"], 1)
                elif name == "final_turn":
                    for b in range(2):
                        act.wait_ge(S["fl_e"], 2 * i + b + 1)
                        A(z[:, b * N4:(b + 1) * N4], B[2 + b][:, 0:N4], ACT.Identity,
                          scale=gain_s[:, 7:8], bias=gains[:, 15:16]).then_inc(S["z"], 1)
                elif name == "proj":
                    for b in range(4):
                        act.wait_ge(S["pj"], 4 * i + b + 1)
                        A(h0[i][:, 2 * b:2 * b + 2, :], B[b][0:TP, 0:2 * D].rearrange("p (t d) -> p t d", t=2),
                          ACT.Copy).then_inc(S["h0"], 1)
                elif name in ("kv_a", "kv_b"):
                    if name == "kv_a":
                        act.wait_ge(S["r2"], i + 1)
                    for t in range(4) if name == "kv_a" else range(4, 8):
                        act.wait_ge(S["kv"], 9 * i + t + 1)
                        A(KV[:, t, :], B[t % 4][0:TP, 0:2 * D], ACT.Identity, scale=r2[:, t:t + 1], bias=no_bias[:])\
                            .then_inc(S["kv_s"], 1)
                    if name == "kv_b":
                        act.wait_ge(S["kv"], 9 * i + 9)
                        A(q0[:], B[0][0:TP, 0:D], ACT.Identity, scale=r2[:, 0:1], bias=no_bias[:]).then_inc(S["kv_s"], 1)
                elif name == "exp":
                    act.wait_ge(S["sv"], 2 * i + 2)
                    off = 0
                    for d in range(8):
                        if d < 7:
                            A(EX[:, 9 + d:9 + d + 9 * (6 - d) + 1:9, :], sv[:, off + 1:off + 8 - d, :], ACT.Exp, scale=0.25)
                        if d:
                            A(EX[:, 8 * d:8 * d + 9 * (7 - d) + 1:9, :], sv[:, off:off + 8 - d, :], ACT.Exp, scale=0.25)
                        off += 8 - d
                    act.wait_ge(S["ex0in"], i + 1)
                    A(EX[:, 0:8, :], s0[:], ACT.Exp, scale=0.25).then_inc(S["ex"], 1)
                elif name == "o_turn":
                    copies(XT1, (0, 1), 128, S["ot_e"], 4 * i, S["xt"])
                    copies(XT2, (2, 3), D2, S["ot_e"], 4 * i + 2, S["xt"])
                elif name == "y_turn":
                    copies(YH[i % 2], (0, 1), 128, S["yt_e"], 4 * i, S["yh"])
                    copies(YS[i % 2], (2, 3), D2, S["yt_e"], 4 * i + 2, S["yh"])
                elif name == "router":
                    act.wait_ge(S["gate"], i + 1)
                    A(sc[:], B[0][0:TP, 0:64].rearrange("p (t e) -> p t e", t=8), ACT.Sigmoid).then_inc(S["sig"], 1)
                elif name == "weights_turn":
                    copies(cwT[i % 2], (6, 7), 2 * EXPERTS, S["cwt_e"], 2 * i, S["cwt"])

            def back(i, name, hh, e):
                half = 2 * i + hh
                if name == "expert":
                    n = half * NFE + e
                    act.wait_ge(S["f1"], n + 1)
                    if n > 1:
                        act.wait_ge(S["gated"], n - 1)
                    A(sl[n % 2][:], B[4][:, 0:N4], ACT.Silu).then_inc(S["silu"], 1)
                    act.wait_ge(S["f3"], n + 1)
                    if e == 0 and n:
                        act.wait_ge(S["fo"], half * 4)
                    A(U[:, e, :], B[5][:, 0:N4], ACT.Copy).then_inc(S["h3"], 1)
                elif name == "share":
                    m = half * EXPERTS + e
                    act.wait_ge(S["fc"], m + 1)
                    if m > 1:
                        act.wait_ge(S["hid"], m - 1)
                    A(share[m % 2], B[6][:, 0:N4], ACT.Copy).then_inc(S["share"], 1)
                else:
                    for t in (2 * e, 2 * e + 1):
                        m = half * 4 + t
                        act.wait_ge(S["fo"], m + 1)
                        if m > 1:
                            act.wait_ge(S["res"], m - 1)
                        A(ffn[:, m % 2, :], B[7 - t % 2][0:TP, 0:D], ACT.Copy).then_inc(S["fo_s"], 1)

            run(front, back)

        @block.vector
        def _(dve):
            v = nc.vector
            count = [0]

            def chained(ins):
                count[0] += 1
                ins.then_inc(link, 1)
                dve.wait_ge(link, count[0])

            def rsqrt(source, n, low, eps, factor=1.0, dst=None, done=None):
                x, y0, a, y1 = (t[:, 0:n] for t in rt)
                y1 = y1 if dst is None else dst
                chained(v.tensor_scalar(x, source, low, eps, ALU.max, ALU.add))
                chained(v.tensor_scalar(y0.bitcast(i32), x.bitcast(i32), -0.5, MAGIC, ALU.mult, ALU.add))
                chained(v.tensor_tensor(a, y0, y0, ALU.mult))
                chained(v.scalar_tensor_tensor(a, a, NEWTON1[0], x, ALU.mult, ALU.mult))
                chained(v.scalar_tensor_tensor(y0, a, NEWTON1[1], y0, ALU.add, ALU.mult))
                chained(v.tensor_tensor(a, y0, y0, ALU.mult))
                chained(v.scalar_tensor_tensor(a, a, NEWTON2[0] * factor, x, ALU.mult, ALU.mult))
                last = v.scalar_tensor_tensor(y1, a, NEWTON2[1] * factor, y0, ALU.add, ALU.mult)
                if done is None:
                    chained(last)
                else:
                    last.then_inc(done, 1)
                return y1

            halves = stats[:].rearrange("p a (t x) -> p (a t) x", x=3)
            squares = halves[:, :, 2]

            def token_stats(src):
                for p in range(4):
                    last = v.bn_stats(stats[:, p, :], src[:, 2 * p:2 * p + 2, :].rearrange("p t c -> p c t"))
                chained(last)

            def token_norm(src, n, dst, done):
                token_stats(src)
                r = rsqrt(squares, 8, 0.0, n * 1e-5, math.sqrt(n))
                for t in range(8):
                    last = v.tensor_scalar(dst[:, t, :], src[:, t, :], halves[:, t, 1:2], r[:, t:t + 1],
                                           ALU.subtract, ALU.mult)
                last.then_inc(done, 1)

            def bank_stats(sem_in, base):
                for b in range(2):
                    dve.wait_ge(sem_in, base + b + 1)
                    for p in range(2):
                        chained(v.bn_stats(stats[:, 2 * b + p, :],
                                           B[b][0:TP, p * 256:p * 256 + 256].rearrange("p (t c) -> p c t", t=2)))
                return rsqrt(squares, 8, 0.0, EPS_SUM)

            def rank(x, k, n):
                chained(v.memset(k[:], 0.0))
                for d in range(1, n):
                    c = gc[:, :, 0:n - d]
                    chained(v.tensor_tensor(c, x[:, :, 0:n - d], x[:, :, d:n], ALU.is_ge))
                    chained(v.tensor_tensor(k[:, :, d:n], k[:, :, d:n], c, ALU.add))
                    chained(v.scalar_tensor_tensor(k[:, :, 0:n - d], k[:, :, 0:n - d], 1.0, c, ALU.add, ALU.subtract))

            V = KV[:, :, D:2 * D]
            Vh = V.rearrange("p b (h d) -> p b h d", h=HEADS)
            EQ = EX[:].rearrange("p (q k) h -> p q k h", q=8)

            def front(i, name):
                if name == "conv":
                    r = bank_stats(S["y6"], 2 * i)
                    for b in range(2):
                        v.tensor_tensor(TA[:, 4 * b:4 * b + 4, :], B[b][0:TP, :].rearrange("p (t c) -> p t c", t=4),
                                        r[:, 4 * b:4 * b + 4].unsqueeze(2).to_broadcast([TP, 4, 128]), ALU.mult)\
                            .then_inc(S["t6"], 1)
                elif name == "final_in":
                    r = bank_stats(S["fl_in"], 2 * i)
                    for t in range(8):
                        last = v.tensor_scalar(TA[:, t, :], B[t // 4][0:TP, t % 4 * 128:t % 4 * 128 + 128],
                                               halves[:, t, 1:2], r[:, t:t + 1], ALU.subtract, ALU.mult)
                    last.then_inc(S["fl_t"], 1)
                elif name == "join":
                    dve.wait_ge(S["pt"], 1)
                    v.tensor_copy(PT1[:], B[4][:, 0:128]).then_inc(S["made"], 1)
                    v.tensor_copy(PT2[:], B[4][0:D2, 128:256]).then_inc(S["made"], 1)
                    v.tensor_copy(PB1[:, 0:BROWS:32], B[4][:, 256:257].to_broadcast([128, 2])).then_inc(S["made"], 1)
                    v.tensor_copy(PB2[:, 0:BROWS:32], B[4][0:D2, 257:258].to_broadcast([D2, 2])).then_inc(S["made"], 1)
                    low = slice(32, BROWS)
                    dve.wait_ge(S["pt"], 7)
                    dve.wait_ge(S["m_s"], 2)
                    parts = [(D, 3 * D, B[4][0:BROWS, 0:2 * D]), (0, D, B[6][0:BROWS, D:2 * D]), (3 * D, 5 * D, B[7][0:BROWS, 0:2 * D])]
                    for a, b, rows in parts:
                        chained(v.tensor_copy(bias[:, a:b], rows))
                    for a, b, rows in parts:
                        last = v.tensor_tensor(bias[low, a:b], rows[low, :], bias[low, a:b], ALU.subtract)
                        last.then_inc(S["made"], 1)
                elif name == "proj":
                    dve.wait_ge(S["h0"], 4 * i + 4)
                    token_stats(h0[i])
                    rsqrt(squares, 8, 0.0, D * 1e-5, math.sqrt(D), r2[:], S["r2"])
                elif name == "v_norm":
                    dve.wait_ge(S["kv_s"], 9 * i + 9)
                    chained(v.tensor_tensor(prod0[:], V, V, ALU.mult))
                    chained(v.reduce_sum(n2[:], prod0[:].rearrange("p b (h d) -> p (b h) d", h=HEADS), AX.X))
                    r = rsqrt(n2[:], 96, 1e-12, 0.0)
                    rb = r.rearrange("p (b h) -> p b h", b=8).unsqueeze(3).to_broadcast([TP, 8, HEADS, HD])
                    v.tensor_tensor(vn[:].rearrange("p b (h d) -> p b h d", h=HEADS), Vh, rb, ALU.mult)\
                        .then_inc(S["vn_r"], 1)
                elif name == "q_scores":
                    chained(v.tensor_tensor(prod0[:], KV[:, :, 0:D], q0[:].unsqueeze(1).to_broadcast([TP, 8, D]), ALU.mult))
                    chained(v.reduce_sum(s0[:], prod0[:].rearrange("p b (h d) -> p b h d", h=HEADS), AX.X))
                    chained(v.reduce_max(m0[:], s0[:].rearrange("p k h -> p h k"), AX.X))
                    v.tensor_tensor(s0[:], s0[:], m0[:].unsqueeze(1).to_broadcast([TP, 8, HEADS]), ALU.subtract)\
                        .then_inc(S["ex0in"], 1)
                elif name == "vv_scores":
                    dve.wait_ge(S["vn_r"], i + 1)
                    off = 0
                    for d in range(POOL_PAIRS[i]):
                        last = v.tensor_tensor(prod[:, off:off + 8 - d, :], vn[:, 0:8 - d, :], vn[:, d:8, :], ALU.mult)
                        off += 8 - d
                    chained(last)
                elif name in ("vv_sum_a", "vv_sum_b"):
                    a, b = (0, sum_split(i)) if name == "vv_sum_a" else (sum_split(i), PAIRS)
                    if name == "vv_sum_b":
                        dve.wait_ge(S["prod_p"], i + 1)
                    v.reduce_sum(sv[:, a:b, :], prod[:, a:b, :].rearrange("p a (h d) -> p a h d", h=HEADS), AX.X)\
                        .then_inc(S["sv"], 1)
                elif name == "weights":
                    dve.wait_ge(S["ex"], i + 1)
                    chained(v.reduce_sum(Z[:], EQ.rearrange("p q k h -> p q h k"), AX.X))
                    chained(v.reciprocal(RZ[:], Z[:]))
                    v.tensor_tensor(EQ, EQ, RZ[:].unsqueeze(2).to_broadcast([TP, 8, 8, HEADS]), ALU.mult)\
                        .then_inc(S["en"], 1)
                elif name.startswith("mix"):
                    k = "abcd".index(name[-1])
                    if k == 0:
                        dve.wait_ge(S["en"], i + 1)
                    for q in MIX[k]:
                        if q in POOL_Q[i]:
                            m = pool_count(i) + POOL_Q[i].index(q)
                            dve.wait_ge(S["pqm_p"], m + 1)
                            src = PQ[2 + m % 2]
                        else:
                            src = PQ[MIX_ORDER.index(q) % 2]
                            w = EQ[:, q, :, :].unsqueeze(3).to_broadcast([TP, 8, HEADS, HD])
                            chained(v.tensor_tensor(src.rearrange("p b (h d) -> p b h d", h=HEADS), Vh, w, ALU.mult))
                        v.reduce_sum(O[:, q, :], src.rearrange("p k x -> p x k"), AX.X).then_inc(S["o"], 1)
                elif name == "o_proj":
                    for b in range(4):
                        dve.wait_ge(S["op"], 4 * i + b + 1)
                        rows = h0[i][:, 2 * b:2 * b + 2, :]
                        chained(v.tensor_tensor(rows, B[b][0:TP, 0:2 * D].rearrange("p (t d) -> p t d", t=2), rows, ALU.add))
                    token_norm(h0[i], D, xn, S["x_t"])
                elif name == "y_turn":
                    for n, (bank, dst, hi, rows) in enumerate(((0, YL, YH, 0), (1, YL, YH, 0), (2, YS, YS, D2), (3, YS, YS, D2))):
                        b = n % 2
                        c = slice(b * N4, (b + 1) * N4)
                        dve.wait_ge(S["yh"], 4 * i + n + 1)
                        p = D2 if rows else 128
                        v.tensor_tensor(dst[i % 2][rows:rows + p, c], B[bank][0:p, 0:N4], hi[i % 2][0:p, c], ALU.subtract)\
                            .then_inc(S["yl"], 1)
                elif name == "rank_groups":
                    dve.wait_ge(S["sig"], i + 1)
                    chained(v.tensor_tensor(biased[:], sc[:], wt["gate_b"][:].unsqueeze(1).to_broadcast([TP, 8, EXPERTS]), ALU.add))
                    pair = biased[:].rearrange("p t (g k) -> p t g k", k=2)
                    chained(v.tensor_tensor(gs[:], pair[:, :, :, 0], pair[:, :, :, 1], ALU.add))
                    rank(gs, gk, 4)
                    chained(v.tensor_scalar(gk[:], gk[:], 1.5, None, ALU.is_lt))
                    chained(v.tensor_scalar(gs[:], gk[:], -1.0, 1e30, ALU.add, ALU.mult))
                    e4 = em[:].rearrange("p t (g k) -> p t g k", k=2)
                    chained(v.tensor_tensor(e4, pair, gk[:].unsqueeze(3).to_broadcast([TP, 8, 4, 2]), ALU.mult))
                    chained(v.tensor_tensor(e4, e4, gs[:].unsqueeze(3).to_broadcast([TP, 8, 4, 2]), ALU.add))
                elif name == "rank_experts":
                    rank(em, ek, 8)
                    chained(v.tensor_scalar(ek[:], ek[:], 1.5, None, ALU.is_lt))
                    chained(v.tensor_tensor(cw[:], ek[:], sc[:], ALU.mult))
                    chained(v.reduce_sum(wsum[:], cw[:], AX.X))
                    chained(v.tensor_scalar(wsum[:], wsum[:], 1e-6, None, ALU.add))
                    chained(v.reciprocal(wsum[:], wsum[:]))
                    chained(v.tensor_tensor(cw[:], cw[:], wsum[:].unsqueeze(2).to_broadcast([TP, 8, EXPERTS]), ALU.mult))
                    chained(v.tensor_copy(cwh[:], cw[:]))
                    chained(v.tensor_copy(cw2[:, :, 0:EXPERTS], cwh[:]))
                    v.tensor_tensor(cw2[:, :, EXPERTS:], cw[:], cwh[:], ALU.subtract).then_inc(S["cw"], 1)

            for t, value in ((ones, 1.0), (two, 0.0), (PB1, 0.0), (PB2, 0.0), (no_bias, 0.0)):
                chained(v.memset(t[:], value))
            chained(v.memset(two[:, 0:BROWS:32], 1.0))
            for w, mean, centred in ((wt["proj"], p_mean, Pc), (wt["proj_b"], pb_mean, pbc)):
                chained(v.reduce_sum(mean[:], w[:], AX.X))
                chained(v.tensor_scalar(mean[:], mean[:], -1.0 / D, None, ALU.mult))
                v.tensor_tensor(centred[:], w[:], mean[:].to_broadcast(list(w.shape)), ALU.add).then_inc(S["pc"], 1)
            run(front, lambda *stage: None)

        @block.gpsimd
        def _(pool):
            tt = nc.gpsimd.tensor_tensor

            def front(i, name):
                if name == "vv_scores":
                    pool.wait_ge(S["vn_r"], i + 1)
                    off = sum_split(i)
                    for d in range(POOL_PAIRS[i], 8):
                        last = tt(prod[:, off:off + 8 - d, :], vn[:, 0:8 - d, :], vn[:, d:8, :], ALU.mult)
                        off += 8 - d
                    last.then_inc(S["prod_p"], 1)
                elif name.startswith("mix"):
                    EQ = EX[:].rearrange("p (q k) h -> p q k h", q=8)
                    Vh = KV[:, :, D:2 * D].rearrange("p b (h d) -> p b h d", h=HEADS)
                    for q in [q for q in MIX["abcd".index(name[-1])] if q in POOL_Q[i]]:
                        n = POOL_Q[i].index(q)
                        m = pool_count(i) + n
                        if n == 0:
                            pool.wait_ge(S["en"], i + 1)
                        if n >= 2:
                            pool.wait_ge(S["o"], 8 * i + MIX_ORDER.index(POOL_Q[i][n - 2]) + 1)
                        w = EQ[:, q, :, :].unsqueeze(3).to_broadcast([TP, 8, HEADS, HD])
                        tt(PQ[2 + m % 2].rearrange("p b (h d) -> p b h d", h=HEADS), Vh, w, ALU.mult).then_inc(S["pqm_p"], 1)

            def back(i, name, hh, e):
                half = 2 * i + hh
                if name == "expert":
                    n = half * NFE + e
                    pool.wait_ge(S["silu"], n + 1)
                    pool.wait_ge(S["h3"], n + 1)
                    g = U[:, e, :]
                    tt(g, sl[n % 2][:], g, ALU.mult).then_inc(S["gated"], 1)
                elif name == "share":
                    m = half * EXPERTS + e
                    g = U[:, e, :]
                    pool.wait_ge(S["gated"], half * NFE + e + 1)
                    pool.wait_ge(S["share"], m + 1)
                    tt(g, g, share[m % 2], ALU.mult).then_inc(S["hid"], 1)
                else:
                    for t in (2 * e, 2 * e + 1):
                        m = half * 4 + t
                        pool.wait_ge(S["fo_s"], m + 1)
                        x = h0[i][:, hh * 4 + t, :]
                        tt(x, ffn[:, m % 2, :], x, ALU.add).then_inc(S["res"], 1)

            run(front, back)

        @block.sync
        def _(sp):
            for i in range(THIRDS):
                rows = TP if i < THIRDS - 1 else POS - TP * (THIRDS - 1)
                for t in range(8):
                    sp.wait_ge(S["res"], 8 * i + t + 1)
                    sp.dma_start(out[t, i * TP:i * TP + rows, :], h0[i][0:rows, t, :]).then_inc(out_left, 16)
            sp.wait_ge(out_left, 16 * 8 * THIRDS)


WEIGHTS = {
    "proj": [128, D], "proj_b": [1, D], "qkv1": [128, 3 * D], "qkv2": [D2, 3 * D],
    "op1": [128, D], "op2": [D2, D], "op_b": [1, D], "gate_b": [TP, EXPERTS], "w2": [INTER, 9, D],
    "pick": [2 * EXPERTS, EXPERTS, 128],
}
SPLIT = {"gate": [EXPERTS], "w1": [9, INTER], "w3": [9, INTER]}


def audio_tower(nc, d, out):
    ctx = ExitStack()
    with ctx:
        def sb(name, shape, dt=f32):
            return ctx.enter_context(nc.sbuf_tensor(name, shape, dt))
        ident = sb("ident", [128, 128])
        gains = sb("gains", [128, 16])
        gain_s = sb("gain_scaled", [128, 8])
        WH = sb("conv_w_high", [128, 16, CH], f16)
        WL = sb("conv_w_low", [128, 16, CH], f16)
        H5 = sb("act5", [128, 2, (STEPS + 2) * 128], f16)
        wt = {n: sb("w_" + n, shape, f16 if n == "pick" else f32) for n, shape in WEIGHTS.items()}
        src = {
            "proj": d["proj"], "proj_b": d["proj_b"], "qkv1": d["wqkv"][0:128, :], "qkv2": d["wqkv"][128:D, :],
            "op1": d["wo"][0:128, :], "op2": d["wo"][128:D, :], "op_b": d["wo_b"],
            "gate_b": d["gate_b"], "w2": d["w2"], "pick": d["pick"],
        }
        loads = [(wt[n][:], src[n]) for n in WEIGHTS]
        splits = []
        for n, shape in SPLIT.items():
            for part, rows in (("a", 128), ("b", D2)):
                hi = sb(f"w_{n}{part}_high", [128, *shape], f16)
                lo = sb(f"w_{n}{part}_low", [rows, *shape], f16)
                wt[f"{n}{part}h"], wt[f"{n}{part}l"] = hi, lo
                top, rest = d[n][0:128], d[n][128:D]
                splits.append(([(0, top)] if part == "a" else [(0, rest), (D2, rest)], hi, lo))
        keep = (ident, gains, gain_s, WH, WL, H5)
        conv_tower(nc, d["x5"], d["w0t"], d["wconv"], d["gb"], (d["ident"], d["mask"], d["chunk_sum"]), (*keep, loads, splits))
        tokens_part(nc, keep, wt, out)


def layout(inputs):
    f = lambda name: np.asarray(inputs[name])
    x = np.zeros(5 * X_LEN, np.float32)
    flat = f("x").reshape(-1)
    x[5:5 + flat.size] = flat
    x5 = np.ascontiguousarray(x.reshape(X_LEN, 5).T)
    t = "L0_tok_"
    w0t = np.ascontiguousarray(f(t + "conv_w0")[:, 0, :].T)
    wconv = np.concatenate([f(f"{t}conv_w{l}").transpose(1, 2, 0) for l in range(1, 7)], axis=1)
    gb = np.stack([f(f"{t}ln_g{l}") for l in range(7)] + [f(t + "fln_g")] + [f(f"{t}ln_b{l}") for l in range(7)]
                  + [f(t + "fln_b")], axis=1)
    rows = np.arange(XROWS)
    chunk = rows // 40 * 4 + rows % 4
    n = "L0_ffn_"
    both = lambda a, b, axes: np.concatenate([f(n + a), f(n + b)[None]], axis=0).transpose(axes)
    pick = np.zeros((2, EXPERTS, EXPERTS, 128), np.float16)
    pick[:, np.arange(EXPERTS), np.arange(EXPERTS)] = 1.0
    made = {
        "x5": x5, "w0t": w0t, "wconv": wconv, "gb": gb,
        "ident": np.eye(128, dtype=np.float32),
        "mask": (chunk[:, None] == chunk[None, :]).astype(np.float32),
        "chunk_sum": (chunk[:, None] == np.arange(8)[None, :]).astype(np.float32),
        "proj": f(t + "proj_w"), "proj_b": f(t + "proj_b")[None],
        "wqkv": f("L0_attn_w_qkv").T, "wo": f("L0_attn_w_proj").T, "wo_b": f("L0_attn_b_proj")[None],
        "gate": f(n + "gate_weight").T, "gate_b": np.broadcast_to(f(n + "gate_bias")[None], (TP, EXPERTS)),
        "w1": both("w1", "sw1", (2, 0, 1)), "w3": both("w3", "sw3", (2, 0, 1)), "w2": both("w2", "sw2", (2, 0, 1)),
        "pick": pick.reshape(2 * EXPERTS, EXPERTS, 128),
    }
    return {k: np.ascontiguousarray(a) for k, a in made.items()}


def kernel(**inputs):
    import concourse.bacc as bacc
    from concourse.bass_utils import run_bass_kernel_spmd

    arrays = {f"in_{k}": a for k, a in layout(inputs).items()}
    nc = bacc.Bacc("TRN2", target_bir_lowering=False, num_devices=1)
    d = {k[3:]: nc.dram_tensor(k, a.shape, mybir.dt.from_np(a.dtype), kind="ExternalInput").ap() for k, a in arrays.items()}
    out = nc.dram_tensor("out", (BATCH, POS, D), f32, kind="ExternalOutput").ap()
    audio_tower(nc, d, out)
    r = run_bass_kernel_spmd(nc, [arrays], core_ids=[0])
    return r.results[0]["out"]
```
